# Optimizing a Trainium2 kernel written in Bass

```python
import numpy as np
import jax
import jax.numpy as jnp

def _softmax(x, axis=-1):
    return jax.nn.softmax(x, axis=axis)

def _gelu(x):
    return jax.nn.gelu(x, approximate=True)

def _silu(x):
    return jax.nn.silu(x)

def _sigmoid(x):
    return jax.nn.sigmoid(x)

def _layernorm(x, axis=-1, eps=1e-05):
    m = jnp.mean(x, axis=axis, keepdims=True)
    v = jnp.var(x, axis=axis, keepdims=True)
    return (x - m) / jnp.sqrt(v + eps)

def _scatter_add(tgt, idx, src, axis=0):
    return tgt.at[idx].add(src)

def _segment_sum(src, seg, n):
    return jax.ops.segment_sum(src, seg, n)
kernel_name = 'mk_decoder_preln_d4_seqx_r4_55d34e'

def setup_inputs(seed: int=0):
    np.random.seed(seed)
    _w = jnp.asarray

    def _rec_inputs():
        import jax
        import jax.numpy as jnp
        _rk = jax.random.key(seed)
        x = -0.0002928 + 1 * jax.random.normal(jax.random.fold_in(_rk, 1), (8, 100, 256), jnp.float32)
        _lenS = 100 - jax.random.randint(jax.random.fold_in(_rk, 7), (8,), 0, max(1, 100 // 4) + 1, jnp.int32)
        _lenS2 = 361 - jax.random.randint(jax.random.fold_in(_rk, 8), (8,), 0, max(1, 361 // 4) + 1, jnp.int32)
        _ctx_1024P = jax.random.normal(jax.random.fold_in(_rk, 11), (8, 16, 256), jnp.float32)
        _ctx_1024c = jax.random.dirichlet(jax.random.fold_in(_rk, 511), 0.3 * jnp.ones((16,), jnp.float32), (8, 361))
        _ctx_1024t = jnp.einsum('bsk,bkd->bsd', _ctx_1024c, _ctx_1024P)
        _ctx_1024t = _ctx_1024t * jax.lax.rsqrt(jnp.mean(jnp.square(_ctx_1024t)) + 1e-12) * 0.953939
        ctx_1024 = -1.39393e-06 + 0.999914 * (_ctx_1024t + 0.3 * jax.random.normal(jax.random.fold_in(_rk, 611), (8, 361, 256), jnp.float32))
        _ctxb_2048x8P = jax.random.normal(jax.random.fold_in(_rk, 13), (8, 16, 8), jnp.float32)
        _ctxb_2048x8c = jax.random.dirichlet(jax.random.fold_in(_rk, 513), 0.3 * jnp.ones((16,), jnp.float32), (8, 361))
        _ctxb_2048x8t = jnp.einsum('bsk,bkd->bsd', _ctxb_2048x8c, _ctxb_2048x8P)
        _ctxb_2048x8t = _ctxb_2048x8t * jax.lax.rsqrt(jnp.mean(jnp.square(_ctxb_2048x8t)) + 1e-12) * 0.953939
        ctxb_2048x8 = -0.00745576 + 0.997402 * (_ctxb_2048x8t + 0.3 * jax.random.normal(jax.random.fold_in(_rk, 613), (8, 361, 8), jnp.float32))
        _validS = jnp.arange(100)[None, :] < _lenS[:, None]
        _validS2 = jnp.arange(361)[None, :] < _lenS2[:, None]
        _causal = jnp.tril(jnp.ones((100, 100), dtype=bool))
        mask_Bx1x1xS2_if1 = jnp.where(jnp.ones((8, 1, 1, 361), dtype=bool), 1, 0).astype(jnp.int32)
        mask_BxSxS2_bk0 = jnp.logical_not(jnp.broadcast_to(_validS2[:, None, :], (8, 100, 361)))
        return (x, ctx_1024, ctxb_2048x8, mask_Bx1x1xS2_if1, mask_BxSxS2_bk0)
    x, ctx_1024, ctxb_2048x8, mask_Bx1x1xS2_if1, mask_BxSxS2_bk0 = _rec_inputs()

    def _L0_attn_setup():
        import jax, jax.numpy as jnp
        import numpy as np
        import math
        B, T, C = (2, 512, 256)
        H, DK, DV = (16, 64, 64)
        key = jax.random.key(seed)
        ks = jax.random.split(key, 5)
        x = jax.random.normal(ks[0], (B, T, C), dtype=jnp.float32)
        w_q = jax.random.normal(ks[1], (H, DK, C), dtype=jnp.float32) / math.sqrt(C)
        w_k = jax.random.normal(ks[2], (H, DK, C), dtype=jnp.float32) / math.sqrt(C)
        w_v = jax.random.normal(ks[3], (H, DV, C), dtype=jnp.float32) / math.sqrt(C)
        w_o = jax.random.normal(ks[4], (H * DV, C), dtype=jnp.float32) / math.sqrt(C)
        return {'x': x, 'w_q': w_q, 'w_k': w_k, 'w_v': w_v, 'w_o': w_o}
    _L0_attn_all = _L0_attn_setup()
    _L0_attn_in = {k: v for k, v in _L0_attn_all.items() if k in ('w_q', 'w_k', 'w_v', 'w_o')}
    del _L0_attn_all

    def _L0_xattn_setup():
        import jax, jax.numpy as jnp
        import numpy as np
        EMBED_DIM = 256
        NUM_HEADS = 16
        HEAD_DIM = EMBED_DIM // NUM_HEADS
        ROPE_BASE = 10000.0

        def _rope_cos_sin(seq_len, dim):
            inv_freq = 1.0 / ROPE_BASE ** (jnp.arange(0, dim, 2, dtype=jnp.float32) / dim)
            freqs = jnp.arange(seq_len, dtype=jnp.float32)[:, None] * inv_freq[None, :]
            emb = jnp.concatenate([freqs, freqs], axis=-1)
            return (jnp.cos(emb), jnp.sin(emb))

        def _rotate_half(x):
            d = x.shape[-1] // 2
            return jnp.concatenate([-x[..., d:], x[..., :d]], axis=-1)
        key = jax.random.key(seed)
        ks = jax.random.split(key, 12)
        B, S, E = (2, 512, EMBED_DIM)
        s = 1.0 / np.sqrt(E)
        return {'query': jax.random.normal(ks[0], (B, S, E), jnp.float32), 'key': jax.random.normal(ks[1], (B, S, E), jnp.float32), 'value': jax.random.normal(ks[2], (B, S, E), jnp.float32), 'mask': jnp.ones((B, 1, 1, S), jnp.int32), 'Wq': jax.random.normal(ks[3], (E, E), jnp.float32) * s, 'bq': jnp.zeros((E,), jnp.float32), 'Wk': jax.random.normal(ks[4], (E, E), jnp.float32) * s, 'bk': jnp.zeros((E,), jnp.float32), 'Wv': jax.random.normal(ks[5], (E, E), jnp.float32) * s, 'bv': jnp.zeros((E,), jnp.float32), 'Wo': jax.random.normal(ks[6], (E, E), jnp.float32) * s, 'bo': jnp.zeros((E,), jnp.float32)}
    _L0_xattn_all = _L0_xattn_setup()
    _L0_xattn_in = {k: v for k, v in _L0_xattn_all.items() if k in ('Wq', 'bq', 'Wk', 'bk', 'Wv', 'bv', 'Wo', 'bo')}
    del _L0_xattn_all

    def _L0_ffn_setup():
        import jax, jax.numpy as jnp
        import numpy as np
        D_MODEL = 256
        EXPERT_DIM = 128
        N_EXPERTS = 8
        TOP_K = 2

        def _sq_relu(h):
            return jnp.square(jax.nn.relu(h))
        key = jax.random.key(seed)
        ks = jax.random.split(key, 6)
        s = 0.02
        x = jax.random.normal(ks[0], (2, 512, D_MODEL), dtype=jnp.float32)
        Ws1 = jax.random.normal(ks[1], (D_MODEL, EXPERT_DIM), dtype=jnp.float32) * s
        Ws2 = jax.random.normal(ks[2], (EXPERT_DIM, D_MODEL), dtype=jnp.float32) * s
        W1 = jax.random.normal(ks[3], (N_EXPERTS, D_MODEL, EXPERT_DIM), dtype=jnp.float32) * s
        W2 = jax.random.normal(ks[4], (N_EXPERTS, EXPERT_DIM, D_MODEL), dtype=jnp.float32) * s
        Wr = jax.random.normal(ks[5], (D_MODEL, N_EXPERTS), dtype=jnp.float32) * s
        return {'x': x, 'Ws1': Ws1, 'Ws2': Ws2, 'W1': W1, 'W2': W2, 'Wr': Wr}
    _L0_ffn_all = _L0_ffn_setup()
    _L0_ffn_in = {k: v for k, v in _L0_ffn_all.items() if k in ('Ws1', 'Ws2', 'W1', 'W2', 'Wr')}
    del _L0_ffn_all

    def _L1_attn_setup():
        import jax, jax.numpy as jnp
        import numpy as np
        E = 256
        H = 16
        D = E // H
        B = 2
        S = 512
        YAT_EPS = 0.1
        key = jax.random.key(seed)
        ks = jax.random.split(key, 5)
        w_scale = (6.0 / (E + E)) ** 0.5

        def xavier(k):
            return jax.random.uniform(k, (E, E), jnp.float32, -w_scale, w_scale)
        return {'x': jax.random.normal(ks[0], (B, S, E), jnp.float32), 'Wq': xavier(ks[1]), 'bq': jnp.zeros((E,), jnp.float32), 'Wk': xavier(ks[2]), 'bk': jnp.zeros((E,), jnp.float32), 'Wv': xavier(ks[3]), 'bv': jnp.zeros((E,), jnp.float32), 'Wo': xavier(ks[4]), 'bo': jnp.zeros((E,), jnp.float32)}
    _L1_attn_all = _L1_attn_setup()
    _L1_attn_in = {k: v for k, v in _L1_attn_all.items() if k in ('Wq', 'bq', 'Wk', 'bk', 'Wv', 'bv', 'Wo', 'bo')}
    del _L1_attn_all

    def _L1_xattn_setup():
        import jax, jax.numpy as jnp
        import numpy as np
        D_MODEL = 256
        NUM_HEADS = 16
        THRESHOLD = 0.1
        key = jax.random.key(seed)
        ks = jax.random.split(key, 12)
        B, L, D, C = (2, 512, D_MODEL, 8)
        s = 1.0 / np.sqrt(D)
        inp = {'q_x': jax.random.normal(ks[0], (B, L, D), jnp.float32), 'k_x': jax.random.normal(ks[1], (B, L, D), jnp.float32), 'v_x': jax.random.normal(ks[2], (B, L, D), jnp.float32), 'energy_coeffs': jax.random.normal(ks[3], (B, L, C), jnp.float32), 'Wq': jax.random.normal(ks[4], (D, D), jnp.float32) * s, 'bq': jnp.zeros((D,), jnp.float32), 'Wk': jax.random.normal(ks[5], (D, D), jnp.float32) * s, 'bk': jnp.zeros((D,), jnp.float32), 'Wv': jax.random.normal(ks[6], (D, D), jnp.float32) * s, 'bv': jnp.zeros((D,), jnp.float32), 'Wo': jax.random.normal(ks[7], (D, D), jnp.float32) * s, 'bo': jnp.zeros((D,), jnp.float32)}
        return inp
    _L1_xattn_all = _L1_xattn_setup()
    _L1_xattn_in = {k: v for k, v in _L1_xattn_all.items() if k in ('Wq', 'bq', 'Wk', 'bk', 'Wv', 'bv', 'Wo', 'bo')}
    del _L1_xattn_all

    def _L1_ffn_setup():
        import jax, jax.numpy as jnp
        import numpy as np
        B, S, DIM = (4, 512, 256)
        E, K, HID = (8, 2, 1024)
        key = jax.random.key(seed)
        ks = jax.random.split(key, 8)
        init = lambda k, sh: jax.random.normal(k, sh, jnp.float32) * 0.02
        return {'x': jax.random.normal(ks[0], (B, S, DIM), jnp.float32), 'gate_w': init(ks[1], (DIM, E)), 'gate_b': jnp.zeros((E,), jnp.float32), 'w1': init(ks[2], (E, DIM, HID)), 'b1': jnp.zeros((E, HID), jnp.float32), 'w2': init(ks[3], (E, HID, DIM)), 'b2': jnp.zeros((E, DIM), jnp.float32), 'ws1': init(ks[4], (DIM, HID)), 'bs1': jnp.zeros((HID,), jnp.float32), 'ws2': init(ks[5], (HID, DIM)), 'bs2': jnp.zeros((DIM,), jnp.float32)}
    _L1_ffn_all = _L1_ffn_setup()
    _L1_ffn_in = {k: v for k, v in _L1_ffn_all.items() if k in ('gate_w', 'gate_b', 'w1', 'b1', 'w2', 'b2', 'ws1', 'bs1', 'ws2', 'bs2')}
    del _L1_ffn_all

    def _L2_attn_setup():
        import jax, jax.numpy as jnp
        import numpy as np
        import math
        EMBED_DIM = 256
        NDIM = 2
        SCALE = math.sqrt(1.0 / NDIM)

        def _ema_kernel(delta, alpha, beta, gamma, length):
            p = jax.nn.sigmoid(delta)
            a = jax.nn.sigmoid(alpha)
            q = 1.0 - p * a
            t = jnp.arange(length, dtype=q.dtype)
            vander = t[None, None, :] * jnp.log(q)
            kernel = p * beta * jnp.exp(vander)
            return jnp.einsum('dnl,dn->dl', kernel, gamma * SCALE)
        key = jax.random.key(seed)
        ks = jax.random.split(key, 6)
        B, S, D, N = (4, 2048, EMBED_DIM, NDIM)
        x = jax.random.normal(ks[0], (B, S, D), dtype=jnp.float32)
        delta = 0.2 * jax.random.normal(ks[1], (D, N, 1), dtype=jnp.float32)
        alpha = 0.2 * jax.random.normal(ks[2], (D, N, 1), dtype=jnp.float32)
        val = jnp.where(jnp.arange(N) % 2 == 1, -1.0, 1.0).reshape(N, 1).astype(jnp.float32)
        beta = 0.02 * jax.random.normal(ks[3], (D, N, 1), dtype=jnp.float32) + val
        gamma = jax.random.normal(ks[4], (D, N), dtype=jnp.float32)
        omega = jax.random.normal(ks[5], (D,), dtype=jnp.float32)
        return {'x': x, 'delta': delta, 'alpha': alpha, 'beta': beta, 'gamma': gamma, 'omega': omega}
    _L2_attn_all = _L2_attn_setup()
    _L2_attn_in = {k: v for k, v in _L2_attn_all.items() if k in ('delta', 'alpha', 'beta', 'gamma', 'omega')}
    del _L2_attn_all

    def _L2_xattn_setup():
        import jax, jax.numpy as jnp
        import numpy as np
        DIM = 256
        HEAD_DIM = 64
        NUM_HEADS = DIM // HEAD_DIM
        SCALE = HEAD_DIM ** (-0.5)
        B, N, M = (2, 256, 1024)
        key = jax.random.key(seed)
        ks = jax.random.split(key, 6)
        x = jax.random.normal(ks[0], (B, N, DIM), dtype=jnp.float32)
        context = jax.random.normal(ks[1], (B, M, DIM), dtype=jnp.float32)
        mask = jax.random.randint(ks[2], (B, N, M), 0, 2).astype(bool)
        Wq = jax.random.normal(ks[3], (DIM, DIM), dtype=jnp.float32) * 0.02
        Wkv = jax.random.normal(ks[4], (2 * DIM, DIM), dtype=jnp.float32) * 0.02
        Wout = jax.random.normal(ks[5], (DIM, DIM), dtype=jnp.float32) * 0.02
        return {'x': x, 'context': context, 'mask': mask, 'Wq': Wq, 'Wkv': Wkv, 'Wout': Wout}
    _L2_xattn_all = _L2_xattn_setup()
    _L2_xattn_in = {k: v for k, v in _L2_xattn_all.items() if k in ('Wq', 'Wkv', 'Wout')}
    del _L2_xattn_all

    def _L2_ffn_setup():
        import jax, jax.numpy as jnp
        import numpy as np
        B, T, D, FF, E, TOP_K = (8, 512, 256, 1024, 8, 2)
        key = jax.random.key(seed)
        kx, kr, k1, k2 = jax.random.split(key, 4)
        x = jax.random.normal(kx, (B, T, D), dtype=jnp.float32)
        Wr = jax.random.normal(kr, (E, D), dtype=jnp.float32) * 0.02
        W1 = jax.random.normal(k1, (E, D, FF), dtype=jnp.float32) * 0.02
        W2 = jax.random.normal(k2, (E, FF, D), dtype=jnp.float32) * 0.02
        return {'x': x, 'Wr': Wr, 'W1': W1, 'W2': W2}
    _L2_ffn_all = _L2_ffn_setup()
    _L2_ffn_in = {k: v for k, v in _L2_ffn_all.items() if k in ('Wr', 'W1', 'W2')}
    del _L2_ffn_all

    def _L3_attn_setup():
        import jax, jax.numpy as jnp
        import numpy as np
        S, B, D, H, C = (256, 1, 256, 16, 64)
        DH = D // H

        def _xavier(key, shape):
            fan_in, fan_out = (shape[1], shape[0])
            a = float(np.sqrt(6.0 / (fan_in + fan_out)))
            return jax.random.uniform(key, shape, jnp.float32, -a, a)
        key = jax.random.key(seed)
        ks = jax.random.split(key, 7)
        x = jax.random.normal(ks[0], (S, B, D), jnp.float32)
        q_c = _xavier(ks[1], (C, D))
        beta = jnp.zeros((H,), jnp.float32)
        Wq = _xavier(ks[2], (D, D))
        bq = jnp.zeros((D,), jnp.float32)
        Wk = _xavier(ks[3], (D, D))
        bk = jnp.zeros((D,), jnp.float32)
        Wv = _xavier(ks[4], (D, D))
        bv = jnp.zeros((D,), jnp.float32)
        Wo = _xavier(ks[5], (D, D))
        bo = jnp.zeros((D,), jnp.float32)
        return {'x': x, 'q_c': q_c, 'beta': beta, 'Wq': Wq, 'bq': bq, 'Wk': Wk, 'bk': bk, 'Wv': Wv, 'bv': bv, 'Wo': Wo, 'bo': bo}
    _L3_attn_all = _L3_attn_setup()
    _L3_attn_in = {k: v for k, v in _L3_attn_all.items() if k in ('q_c', 'beta', 'Wq', 'bq', 'Wk', 'bk', 'Wv', 'bv', 'Wo', 'bo')}
    del _L3_attn_all

    def _L3_xattn_setup():
        import jax, jax.numpy as jnp
        import numpy as np
        EMB = 256
        HEADS = 16
        HEAD_DIM = EMB // HEADS
        key = jax.random.key(seed)
        ks = jax.random.split(key, 7)
        B, Q, KV = (2, 512, 1024)
        s = 1.0 / np.sqrt(EMB)
        return {'x': jax.random.normal(ks[0], (B, Q, EMB), dtype=jnp.float32), 'context': jax.random.normal(ks[1], (B, KV, EMB), dtype=jnp.float32), 'Wq': jax.random.normal(ks[2], (EMB, EMB), dtype=jnp.float32) * s, 'Wk': jax.random.normal(ks[3], (EMB, EMB), dtype=jnp.float32) * s, 'Wv': jax.random.normal(ks[4], (EMB, EMB), dtype=jnp.float32) * s, 'Wo': jax.random.normal(ks[5], (EMB, EMB), dtype=jnp.float32) * s, 'bo': jax.random.normal(ks[6], (EMB,), dtype=jnp.float32) * 0.01}
    _L3_xattn_all = _L3_xattn_setup()
    _L3_xattn_in = {k: v for k, v in _L3_xattn_all.items() if k in ('Wq', 'Wk', 'Wv', 'Wo', 'bo')}
    del _L3_xattn_all

    def _L3_ffn_setup():
        import jax, jax.numpy as jnp
        import numpy as np
        B, S, D, E = (4, 1024, 256, 8)
        key = jax.random.key(seed)
        k1, k2, k3, k4, k5 = jax.random.split(key, 5)
        scale = 1.0 / np.sqrt(D)
        return {'x': jax.random.normal(k1, (B, S, D), dtype=jnp.float32), 'Wg': jax.random.normal(k2, (D, D), dtype=jnp.float32) * scale, 'bg': jnp.zeros((D,), dtype=jnp.float32), 'We': jax.random.normal(k3, (E, D, D), dtype=jnp.float32) * scale, 'be': jnp.zeros((E, D), dtype=jnp.float32)}
    _L3_ffn_all = _L3_ffn_setup()
    _L3_ffn_in = {k: v for k, v in _L3_ffn_all.items() if k in ('Wg', 'bg', 'We', 'be')}
    del _L3_ffn_all
    return {'x': x, 'ctx_1024': ctx_1024, 'ctxb_2048x8': ctxb_2048x8, 'mask_Bx1x1xS2_if1': mask_Bx1x1xS2_if1, 'mask_BxSxS2_bk0': mask_BxSxS2_bk0, 'L0_attn_w_q': _L0_attn_in['w_q'], 'L0_attn_w_k': _L0_attn_in['w_k'], 'L0_attn_w_v': _L0_attn_in['w_v'], 'L0_attn_w_o': _L0_attn_in['w_o'], 'L0_xattn_Wq': _L0_xattn_in['Wq'], 'L0_xattn_bq': _L0_xattn_in['bq'], 'L0_xattn_Wk': _L0_xattn_in['Wk'], 'L0_xattn_bk': _L0_xattn_in['bk'], 'L0_xattn_Wv': _L0_xattn_in['Wv'], 'L0_xattn_bv': _L0_xattn_in['bv'], 'L0_xattn_Wo': _L0_xattn_in['Wo'], 'L0_xattn_bo': _L0_xattn_in['bo'], 'L0_ffn_Ws1': _L0_ffn_in['Ws1'], 'L0_ffn_Ws2': _L0_ffn_in['Ws2'], 'L0_ffn_W1': _L0_ffn_in['W1'], 'L0_ffn_W2': _L0_ffn_in['W2'], 'L0_ffn_Wr': _L0_ffn_in['Wr'], 'L1_attn_Wq': _L1_attn_in['Wq'], 'L1_attn_bq': _L1_attn_in['bq'], 'L1_attn_Wk': _L1_attn_in['Wk'], 'L1_attn_bk': _L1_attn_in['bk'], 'L1_attn_Wv': _L1_attn_in['Wv'], 'L1_attn_bv': _L1_attn_in['bv'], 'L1_attn_Wo': _L1_attn_in['Wo'], 'L1_attn_bo': _L1_attn_in['bo'], 'L1_xattn_Wq': _L1_xattn_in['Wq'], 'L1_xattn_bq': _L1_xattn_in['bq'], 'L1_xattn_Wk': _L1_xattn_in['Wk'], 'L1_xattn_bk': _L1_xattn_in['bk'], 'L1_xattn_Wv': _L1_xattn_in['Wv'], 'L1_xattn_bv': _L1_xattn_in['bv'], 'L1_xattn_Wo': _L1_xattn_in['Wo'], 'L1_xattn_bo': _L1_xattn_in['bo'], 'L1_ffn_gate_w': _L1_ffn_in['gate_w'], 'L1_ffn_gate_b': _L1_ffn_in['gate_b'], 'L1_ffn_w1': _L1_ffn_in['w1'], 'L1_ffn_b1': _L1_ffn_in['b1'], 'L1_ffn_w2': _L1_ffn_in['w2'], 'L1_ffn_b2': _L1_ffn_in['b2'], 'L1_ffn_ws1': _L1_ffn_in['ws1'], 'L1_ffn_bs1': _L1_ffn_in['bs1'], 'L1_ffn_ws2': _L1_ffn_in['ws2'], 'L1_ffn_bs2': _L1_ffn_in['bs2'], 'L2_attn_delta': _L2_attn_in['delta'], 'L2_attn_alpha': _L2_attn_in['alpha'], 'L2_attn_beta': _L2_attn_in['beta'], 'L2_attn_gamma': _L2_attn_in['gamma'], 'L2_attn_omega': _L2_attn_in['omega'], 'L2_xattn_Wq': _L2_xattn_in['Wq'], 'L2_xattn_Wkv': _L2_xattn_in['Wkv'], 'L2_xattn_Wout': _L2_xattn_in['Wout'], 'L2_ffn_Wr': _L2_ffn_in['Wr'], 'L2_ffn_W1': _L2_ffn_in['W1'], 'L2_ffn_W2': _L2_ffn_in['W2'], 'L3_attn_q_c': _L3_attn_in['q_c'], 'L3_attn_beta': _L3_attn_in['beta'], 'L3_attn_Wq': _L3_attn_in['Wq'], 'L3_attn_bq': _L3_attn_in['bq'], 'L3_attn_Wk': _L3_attn_in['Wk'], 'L3_attn_bk': _L3_attn_in['bk'], 'L3_attn_Wv': _L3_attn_in['Wv'], 'L3_attn_bv': _L3_attn_in['bv'], 'L3_attn_Wo': _L3_attn_in['Wo'], 'L3_attn_bo': _L3_attn_in['bo'], 'L3_xattn_Wq': _L3_xattn_in['Wq'], 'L3_xattn_Wk': _L3_xattn_in['Wk'], 'L3_xattn_Wv': _L3_xattn_in['Wv'], 'L3_xattn_Wo': _L3_xattn_in['Wo'], 'L3_xattn_bo': _L3_xattn_in['bo'], 'L3_ffn_Wg': _L3_ffn_in['Wg'], 'L3_ffn_bg': _L3_ffn_in['bg'], 'L3_ffn_We': _L3_ffn_in['We'], 'L3_ffn_be': _L3_ffn_in['be']}

def reference(x, ctx_1024, ctxb_2048x8, mask_Bx1x1xS2_if1, mask_BxSxS2_bk0, L0_attn_w_q, L0_attn_w_k, L0_attn_w_v, L0_attn_w_o, L0_xattn_Wq, L0_xattn_bq, L0_xattn_Wk, L0_xattn_bk, L0_xattn_Wv, L0_xattn_bv, L0_xattn_Wo, L0_xattn_bo, L0_ffn_Ws1, L0_ffn_Ws2, L0_ffn_W1, L0_ffn_W2, L0_ffn_Wr, L1_attn_Wq, L1_attn_bq, L1_attn_Wk, L1_attn_bk, L1_attn_Wv, L1_attn_bv, L1_attn_Wo, L1_attn_bo, L1_xattn_Wq, L1_xattn_bq, L1_xattn_Wk, L1_xattn_bk, L1_xattn_Wv, L1_xattn_bv, L1_xattn_Wo, L1_xattn_bo, L1_ffn_gate_w, L1_ffn_gate_b, L1_ffn_w1, L1_ffn_b1, L1_ffn_w2, L1_ffn_b2, L1_ffn_ws1, L1_ffn_bs1, L1_ffn_ws2, L1_ffn_bs2, L2_attn_delta, L2_attn_alpha, L2_attn_beta, L2_attn_gamma, L2_attn_omega, L2_xattn_Wq, L2_xattn_Wkv, L2_xattn_Wout, L2_ffn_Wr, L2_ffn_W1, L2_ffn_W2, L3_attn_q_c, L3_attn_beta, L3_attn_Wq, L3_attn_bq, L3_attn_Wk, L3_attn_bk, L3_attn_Wv, L3_attn_bv, L3_attn_Wo, L3_attn_bo, L3_xattn_Wq, L3_xattn_Wk, L3_xattn_Wv, L3_xattn_Wo, L3_xattn_bo, L3_ffn_Wg, L3_ffn_bg, L3_ffn_We, L3_ffn_be):
    import jax
    import jax.numpy as jnp

    def _L0_attn_ref(x, w_q, w_k, w_v, w_o):
        import jax, jax.numpy as jnp
        import numpy as np
        import math
        B, T, C = (2, 512, 256)
        H, DK, DV = (16, 64, 64)
        dk = w_q.shape[1]
        q = jnp.einsum('ntc,hdc->nhtd', x, w_q)
        k = jnp.einsum('ntc,hdc->nhtd', x, w_k)
        v = jnp.einsum('ntc,hdc->nhtd', x, w_v)
        a = jnp.einsum('nhtd,nhsd->nhts', q, k) / jnp.sqrt(jnp.asarray(dk, x.dtype))
        t = a.shape[-1]
        mask = jnp.arange(t)[:, None] < jnp.arange(t)[None, :]
        a = jnp.where(mask[None, None], jnp.asarray(-jnp.inf, a.dtype), a)
        a = jax.nn.softmax(a, axis=-1)
        y = jnp.einsum('nhts,nhsd->nthd', a, v)
        y = y.reshape(y.shape[0], y.shape[1], -1)
        return y @ w_o

    def _L0_xattn_ref(query, key, value, mask, Wq, bq, Wk, bk, Wv, bv, Wo, bo):
        import jax, jax.numpy as jnp
        import numpy as np
        EMBED_DIM = 256
        NUM_HEADS = 16
        HEAD_DIM = EMBED_DIM // NUM_HEADS
        ROPE_BASE = 10000.0

        def _rope_cos_sin(seq_len, dim):
            inv_freq = 1.0 / ROPE_BASE ** (jnp.arange(0, dim, 2, dtype=jnp.float32) / dim)
            freqs = jnp.arange(seq_len, dtype=jnp.float32)[:, None] * inv_freq[None, :]
            emb = jnp.concatenate([freqs, freqs], axis=-1)
            return (jnp.cos(emb), jnp.sin(emb))

        def _rotate_half(x):
            d = x.shape[-1] // 2
            return jnp.concatenate([-x[..., d:], x[..., :d]], axis=-1)
        B, Sq, E = query.shape
        Sk = key.shape[1]
        H, D = (NUM_HEADS, HEAD_DIM)
        q = (query @ Wq + bq).reshape(B, Sq, H, D)
        k = (key @ Wk + bk).reshape(B, Sk, H, D)
        v = (value @ Wv + bv).reshape(B, Sk, H, D)
        cos, sin = _rope_cos_sin(max(Sq, Sk), D)
        cq, sq_ = (cos[:Sq][None, :, None, :], sin[:Sq][None, :, None, :])
        ck, sk_ = (cos[:Sk][None, :, None, :], sin[:Sk][None, :, None, :])
        q = q * cq + _rotate_half(q) * sq_
        k = k * ck + _rotate_half(k) * sk_
        scores = jnp.einsum('bqhd,bkhd->bhqk', q, k) / jnp.sqrt(jnp.float32(D))
        scores = jnp.where(mask == 0, jnp.float32(-1e+30), scores)
        attn = jax.nn.softmax(scores, axis=-1)
        ctx = jnp.einsum('bhqk,bkhd->bqhd', attn, v).reshape(B, Sq, E)
        return ctx @ Wo + bo

    def _L0_ffn_ref(x, Ws1, Ws2, W1, W2, Wr):
        import jax, jax.numpy as jnp
        import numpy as np
        D_MODEL = 256
        EXPERT_DIM = 128
        N_EXPERTS = 8
        TOP_K = 2

        def _sq_relu(h):
            return jnp.square(jax.nn.relu(h))
        shape = x.shape
        xf = x.reshape(-1, D_MODEL)
        out_shared = _sq_relu(xf @ Ws1) @ Ws2
        logits = xf @ Wr
        top_vals, top_idx = jax.lax.top_k(logits, TOP_K)
        rw = jax.nn.softmax(top_vals.astype(jnp.float32), axis=-1).astype(x.dtype)
        onehot = jax.nn.one_hot(top_idx, N_EXPERTS, dtype=x.dtype)
        prob = jnp.einsum('tk,tke->te', rw, onehot)
        prob = jnp.trunc(prob)
        h = _sq_relu(jnp.einsum('td,edf->tef', xf, W1))
        y = jnp.einsum('tef,efd->ted', h, W2)
        out_routed = jnp.einsum('ted,te->td', y, prob)
        return (out_shared + out_routed).reshape(shape)

    def _L1_attn_ref(x, Wq, bq, Wk, bk, Wv, bv, Wo, bo):
        import jax, jax.numpy as jnp
        import numpy as np
        E = 256
        H = 16
        D = E // H
        B = 2
        S = 512
        YAT_EPS = 0.1
        b, s, _ = x.shape
        Q = x @ Wq + bq
        K = x @ Wk + bk
        V = x @ Wv + bv
        Q = Q.reshape(b, s, H, D).transpose(0, 2, 1, 3)
        K = K.reshape(b, s, H, D).transpose(0, 2, 1, 3)
        V = V.reshape(b, s, H, D).transpose(0, 2, 1, 3)
        Qn = Q / (jnp.linalg.norm(Q, axis=-1, keepdims=True) + 1e-08)
        Kn = K / (jnp.linalg.norm(K, axis=-1, keepdims=True) + 1e-08)
        dot = jnp.einsum('bhqd,bhkd->bhqk', Qn, Kn)
        scores = (1.0 + dot) ** 2 / (YAT_EPS + (1.0 - dot))
        attn = scores / (jnp.sum(scores, axis=-1, keepdims=True) + 1e-06)
        out = jnp.einsum('bhqk,bhkd->bhqd', attn, V)
        out = out.transpose(0, 2, 1, 3).reshape(b, s, E)
        return out @ Wo + bo

    def _L1_xattn_ref(q_x, k_x, v_x, energy_coeffs, Wq, bq, Wk, bk, Wv, bv, Wo, bo):
        import jax, jax.numpy as jnp
        import numpy as np
        D_MODEL = 256
        NUM_HEADS = 16
        THRESHOLD = 0.1
        B, L, D = q_x.shape
        H = NUM_HEADS
        Dh = D // H

        def proj(x, W, b):
            y = x @ W + b
            return y.reshape(B, -1, H, Dh).transpose(0, 2, 1, 3)
        Q = proj(q_x, Wq, bq)
        K = proj(k_x, Wk, bk)
        V = proj(v_x, Wv, bv)
        scores = jnp.einsum('bhqd,bhkd->bhqk', Q, K) / np.sqrt(Dh).astype(np.float32)
        attn = jax.nn.softmax(scores, axis=-1)
        attn = jnp.nan_to_num(attn, nan=0.0)
        energy = jnp.abs(energy_coeffs).mean(axis=-1)
        gate = jax.nn.sigmoid((energy - THRESHOLD) * 10.0)[:, None, None, :]
        attn = attn * gate
        out = jnp.einsum('bhqk,bhkd->bhqd', attn, V)
        out = out.transpose(0, 2, 1, 3).reshape(B, L, D)
        return out @ Wo + bo

    def _L1_ffn_ref(x, gate_w, gate_b, w1, b1, w2, b2, ws1, bs1, ws2, bs2):
        import jax, jax.numpy as jnp
        import numpy as np
        B, S, DIM = (4, 512, 256)
        E, K, HID = (8, 2, 1024)
        orig_shape = x.shape
        xf = x.reshape(-1, DIM)
        logits = xf @ gate_w + gate_b
        top_w, top_i = jax.lax.top_k(logits, K)
        gw = jax.nn.softmax(top_w, axis=-1).astype(xf.dtype)
        combine = (gw[:, :, None] * jax.nn.one_hot(top_i, E, dtype=xf.dtype)).sum(axis=1)
        out = jnp.zeros_like(xf)
        for e in range(E):
            h = jax.nn.gelu(xf @ w1[e] + b1[e], approximate=False)
            out = out + combine[:, e:e + 1] * (h @ w2[e] + b2[e])
        shared = jax.nn.gelu(xf @ ws1 + bs1, approximate=False) @ ws2 + bs2
        return (out + shared).reshape(orig_shape)

    def _L2_attn_ref(x, delta, alpha, beta, gamma, omega):
        import jax, jax.numpy as jnp
        import numpy as np
        import math
        EMBED_DIM = 256
        NDIM = 2
        SCALE = math.sqrt(1.0 / NDIM)

        def _ema_kernel(delta, alpha, beta, gamma, length):
            p = jax.nn.sigmoid(delta)
            a = jax.nn.sigmoid(alpha)
            q = 1.0 - p * a
            t = jnp.arange(length, dtype=q.dtype)
            vander = t[None, None, :] * jnp.log(q)
            kernel = p * beta * jnp.exp(vander)
            return jnp.einsum('dnl,dn->dl', kernel, gamma * SCALE)
        B, S, D = x.shape
        residual = x * omega
        xt = jnp.transpose(x, (0, 2, 1))
        k = _ema_kernel(delta, alpha, beta, gamma, S)
        n = 2 * S
        k_f = jnp.fft.rfft(k.astype(jnp.float32), n=n)
        x_f = jnp.fft.rfft(xt.astype(jnp.float32), n=n)
        out = jnp.fft.irfft(x_f * k_f, n=n)[..., :S]
        out = out.astype(x.dtype)
        return jax.nn.silu(jnp.transpose(out, (0, 2, 1)) + residual)

    def _L2_xattn_ref(x, context, mask, Wq, Wkv, Wout):
        import jax, jax.numpy as jnp
        import numpy as np
        DIM = 256
        HEAD_DIM = 64
        NUM_HEADS = DIM // HEAD_DIM
        SCALE = HEAD_DIM ** (-0.5)
        B, N, M = (2, 256, 1024)
        b, n, c = x.shape
        m = context.shape[1]
        h, d = (NUM_HEADS, HEAD_DIM)
        q = (x @ Wq.T).reshape(b, n, h, d).transpose(0, 2, 1, 3)
        kv = (context @ Wkv.T).reshape(b, m, 2, h, d)
        k = kv[:, :, 0].transpose(0, 2, 1, 3)
        v = kv[:, :, 1].transpose(0, 2, 1, 3)
        attn = jnp.einsum('bhnd,bhmd->bhnm', q, k) * SCALE
        attn = jnp.where(mask[:, None, :, :], attn, -jnp.inf)
        attn = jax.nn.softmax(attn, axis=-1)
        out = jnp.einsum('bhnm,bhmd->bhnd', attn, v)
        out = out.transpose(0, 2, 1, 3).reshape(b, n, c)
        return out @ Wout.T

    def _L2_ffn_ref(x, Wr, W1, W2):
        import jax, jax.numpy as jnp
        import numpy as np
        B, T, D, FF, E, TOP_K = (8, 512, 256, 1024, 8, 2)
        Bs, Ts, Ds = x.shape
        Ne = Wr.shape[0]
        xf = x.reshape(-1, Ds)
        N = xf.shape[0]
        logits = xf @ Wr.T
        topk_vals, topk_idx = jax.lax.top_k(logits, TOP_K)
        w = jax.nn.softmax(topk_vals.astype(jnp.float32), axis=-1).astype(x.dtype)
        idx_flat = topk_idx.reshape(-1)
        w_flat = w.reshape(-1)
        sort_idx = jnp.argsort(idx_flat)
        rev = sort_idx // TOP_K
        sw = w_flat[sort_idx]
        perm = xf[rev]
        S = perm.shape[0]
        chunks = perm.reshape(Ne, S // Ne, Ds)
        h = jax.nn.gelu(jnp.einsum('ecd,edf->ecf', chunks, W1), approximate=False)
        eo = jnp.einsum('ecf,efd->ecd', h, W2).reshape(S, Ds)
        out = jnp.zeros((N, Ds), dtype=x.dtype).at[rev].add(eo * sw[:, None])
        return out.reshape(Bs, Ts, Ds)

    def _L3_attn_ref(x, q_c, beta, Wq, bq, Wk, bk, Wv, bv, Wo, bo):
        import jax, jax.numpy as jnp
        import numpy as np
        S, B, D, H, C = (256, 1, 256, 16, 64)
        DH = D // H

        def _xavier(key, shape):
            fan_in, fan_out = (shape[1], shape[0])
            a = float(np.sqrt(6.0 / (fan_in + fan_out)))
            return jax.random.uniform(key, shape, jnp.float32, -a, a)
        s_len, bsz, d_model = x.shape
        h, dh = (H, DH)
        c_len = q_c.shape[0]

        def proj(W, b):
            return (x @ W.T + b).reshape(s_len, bsz, h, dh).transpose(1, 2, 0, 3)
        q = proj(Wq, bq)
        k = proj(Wk, bk)
        v = proj(Wv, bv)
        qc = q_c.reshape(c_len, h, dh).transpose(1, 0, 2)
        cw = jnp.einsum('hcd,bhsd->bhcs', qc, k)
        cw = jnp.exp(cw - jnp.max(cw, axis=-1, keepdims=True))
        norm = jnp.cumsum(cw, axis=-1)
        kv = jnp.concatenate([k, v], axis=-1)
        kv_c = jnp.cumsum(cw[..., None] * kv[:, :, None, :, :], axis=3) / norm[..., None]
        k_c, v_c = (kv_c[..., :dh], kv_c[..., dh:])
        q = q / (jnp.sqrt(jnp.float32(dh)) * jnp.exp(beta)[None, :, None, None])
        sw = jax.nn.softmax(jnp.einsum('bhsd,bhcsd->bhsc', q, k_c), axis=-1)
        o = jnp.einsum('bhsc,bhcsd->bhsd', sw, v_c)
        o = o.transpose(2, 0, 1, 3).reshape(s_len, bsz, d_model)
        return o @ Wo.T + bo

    def _L3_xattn_ref(x, context, Wq, Wk, Wv, Wo, bo):
        import jax, jax.numpy as jnp
        import numpy as np
        EMB = 256
        HEADS = 16
        HEAD_DIM = EMB // HEADS
        B, Qlen, _ = x.shape
        KVlen = context.shape[1]
        scale = jnp.asarray(HEAD_DIM ** 0.5, x.dtype)
        q = (x @ Wq.T).reshape(B, Qlen, HEADS, HEAD_DIM).transpose(0, 2, 1, 3)
        k = (context @ Wk.T).reshape(B, KVlen, HEADS, HEAD_DIM).transpose(0, 2, 1, 3)
        v = (context @ Wv.T).reshape(B, KVlen, HEADS, HEAD_DIM).transpose(0, 2, 1, 3)
        scores = jnp.einsum('bhqd,bhkd->bhqk', q, k) / scale
        attn = jax.nn.softmax(scores, axis=-1)
        out = jnp.einsum('bhqk,bhkd->bhqd', attn, v)
        out = out.transpose(0, 2, 1, 3).reshape(B, Qlen, EMB)
        return out @ Wo.T + bo

    def _L3_ffn_ref(x, Wg, bg, We, be):
        import jax, jax.numpy as jnp
        import numpy as np
        B, S, D, E = (4, 1024, 256, 8)
        probs = jax.nn.softmax(x @ Wg + bg, axis=-1)
        idx = jnp.argmax(probs, axis=-1)
        p = jnp.take_along_axis(probs, idx[..., None], axis=-1)[..., 0]
        e_idx = idx % We.shape[0]
        h = jax.nn.relu(jnp.einsum('bsd,edf->besf', x, We) + be[None, :, None, :])
        onehot = jax.nn.one_hot(e_idx, We.shape[0], dtype=x.dtype)
        out = jnp.einsum('besf,bse->bsf', h, onehot) * p[..., None]
        return out
    x = x + _L0_attn_ref(_layernorm(x, axis=-1), L0_attn_w_q, L0_attn_w_k, L0_attn_w_v, L0_attn_w_o)
    x = x + _L0_xattn_ref(_layernorm(x, axis=-1), ctx_1024, ctx_1024, mask_Bx1x1xS2_if1, L0_xattn_Wq, L0_xattn_bq, L0_xattn_Wk, L0_xattn_bk, L0_xattn_Wv, L0_xattn_bv, L0_xattn_Wo, L0_xattn_bo)
    x = x + _L0_ffn_ref(_layernorm(x, axis=-1), L0_ffn_Ws1, L0_ffn_Ws2, L0_ffn_W1, L0_ffn_W2, L0_ffn_Wr)
    x = x + _L1_attn_ref(_layernorm(x, axis=-1), L1_attn_Wq, L1_attn_bq, L1_attn_Wk, L1_attn_bk, L1_attn_Wv, L1_attn_bv, L1_attn_Wo, L1_attn_bo)
    x = x + _L1_xattn_ref(_layernorm(x, axis=-1), ctx_1024, ctx_1024, ctxb_2048x8, L1_xattn_Wq, L1_xattn_bq, L1_xattn_Wk, L1_xattn_bk, L1_xattn_Wv, L1_xattn_bv, L1_xattn_Wo, L1_xattn_bo)
    x = x + _L1_ffn_ref(_layernorm(x, axis=-1), L1_ffn_gate_w, L1_ffn_gate_b, L1_ffn_w1, L1_ffn_b1, L1_ffn_w2, L1_ffn_b2, L1_ffn_ws1, L1_ffn_bs1, L1_ffn_ws2, L1_ffn_bs2)
    x = x + _L2_attn_ref(_layernorm(x, axis=-1), L2_attn_delta, L2_attn_alpha, L2_attn_beta, L2_attn_gamma, L2_attn_omega)
    x = x + _L2_xattn_ref(_layernorm(x, axis=-1), ctx_1024, mask_BxSxS2_bk0, L2_xattn_Wq, L2_xattn_Wkv, L2_xattn_Wout)
    x = x + _L2_ffn_ref(_layernorm(x, axis=-1), L2_ffn_Wr, L2_ffn_W1, L2_ffn_W2)
    x = x + _L3_attn_ref(_layernorm(x, axis=-1), L3_attn_q_c, L3_attn_beta, L3_attn_Wq, L3_attn_bq, L3_attn_Wk, L3_attn_bk, L3_attn_Wv, L3_attn_bv, L3_attn_Wo, L3_attn_bo)
    x = x + _L3_xattn_ref(_layernorm(x, axis=-1), ctx_1024, L3_xattn_Wq, L3_xattn_Wk, L3_xattn_Wv, L3_xattn_Wo, L3_xattn_bo)
    x = x + _L3_ffn_ref(_layernorm(x, axis=-1), L3_ffn_Wg, L3_ffn_bg, L3_ffn_We, L3_ffn_be)
    return x

_drawn_inputs = setup_inputs


def setup_inputs(seed=0):
    import zlib

    import numpy as np

    out = dict(_drawn_inputs(seed))
    spreads = {'L0_xattn_bq': (0.0, 0.1),
     'L0_xattn_bk': (0.0, 0.1),
     'L0_xattn_bv': (0.0, 0.1),
     'L0_xattn_bo': (0.0, 0.1),
     'L1_attn_bq': (0.0, 0.1),
     'L1_attn_bk': (0.0, 0.1),
     'L1_attn_bv': (0.0, 0.1),
     'L1_attn_bo': (0.0, 0.1),
     'L1_xattn_bq': (0.0, 0.1),
     'L1_xattn_bk': (0.0, 0.1),
     'L1_xattn_bv': (0.0, 0.1),
     'L1_xattn_bo': (0.0, 0.1),
     'L1_ffn_gate_b': (0.0, 0.1),
     'L1_ffn_b1': (0.0, 0.1),
     'L1_ffn_b2': (0.0, 0.1),
     'L1_ffn_bs1': (0.0, 0.1),
     'L1_ffn_bs2': (0.0, 0.1),
     'L3_attn_beta': (0.0, 0.1),
     'L3_attn_bq': (0.0, 0.1),
     'L3_attn_bk': (0.0, 0.1),
     'L3_attn_bv': (0.0, 0.1),
     'L3_attn_bo': (0.0, 0.1),
     'L3_ffn_bg': (0.0, 0.1),
     'L3_ffn_be': (0.0, 0.1)}
    factors = {}
    for name, (base, spread) in spreads.items():
        noise = np.random.default_rng([zlib.crc32(name.encode()), seed]).standard_normal(out[name].shape)
        drawn = base * np.exp(spread * noise) if base else spread * noise
        out[name] = jnp.asarray(drawn.astype(out[name].dtype))
    for name, factor in factors.items():
        out[name] = (out[name] * factor).astype(out[name].dtype)
    return out
```

```python
from contextlib import ExitStack

import numpy as np

import concourse.bass as bass
from concourse import mybir

B, S, E = 8, 100, 256
P = 128
KC = E // P
SKV = 361
CH = 121
NCH = 3
PADKV = CH * NCH
LAST = SKV - CH * (NCH - 1)
EPS = 1e-5
NEG = -1e30
NE = 8

ALU = mybir.AluOpType
ACT = mybir.ActivationFunctionType
F32 = mybir.dt.float32
I32 = mybir.dt.int32
U32 = mybir.dt.uint32
U8 = mybir.dt.uint8
X_AX = mybir.AxisListType.X


class Net:

    def __init__(self, nc, ctx, dram):
        self.nc, self.ctx, self.dram = nc, ctx, dram
        self.x = ctx.enter_context(nc.sbuf_tensor("x", [S, B, E], F32))
        self.ident = ctx.enter_context(nc.sbuf_tensor("ident", [P, P], F32))
        self.stats = ctx.enter_context(nc.sbuf_tensor("stats", [S, B, 6], F32))
        self.moments = ctx.enter_context(nc.sbuf_tensor("moments", [S, B, 2], F32))
        self.std = ctx.enter_context(nc.sbuf_tensor("std", [S, B, 1], F32))
        self.rstd = ctx.enter_context(nc.sbuf_tensor("rstd", [S, B, 1], F32))
        self.wide = ctx.enter_context(nc.psum_tensor("wide", [P, 4, 512], F32))
        self.turned = ctx.enter_context(nc.psum_tensor("turned", [P, 2, 512], F32))
        self.summed = ctx.enter_context(nc.psum_tensor("summed", [P, 2, 512], F32))

        self.sems = []

    def sem(self, name):
        self.sems.append(self.nc.alloc_semaphore(name=name))
        return self.sems[-1]

    def end_sublayer(self):
        self.nc.clear_and_free_semaphores(self.sems)
        self.nc.all_engine_barrier()
        self.sems = []


def sublayer(emit):
    def whole(net, *args, **kwargs):
        emit(net, *args, **kwargs)
        net.end_sublayer()
    return whole


def load_weights(sp, net, pairs, loaded):
    for tile, source in pairs:
        sp.dma_start(tile, source).then_inc(loaded, 16)
    return 16 * len(pairs)


def norm_stats_vector(dve, net, var_ready, std_ready):
    with dve.Fori(0, B) as b:
        dve.bn_stats(net.stats[:, b, :], net.x[:, b, :])
    dve.drain()
    for b in range(B):
        dve.bn_aggr(net.moments[:, b, :], net.stats[:, b, :])
    dve.drain()
    dve.tensor_scalar(net.std[:], net.moments[:, :, 1:2], EPS, None, ALU.add).then_inc(var_ready, 1)
    dve.wait_ge(std_ready, 1)
    dve.reciprocal(net.rstd[:], net.std[:])
    dve.drain()


def norm_stats_scalar(act, net, var_ready, std_ready):
    act.wait_ge(var_ready, 1)
    act.activation(net.std[:], net.std[:], ACT.Sqrt).then_inc(std_ready, 1)


def normalise(dve, net, out, b):
    return dve.tensor_scalar(out, net.x[:, b, :], net.moments[:, b, 0:1], net.rstd[:, b, :],
                             ALU.subtract, ALU.mult)


@sublayer
def setup(net):
    nc = net.nc
    loaded = net.sem("setup_loaded")
    with nc.Block() as block:
        @block.sync
        def _(sp):
            sp.dma_start(net.x[:], net.dram["x"].rearrange("b s d -> s b d")).then_inc(loaded, 16)
            sp.dma_start(net.ident[:], net.dram["ident"]).then_inc(loaded, 16)
            sp.wait_ge(loaded, 32)


def store(net):
    nc = net.nc
    stored = net.sem("stored")
    with nc.Block() as block:
        @block.sync
        def _(sp):
            sp.dma_start(net.dram["out"].rearrange("b s d -> s b d"), net.x[:]).then_inc(stored, 16)
            sp.wait_ge(stored, 16)


@sublayer
def l0_attn(net):
    nc, dram = net.nc, net.dram
    H, D, G = 16, 64, 4
    HD = H * D
    MC = HD // P
    PER = MC // 2
    NG = H // G

    def first_head(g):
        return (g // 2) * 2 * G + g % 2

    with ExitStack() as ctx:
        def sb(name, shape, dt=F32):
            return ctx.enter_context(nc.sbuf_tensor("l0a_" + name, shape, dt))

        wq, wk, wv = (sb(n, [P, KC, HD]) for n in ("wq", "wk", "wv"))
        wo = sb("wo", [P, MC, E])
        causal = sb("causal", [S, S])
        xn = sb("xn", [S, E])
        xt = sb("xt", [P, KC, S])
        qt, kt = sb("qt", [P, MC, S]), sb("kt", [P, MC, S])
        v1 = sb("v1", [S, H, D + 1])
        sc = sb("sc", [S, 2, G, S])
        mx = sb("mx", [S, H])
        pr = sb("pr", [S, 2, G, S])
        pt = sb("pt", [S, 2, G, S])
        rs = sb("rs", [S, H])
        y = sb("y", [S, H, D])
        yt = sb("yt", [P, MC, S])

        loaded, var_ready, std_ready, v1_ones, xn_ready, xt_psum, xt_ready, qk_psum, v_psum, q_ready, k_ready, v_ready, \
            s_psum, s_ready, p_ready, pt_psum, pt_ready, y_psum, y_ready, yt_psum, yt_ready, out_psum = (
                net.sem("l0a_" + n) for n in (
                    "loaded", "var_ready", "std_ready", "v1_ones", "xn_ready", "xt_psum", "xt_ready", "qk_psum", "v_psum",
                    "q_ready", "k_ready", "v_ready", "s_psum", "s_ready", "p_ready", "pt_psum", "pt_ready",
                    "y_psum", "y_ready", "yt_psum", "yt_ready", "out_psum"))
        wide, turned, summed = net.wide, net.turned, net.summed

        with nc.Block() as block:
            @block.sync
            def _(sp):
                load_weights(sp, net, [(wq[:], dram["l0a_wq"]), (wk[:], dram["l0a_wk"]), (wv[:], dram["l0a_wv"]),
                                       (wo[:], dram["l0a_wo"]), (causal[:], dram["causal"])], loaded)

            @block.tensor
            def _(pe):
                pe.wait_ge(loaded, 80)
                with pe.Fori(0, B) as b:
                    pe.wait_ge(xn_ready, b + 1)
                    for k in range(KC):
                        last = pe.transpose(turned[:, 0, k * S:(k + 1) * S], xn[:, k * P:(k + 1) * P], net.ident[0:S, 0:S])
                    last.then_inc(xt_psum, 1)
                    pe.wait_ge(xt_ready, b + 1)
                    for w, bank in ((wq, 0), (wk, 2)):
                        for m in range(MC):
                            for k in range(KC):
                                last = pe.matmul(wide[:, bank + m // PER, (m % PER) * S:(m % PER + 1) * S],
                                                 w[:, k, m * P:(m + 1) * P], xt[:, k, :], start=k == 0, stop=k == KC - 1)
                        last.then_inc(qk_psum, 1)
                    for n in range(2):
                        for k in range(KC):
                            last = pe.matmul(summed[0:S, n, :], xt[:, k, :], wv[:, k, n * 512:(n + 1) * 512],
                                             start=k == 0, stop=k == KC - 1)
                    last.then_inc(v_psum, 1)

                    def scores(g):
                        r = (g % 2) * D
                        for j in range(G):
                            m = first_head(g) // 2 + j
                            last = pe.matmul(wide[0:S, g, j * S:(j + 1) * S], qt[r:r + D, m, :],
                                             kt[r:r + D, m, :], start=True, stop=True)
                        last.then_inc(s_psum, 1)

                    def turn(g):
                        pe.wait_ge(p_ready, b * NG + g + 1)
                        if g >= 2:
                            pe.wait_ge(pt_ready, b * NG + g - 1)
                        for j in range(G):
                            last = pe.transpose(turned[0:S, g % 2, j * S:(j + 1) * S], pr[:, g % 2, j, :],
                                                net.ident[0:S, 0:S])
                        last.then_inc(pt_psum, 1)

                    def weigh(g):
                        pe.wait_ge(pt_ready, b * NG + g + 1)
                        if g >= 2:
                            pe.wait_ge(y_ready, b * NG + g - 1)
                        for j in range(G):
                            last = pe.matmul(summed[0:S, g % 2, j * (D + 1):(j + 1) * (D + 1)], pt[:, g % 2, j, :],
                                             v1[:, first_head(g) + 2 * j, :], start=True, stop=True)
                        last.then_inc(y_psum, 1)

                    pe.wait_ge(q_ready, b + 1)
                    pe.wait_ge(k_ready, b + 1)
                    scores(0)
                    scores(1)
                    turn(0)
                    pe.wait_ge(v_ready, b + 1)
                    scores(2)
                    turn(1)
                    weigh(0)
                    scores(3)
                    turn(2)
                    weigh(1)
                    turn(3)
                    weigh(2)
                    weigh(3)
                    pe.wait_ge(y_ready, b * NG + NG)
                    for m in range(MC):
                        last = pe.transpose(wide[:, m // PER, (m % PER) * S:(m % PER + 1) * S],
                                            y[:, 2 * m:2 * m + 2, :].rearrange("s h d -> s (h d)"), net.ident[0:S, 0:S])
                    last.then_inc(yt_psum, 1)
                    pe.wait_ge(yt_ready, b + 1)
                    for m in range(MC):
                        last = pe.matmul(summed[0:S, 0, 0:E], yt[:, m, :], wo[:, m, :], start=m == 0, stop=m == MC - 1)
                    last.then_inc(out_psum, 1)

            @block.scalar
            def _(act):
                norm_stats_scalar(act, net, var_ready, std_ready)
                with act.Fori(0, B) as b:
                    act.wait_ge(xt_psum, b + 1)
                    act.activation(xt[:], turned[:, 0, 0:KC * S].rearrange("p (k s) -> p k s", k=KC), ACT.Copy).then_inc(xt_ready, 1)
                    act.wait_ge(qk_psum, 2 * b + 1)
                    act.activation(qt[:].rearrange("p (a m) s -> p a (m s)", a=2), wide[:, 0:2, 0:PER * S], ACT.Copy).then_inc(q_ready, 1)
                    act.wait_ge(v_psum, b + 1)
                    act.activation(v1[:, :, 0:D], summed[0:S, :, :].rearrange("s a (h d) -> s (a h) d", d=D), ACT.Copy).then_inc(v_ready, 1)

                    def exps(g):
                        act.wait_ge(s_ready, b * NG + g + 1)
                        if g >= 2:
                            act.wait_ge(pt_psum, b * NG + g - 1)
                        act.activation(pr[:, g % 2], sc[:, g % 2], ACT.Exp, scale=D ** -0.5).then_inc(p_ready, 1)

                    def copy_pt(g):
                        act.wait_ge(pt_psum, b * NG + g + 1)
                        if g >= 2:
                            act.wait_ge(y_psum, b * NG + g - 1)
                        act.activation(pt[:, g % 2], turned[0:S, g % 2, 0:G * S].rearrange("s (j t) -> s j t", j=G), ACT.Copy).then_inc(pt_ready, 1)

                    exps(0)
                    exps(1)
                    copy_pt(0)
                    exps(2)
                    copy_pt(1)
                    exps(3)
                    copy_pt(2)
                    copy_pt(3)
                    act.wait_ge(yt_psum, b + 1)
                    act.activation(yt[:].rearrange("p (a m) s -> p a (m s)", a=2), wide[:, 0:2, 0:PER * S], ACT.Copy).then_inc(yt_ready, 1)

            @block.vector
            def _(dve):
                dve.memset(v1[:, :, D:D + 1], 1.0)
                norm_stats_vector(dve, net, var_ready, std_ready)
                dve.wait_ge(loaded, 80)
                with dve.Fori(0, B) as b:
                    normalise(dve, net, xn[:], b).then_inc(xn_ready, 1)
                    dve.wait_ge(qk_psum, 2 * b + 2)
                    dve.tensor_copy(kt[:].rearrange("p (a m) s -> p a (m s)", a=2), wide[:, 2:4, 0:PER * S]).then_inc(k_ready, 1)

                    def shift(g):
                        dve.wait_ge(s_psum, b * NG + g + 1)
                        if g >= 2:
                            dve.wait_ge(p_ready, b * NG + g - 1)
                        one = sc[:, g % 2]
                        dve.tensor_tensor(one, wide[0:S, g, 0:G * S].rearrange("s (j t) -> s j t", j=G),
                                          causal[:].unsqueeze(1).broadcast_to([S, G, S]), ALU.add)
                        dve.drain()
                        dve.tensor_reduce(mx[:, g * G:(g + 1) * G], one, X_AX, ALU.max)
                        dve.drain()
                        dve.tensor_tensor(one, one, mx[:, g * G:(g + 1) * G].unsqueeze(2).broadcast_to([S, G, S]),
                                          ALU.subtract).then_inc(s_ready, 1)

                    def divide(g):
                        dve.wait_ge(y_psum, b * NG + g + 1)
                        got = summed[0:S, g % 2, 0:G * (D + 1)].rearrange("s (j d) -> s j d", j=G)
                        dve.reciprocal(rs[:, g * G:(g + 1) * G].unsqueeze(2), got[:, :, D:D + 1])
                        dve.drain()
                        dve.tensor_tensor(y[:, first_head(g):first_head(g) + 2 * G - 1:2, :], got[:, :, 0:D],
                                          rs[:, g * G:(g + 1) * G].unsqueeze(2).broadcast_to([S, G, D]), ALU.mult).then_inc(y_ready, 1)

                    for g in range(NG):
                        shift(g)
                        if g >= 3:
                            divide(g - 3)
                    for g in range(1, NG):
                        divide(g)
                    dve.wait_ge(out_psum, b + 1)
                    dve.tensor_tensor(net.x[:, b, :], net.x[:, b, :], summed[0:S, 0, 0:E], ALU.add)
                    dve.drain()


@sublayer
def cross_attn(net, name, H, rope=False, biases=False, mask=None, gate=False):
    nc, dram = net.nc, net.dram
    D = E // H
    HP = P // D
    SCALE = D ** -0.5
    with ExitStack() as ctx:
        def sb(n, shape, dt=F32):
            return ctx.enter_context(nc.sbuf_tensor(name + "_" + n, shape, dt))

        w = {n: sb(n, [P, KC, E]) for n in ("wq", "wk", "wv", "wo")}
        pairs = [(w[n][:], dram[name + "_" + n]) for n in w]
        headmask = sb("headmask", [P, HP])
        pairs.append((headmask[:], dram[f"headmask{D}"]))
        if biases:
            bq, bk = sb("bq", [P, KC]), sb("bk", [P, KC])
            bv, bo = sb("bv", [P, E]), sb("bo", [P, E])
            pairs += [(bq[:], dram[name + "_bq"]), (bk[:], dram[name + "_bk"]),
                      (bv[:], dram[name + "_bv"].partition_broadcast(P)), (bo[:], dram[name + "_bo"].partition_broadcast(P))]
        elif name == "l3x":
            bo = sb("bo", [P, E])
            pairs.append((bo[:], dram[name + "_bo"].partition_broadcast(P)))
        else:
            bo = None
        if rope:
            swap = sb("swap", [P, P])
            cos, sin = sb("cos", [P, SKV]), sb("sin", [P, SKV])
            pairs += [(swap[:], dram["rope_swap"]), (cos[:], dram["rope_cos"]), (sin[:], dram["rope_sin"])]
            kraw, qraw = sb("kraw", [P, KC, SKV]), sb("qraw", [P, KC, S])
            ksin, qsin = sb("ksin", [P, KC, SKV]), sb("qsin", [P, KC, S])
        if gate:
            energy = sb("energy", [CH, B * NCH, 8])
            gates = sb("gates", [CH, B * NCH])
            gsum = sb("gsum", [CH, B * NCH])
            pairs.append((energy[:], dram["energy"]))
        n_loaded = 16 * len(pairs)
        if mask:
            words = sb("words", [S, 2, dram[mask[0]].shape[-1]], I32)
            bias = sb("bias", [S, SKV])
            sc = sb("sc", [S, 2, 2, SKV])
        ctxt = sb("ctxt", [P, 2, KC, SKV])
        xn = sb("xn", [S, E])
        xt = sb("xt", [P, KC, S])
        qt = sb("qt", [P, KC, S])
        qm = sb("qm", [P, KC, HP, S])
        kt = sb("kt", [P, KC, PADKV])
        v1 = sb("v1", [CH, NCH, H, D + 1])
        mx = sb("mx", [S, H])
        nmx = sb("nmx", [S, H])
        pr = sb("pr", [S, 2, 2, PADKV])
        pt = sb("pt", [CH, 2, NCH, S])
        rs = sb("rs", [S, H])
        y = sb("y", [S, H, D])
        yt = sb("yt", [P, KC, S])
        delta = sb("delta", [S, E])

        sem = {n: net.sem(name + "_" + n) for n in (
            "loaded", "ctx0", "ctx1", "mask_used", "var_ready", "std_ready", "cleared", "gate_sum", "gate_ready",
            "xn_ready", "xt_psum", "xt_ready", "k_psum", "v_psum", "q_psum", "kraw_ready", "qraw_ready", "kswap_psum", "qswap_psum",
            "k_ready", "v_ready", "q_ready", "s_psum", "m_ready", "p_ready", "pt_psum", "pt_ready", "y_psum", "y_ready",
            "yt_psum", "yt_ready", "out_psum")}
        wide, turned, summed = net.wide, net.turned, net.summed
        NP = H // 2
        ctx_loaded = (sem["ctx0"], sem["ctx1"])
        per_ctx = 32 if mask else 16

        with nc.Block() as block:
            @block.sync
            def _(sp):
                load_weights(sp, net, pairs, sem["loaded"])

                def load_ctx(b, slot):
                    sp.dma_start(ctxt[:, slot], dram["ctxt"][b]).then_inc(ctx_loaded[slot], 16)
                    if mask:
                        src = dram[mask[0]][b]
                        if mask[0] == "key_mask":
                            src = src.partition_broadcast(S)
                        sp.dma_start(words[:, slot], src).then_inc(ctx_loaded[slot], 16)

                load_ctx(0, 0)
                load_ctx(1, 1)
                with sp.Fori(1, B // 2) as i:
                    for slot in range(2):
                        sp.wait_ge(sem["v_psum"], 2 * i + slot - 1)
                        if mask:
                            sp.wait_ge(sem["mask_used"], 2 * i + slot - 1)
                        load_ctx(2 * i + slot, slot)

            @block.tensor
            def _(pe):
                pe.wait_ge(sem["loaded"], n_loaded)
                pe.wait_ge(sem["cleared"], 1)
                if gate:
                    pe.wait_ge(sem["gate_ready"], 1)
                with pe.Fori(0, B // 2) as i:
                    for slot in range(2):
                        b = 2 * i + slot
                        pe.wait_ge(sem["xn_ready"], b + 1)
                        for k in range(KC):
                            last = pe.transpose(turned[:, 0, k * S:(k + 1) * S], xn[:, k * P:(k + 1) * P], net.ident[0:S, 0:S])
                        last.then_inc(sem["xt_psum"], 1)
                        pe.wait_ge(ctx_loaded[slot], per_ctx * (i + 1))
                        for m in range(KC):
                            for k in range(KC):
                                last = pe.matmul(wide[:, m, 0:SKV], w["wk"][:, k, m * P:(m + 1) * P], ctxt[:, slot, k, :],
                                                 start=k == 0, stop=k == KC - 1)
                        last.then_inc(sem["k_psum"], 1)
                        for c in range(NCH):
                            n = CH if c < NCH - 1 else LAST
                            for k in range(KC):
                                last = pe.matmul(wide[0:n, 2 + c // 2, (c % 2) * E:(c % 2 + 1) * E],
                                                 ctxt[:, slot, k, c * CH:c * CH + n], w["wv"][:, k, :],
                                                 start=k == 0, stop=k == KC - 1)
                        last.then_inc(sem["v_psum"], 1)
                        pe.wait_ge(sem["xt_ready"], b + 1)
                        for m in range(KC):
                            for k in range(KC):
                                last = pe.matmul(turned[:, 1, m * S:(m + 1) * S], w["wq"][:, k, m * P:(m + 1) * P], xt[:, k, :],
                                                 start=k == 0, stop=k == KC - 1)
                        last.then_inc(sem["q_psum"], 1)
                        if rope:
                            pe.wait_ge(sem["kraw_ready"], b + 1)
                            for m in range(KC):
                                last = pe.matmul(wide[:, m, 0:SKV], swap[:], kraw[:, m, :], start=True, stop=True)
                            last.then_inc(sem["kswap_psum"], 1)
                            pe.wait_ge(sem["qraw_ready"], b + 1)
                            for m in range(KC):
                                last = pe.matmul(turned[:, 1, m * S:(m + 1) * S], swap[:], qraw[:, m, :], start=True, stop=True)
                            last.then_inc(sem["qswap_psum"], 1)

                        def scores(g):
                            if g >= 2:
                                if mask:
                                    pe.wait_ge(sem["m_ready"], b * NP + g - 1)
                                else:
                                    pe.wait_ge(sem["p_ready"], b * NP + g - 1)
                            for j in range(2):
                                h = 2 * g + j
                                last = pe.matmul(wide[0:S, 2 * (g % 2) + j, 0:SKV], qm[:, h // HP, h % HP, :],
                                                 kt[:, h // HP, 0:SKV], start=True, stop=True)
                            last.then_inc(sem["s_psum"], 1)

                        def turn(h):
                            if h % 2 == 0:
                                pe.wait_ge(sem["p_ready"], b * NP + h // 2 + 1)
                            if h >= 2:
                                pe.wait_ge(sem["pt_ready"], b * H + h - 1)
                            for c in range(NCH):
                                last = pe.transpose(turned[0:CH, h % 2, c * S:(c + 1) * S],
                                                    pr[:, (h // 2) % 2, h % 2, c * CH:(c + 1) * CH], net.ident[0:S, 0:S])
                            last.then_inc(sem["pt_psum"], 1)

                        def weigh(h):
                            pe.wait_ge(sem["pt_ready"], b * H + h + 1)
                            for c in range(NCH):
                                last = pe.matmul(summed[0:S, 0, h * (D + 1):(h + 1) * (D + 1)], pt[:, h % 2, c, :],
                                                 v1[:, c, h, :], start=c == 0, stop=c == NCH - 1)
                            last.then_inc(sem["y_psum"], 1)

                        pe.wait_ge(sem["q_ready"], b + 1)
                        pe.wait_ge(sem["k_ready"], b + 1)
                        pe.wait_ge(sem["v_ready"], b + 1)
                        scores(0)
                        for g in range(NP):
                            if g + 1 < NP:
                                scores(g + 1)
                            for h in (2 * g, 2 * g + 1):
                                turn(h)
                                if h >= 1:
                                    weigh(h - 1)
                        weigh(H - 1)
                        pe.wait_ge(sem["y_ready"], b + 1)
                        for k in range(KC):
                            last = pe.transpose(turned[:, 0, k * S:(k + 1) * S],
                                                y[:].rearrange("s h d -> s (h d)")[:, k * P:(k + 1) * P], net.ident[0:S, 0:S])
                        last.then_inc(sem["yt_psum"], 1)
                        pe.wait_ge(sem["yt_ready"], b + 1)
                        for k in range(KC):
                            last = pe.matmul(summed[0:S, 1, 0:E], yt[:, k, :], w["wo"][:, k, :], start=k == 0, stop=k == KC - 1)
                        last.then_inc(sem["out_psum"], 1)

            @block.scalar
            def _(act):
                norm_stats_scalar(act, net, sem["var_ready"], sem["std_ready"])
                if gate:
                    act.wait_ge(sem["gate_sum"], 1)
                    act.activation(gates[:], gsum[:], ACT.Sigmoid).then_inc(sem["gate_ready"], 1)
                act.wait_ge(sem["loaded"], n_loaded)
                with act.Fori(0, B // 2) as i:
                    for slot in range(2):
                        b = 2 * i + slot
                        act.wait_ge(sem["xt_psum"], b + 1)
                        act.activation(xt[:], turned[:, 0, 0:KC * S].rearrange("p (k s) -> p k s", k=KC), ACT.Copy).then_inc(sem["xt_ready"], 1)
                        act.wait_ge(sem["k_psum"], b + 1)
                        out_k = kraw if rope else kt
                        for m in range(KC):
                            if biases:
                                last = act.activation(out_k[:, m, 0:SKV], wide[:, m, 0:SKV], ACT.Identity, bias=bk[:, m:m + 1])
                            else:
                                last = act.activation(out_k[:, m, 0:SKV], wide[:, m, 0:SKV], ACT.Copy)
                        last.then_inc(sem["kraw_ready"] if rope else sem["k_ready"], 1)
                        for g in range(NP):
                            act.wait_ge(sem["m_ready"], b * NP + g + 1)
                            if g >= 2:
                                act.wait_ge(sem["pt_psum"], b * H + 2 * g - 2)
                            for j in range(2):
                                h = 2 * g + j
                                src = sc[:, g % 2, j, :] if mask else wide[0:S, 2 * (g % 2) + j, 0:SKV]
                                last = act.activation(pr[:, g % 2, j, 0:SKV], src, ACT.Exp, bias=nmx[:, h:h + 1], scale=SCALE)
                            last.then_inc(sem["p_ready"], 1)
                        act.wait_ge(sem["yt_psum"], b + 1)
                        act.activation(yt[:], turned[:, 0, 0:KC * S].rearrange("p (k s) -> p k s", k=KC), ACT.Copy).then_inc(sem["yt_ready"], 1)

            @block.vector
            def _(dve):
                dve.memset(v1[:], 0.0)
                dve.memset(kt[:, :, SKV:PADKV], 0.0)
                dve.memset(pr[:, :, :, SKV:PADKV], 0.0)
                dve.drain()
                dve.memset(v1[:, :, :, D:D + 1], 1.0).then_inc(sem["cleared"], 1)
                norm_stats_vector(dve, net, sem["var_ready"], sem["std_ready"])
                dve.wait_ge(sem["loaded"], n_loaded)
                if gate:
                    dve.tensor_reduce(gates[:], energy[:], X_AX, ALU.add, apply_absolute_value=True)
                    dve.drain()
                    dve.tensor_scalar(gsum[:], gates[:], 10.0 / 8, -10.0 * 0.1, ALU.mult, ALU.add).then_inc(sem["gate_sum"], 1)
                    dve.wait_ge(sem["gate_ready"], 1)
                with dve.Fori(0, B // 2) as i:
                    for slot in range(2):
                        b = 2 * i + slot
                        normalise(dve, net, xn[:], b).then_inc(sem["xn_ready"], 1)
                        if mask:
                            dve.wait_ge(ctx_loaded[slot], per_ctx * (i + 1))
                            dve.tensor_scalar(bias[:], words[:, slot, :].bitcast(mask[1])[:, 0:SKV], 0.0, NEG, ALU.is_equal, ALU.mult).then_inc(sem["mask_used"], 1)
                        dve.wait_ge(sem["v_psum"], b + 1)
                        for c in range(NCH):
                            n = CH if c < NCH - 1 else LAST
                            got = wide[0:n, 2 + c // 2, (c % 2) * E:(c % 2 + 1) * E].rearrange("s (h d) -> s h d", h=H)
                            if biases:
                                last = dve.tensor_tensor(v1[0:n, c, :, 0:D], got, bv[0:n, :].rearrange("s (h d) -> s h d", h=H), ALU.add)
                            else:
                                last = dve.tensor_copy(v1[0:n, c, :, 0:D], got)
                        if gate:
                            dve.drain()
                            for c in range(NCH):
                                n = CH if c < NCH - 1 else LAST
                                last = dve.tensor_scalar(v1[0:n, c, :, 0:D], v1[0:n, c, :, 0:D],
                                                         gates[0:n, bass.ds(b * NCH + c, 1)], None, ALU.mult)
                        last.then_inc(sem["v_ready"], 1)
                        out_q = qraw if rope else qt
                        dve.wait_ge(sem["q_psum"], b + 1)
                        for m in range(KC):
                            if biases:
                                last = dve.tensor_scalar(out_q[:, m, :], turned[:, 1, m * S:(m + 1) * S], bq[:, m:m + 1], None, ALU.add)
                            else:
                                last = dve.tensor_copy(out_q[:, m, :], turned[:, 1, m * S:(m + 1) * S])
                        if rope:
                            last.then_inc(sem["qraw_ready"], 1)
                            dve.wait_ge(sem["kraw_ready"], b + 1)
                            for m in range(KC):
                                dve.tensor_tensor(kt[:, m, 0:SKV], kraw[:, m, :], cos[:], ALU.mult)
                            dve.wait_ge(sem["kswap_psum"], b + 1)
                            for m in range(KC):
                                dve.tensor_tensor(ksin[:, m, :], wide[:, m, 0:SKV], sin[:], ALU.mult)
                            dve.drain()
                            dve.tensor_tensor(kt[:, :, 0:SKV], kt[:, :, 0:SKV], ksin[:], ALU.add).then_inc(sem["k_ready"], 1)
                            for m in range(KC):
                                dve.tensor_tensor(qt[:, m, :], qraw[:, m, :], cos[:, 0:S], ALU.mult)
                            dve.wait_ge(sem["qswap_psum"], b + 1)
                            for m in range(KC):
                                dve.tensor_tensor(qsin[:, m, :], turned[:, 1, m * S:(m + 1) * S], sin[:, 0:S], ALU.mult)
                            dve.drain()
                            dve.tensor_tensor(qt[:], qt[:], qsin[:], ALU.add)
                        dve.drain()
                        for m in range(KC):
                            last = dve.tensor_tensor(qm[:, m], qt[:, m, :].unsqueeze(1).broadcast_to([P, HP, S]),
                                                     headmask[:].unsqueeze(2).broadcast_to([P, HP, S]), ALU.mult)
                        last.then_inc(sem["q_ready"], 1)

                        def maxima(g):
                            dve.wait_ge(sem["s_psum"], b * NP + g + 1)
                            if mask and g >= 2:
                                dve.wait_ge(sem["p_ready"], b * NP + g - 1)
                            if mask:
                                dve.memset(mx[0:1, 2 * g:2 * g + 1], 0.0)
                                dve.drain()
                                for j in range(2):
                                    dve.tensor_tensor_reduce(sc[:, g % 2, j, :], wide[0:S, 2 * (g % 2) + j, 0:SKV], bias[:], 1.0, -3e38,
                                                             ALU.add, ALU.max, mx[:, 2 * g + j:2 * g + j + 1])
                            else:
                                dve.tensor_reduce(mx[:, 2 * g:2 * g + 2], wide[0:S, 2 * (g % 2):2 * (g % 2) + 2, 0:SKV], X_AX, ALU.max)
                            dve.drain()
                            dve.tensor_scalar(nmx[:, 2 * g:2 * g + 2], mx[:, 2 * g:2 * g + 2], -SCALE, None, ALU.mult).then_inc(sem["m_ready"], 1)

                        def copy_pt(h):
                            dve.wait_ge(sem["pt_psum"], b * H + h + 1)
                            if h >= 2:
                                dve.wait_ge(sem["y_psum"], b * H + h - 1)
                            dve.tensor_copy(pt[:, h % 2], turned[0:CH, h % 2, 0:NCH * S].rearrange("s (c t) -> s c t", c=NCH)).then_inc(sem["pt_ready"], 1)

                        maxima(0)
                        for g in range(NP):
                            if g + 1 < NP:
                                maxima(g + 1)
                            copy_pt(2 * g)
                            copy_pt(2 * g + 1)
                        dve.wait_ge(sem["y_psum"], b * H + H)
                        got = summed[0:S, 0, 0:H * (D + 1)].rearrange("s (h d) -> s h d", h=H)
                        dve.reciprocal(rs[:].unsqueeze(2), got[:, :, D:D + 1])
                        dve.drain()
                        dve.tensor_tensor(y[:], got[:, :, 0:D], rs[:].unsqueeze(2).broadcast_to([S, H, D]), ALU.mult).then_inc(sem["y_ready"], 1)
                        dve.wait_ge(sem["out_psum"], b + 1)
                        if bo is not None:
                            dve.tensor_tensor(delta[:], summed[0:S, 1, 0:E], bo[0:S, :], ALU.add)
                            dve.drain()
                            dve.tensor_tensor(net.x[:, b, :], net.x[:, b, :], delta[:], ALU.add)
                        else:
                            dve.tensor_tensor(net.x[:, b, :], net.x[:, b, :], summed[0:S, 1, 0:E], ALU.add)
                        dve.drain()


def top_two_vector(dve, net, t, gap_ready, exp_ready):
    for b in range(B):
        dve.max(t.top[:, b, :], t.logits[:, b, :])
    dve.drain()
    for b in range(B):
        dve.max_index(t.which[:, b, :], t.top[:, b, :], t.logits[:, b, :])
    dve.tensor_tensor(t.gap[:], t.top[:, :, 1:2], t.top[:, :, 0:1], ALU.subtract).then_inc(gap_ready, 1)
    dve.drain()
    dve.tensor_copy(t.whichf[:], t.which[:, :, 0:2])
    dve.drain()
    for k in range(2):
        dve.tensor_tensor(t.hot[k][:], t.whichf[:, :, k:k + 1].broadcast_to([S, B, NE]), t.iota[:], ALU.is_equal)
    dve.wait_ge(exp_ready, 1)
    dve.tensor_scalar(t.den[:], t.exp[:], 1.0, None, ALU.add)
    dve.drain()
    dve.reciprocal(t.prob[0][:], t.den[:])
    dve.drain()
    dve.tensor_tensor(t.prob[1][:], t.exp[:], t.prob[0][:], ALU.mult)
    dve.drain()


class TopTwo:

    def __init__(self, sb):
        self.logits = sb("logits", [S, B, NE])
        self.top = sb("top", [S, B, 8])
        self.which = sb("which", [S, B, 8], U32)
        self.whichf = sb("whichf", [S, B, 2])
        self.gap = sb("gap", [S, B, 1])
        self.exp = sb("exp", [S, B, 1])
        self.den = sb("den", [S, B, 1])
        self.prob = [sb(f"prob{k}", [S, B, 1]) for k in range(2)]
        self.hot = [sb(f"hot{k}", [S, B, NE]) for k in range(2)]
        self.iota = sb("iota", [S, B, NE])


@sublayer
def moe(net, name, F, biases=False):
    nc, dram = net.nc, net.dram
    FC = F // P
    NEX = NE + 1
    SLOTS = 3
    ROUNDS = NEX // SLOTS
    HALF = B * S // 2
    UNITS = 2 * FC
    LAG = 4 if SLOTS * UNITS % 4 == 0 else 2
    with ExitStack() as ctx:
        def sb(n, shape, dt=F32):
            return ctx.enter_context(nc.sbuf_tensor(name + "_" + n, shape, dt))

        w1 = sb("w1", [P, SLOTS, KC, F])
        w2 = sb("w2", [P, SLOTS, FC, E])
        wr = sb("wr", [P, KC, NE])
        t = TopTwo(sb)
        pairs = [(wr[:], dram[name + "_wr"]), (t.iota[:], dram["iota8"])]
        if biases:
            b1 = sb("b1", [P, SLOTS, FC])
            b2 = sb("b2", [NEX, E])
            br = sb("br", [S, NE])
            pairs += [(b2[:], dram[name + "_b2"]), (br[:], dram[name + "_br"].partition_broadcast(S))]
            combine_t = sb("combine_t", [NEX, B, S])
        else:
            relu = sb("relu", [P, HALF])
        n_loaded = 16 * len(pairs)
        per_expert = 48 if biases else 32
        xn = sb("xn", [S, 2, E])
        xt = sb("xt", [P, KC, B * S])
        combine = sb("combine", [S, NEX, B])
        part = sb("part", [S, B, NE])
        weight = sb("weight", [S, B])
        credit = sb("credit", [1, 1])
        hidden = sb("hidden", [P, FC, B * S])
        sem = {n: net.sem(name + "_" + n) for n in (
            "loaded", "w0", "w1", "w2", "var_ready", "std_ready", "xn_ready", "xt_psum", "xt_ready", "l_psum",
            "gap_ready", "exp_ready", "combine_ready", "ct_psum", "ct_ready", "h_psum", "h_ready", "y_psum", "y_added")}
        wide, turned, summed = net.wide, net.turned, net.summed
        w_loaded = [sem[f"w{i}"] for i in range(SLOTS)]

        with nc.Block() as block:
            @block.sync
            def _(sp):
                load_weights(sp, net, pairs, sem["loaded"])

                def load_expert(e, slot):
                    sp.dma_start(w1[:, slot], dram[name + "_w1"][e]).then_inc(w_loaded[slot], 16)
                    sp.dma_start(w2[:, slot], dram[name + "_w2"][e]).then_inc(w_loaded[slot], 16)
                    if biases:
                        sp.dma_start(b1[:, slot], dram[name + "_b1"][e]).then_inc(w_loaded[slot], 16)

                for slot in range(SLOTS):
                    load_expert(slot, slot)
                with sp.Fori(1, ROUNDS) as r:
                    for slot in range(SLOTS):
                        sp.wait_ge(sem["y_psum"], (SLOTS * r + slot - 2) * B)
                        load_expert(SLOTS * r + slot, slot)

            @block.tensor
            def _(pe):
                pe.wait_ge(sem["loaded"], n_loaded)
                for b in range(B):
                    pe.wait_ge(sem["xn_ready"], b + 1)
                    if b >= 2:
                        pe.wait_ge(sem["xt_ready"], b - 1)
                    for k in range(KC):
                        last = pe.transpose(turned[:, b % 2, k * S:(k + 1) * S], xn[:, b % 2, k * P:(k + 1) * P], net.ident[0:S, 0:S])
                    last.then_inc(sem["xt_psum"], 1)
                for b in range(B):
                    pe.wait_ge(sem["xt_ready"], b + 1)
                    for k in range(KC):
                        last = pe.matmul(summed[0:S, 0, b * NE:(b + 1) * NE], xt[:, k, b * S:(b + 1) * S], wr[:, k, :],
                                         start=k == 0, stop=k == KC - 1)
                last.then_inc(sem["l_psum"], 1)
                if biases:
                    pe.wait_ge(sem["combine_ready"], 1)
                    for b in range(B):
                        last = pe.transpose(turned[0:NEX, b // 4, (b % 4) * S:(b % 4 + 1) * S], combine[:, :, b], net.ident[0:S, 0:S])
                    last.then_inc(sem["ct_psum"], 1)
                with pe.Fori(0, ROUNDS) as r:
                    for slot in range(SLOTS):
                        e = SLOTS * r + slot
                        pe.wait_ge(w_loaded[slot], per_expert * (r + 1))
                        for f in range(FC):
                            for half in range(2):
                                u = 2 * f + half
                                pe.wait_ge(sem["h_ready"], e * UNITS + u + 1)
                                for k in range(KC):
                                    last = pe.matmul(wide[:, (slot * UNITS + u) % 4, 0:HALF], w1[:, slot, k, f * P:(f + 1) * P],
                                                     xt[:, k, half * HALF:(half + 1) * HALF], start=k == 0, stop=k == KC - 1)
                                last.then_inc(sem["h_psum"], 1)
                        pe.wait_ge(sem["h_ready"], LAG + (e + 1) * UNITS)
                        for b in range(B):
                            pe.wait_ge(sem["y_added"], e * B + b + 1)
                            for f in range(FC):
                                last = pe.matmul(summed[0:S, b % 2, 0:E], hidden[:, f, b * S:(b + 1) * S], w2[:, slot, f, :],
                                                 start=f == 0, stop=f == FC - 1)
                            last.then_inc(sem["y_psum"], 1)
                if biases:
                    pe.wait_ge(sem["ct_ready"], 1)
                    for b in range(B):
                        pe.wait_ge(sem["y_added"], NEX * B + b + 1)
                        pe.matmul(summed[0:S, b % 2, 0:E], combine_t[:, b, :], b2[:], start=True, stop=True).then_inc(sem["y_psum"], 1)

            @block.scalar
            def _(act):
                norm_stats_scalar(act, net, sem["var_ready"], sem["std_ready"])
                for b in range(B):
                    act.wait_ge(sem["xt_psum"], b + 1)
                    act.activation(xt[:, :, b * S:(b + 1) * S], turned[:, b % 2, 0:KC * S].rearrange("p (k s) -> p k s", k=KC),
                                   ACT.Copy).then_inc(sem["xt_ready"], 1)
                act.wait_ge(sem["gap_ready"], 1)
                act.activation(t.exp[:], t.gap[:], ACT.Exp).then_inc(sem["exp_ready"], 1)
                act.drain()
                if biases:
                    act.wait_ge(sem["ct_psum"], 1)
                    act.activation(combine_t[:].rearrange("e (a b) s -> e a (b s)", a=2), turned[0:NEX, :, 0:4 * S], ACT.Copy).then_inc(sem["ct_ready"], 1)
                act.activation(credit[:], t.exp[0:1, 0, :], ACT.Copy).then_inc(sem["h_ready"], LAG)
                with act.Fori(0, ROUNDS) as r:
                    for slot in range(SLOTS):
                        e = SLOTS * r + slot
                        if biases:
                            act.wait_ge(w_loaded[slot], per_expert * (r + 1))
                        for f in range(FC):
                            for half in range(2):
                                u = 2 * f + half
                                act.wait_ge(sem["h_psum"], e * UNITS + u + 1)
                                src = wide[:, (slot * UNITS + u) % 4, 0:HALF]
                                dst = hidden[:, f, half * HALF:(half + 1) * HALF]
                                if biases:
                                    act.activation(dst, src, ACT.Gelu, bias=b1[:, slot, f:f + 1]).then_inc(sem["h_ready"], 1)
                                else:
                                    act.activation(relu[:], src, ACT.Relu)
                                    act.drain()
                                    act.activation(dst, relu[:], ACT.Square).then_inc(sem["h_ready"], 1)
                                    act.drain()

            @block.vector
            def _(dve):
                norm_stats_vector(dve, net, sem["var_ready"], sem["std_ready"])
                for b in range(B):
                    if b >= 2:
                        dve.wait_ge(sem["xt_psum"], b - 1)
                    normalise(dve, net, xn[:, b % 2, :], b).then_inc(sem["xn_ready"], 1)
                dve.wait_ge(sem["loaded"], n_loaded)
                dve.wait_ge(sem["l_psum"], 1)
                logits = summed[0:S, 0, 0:B * NE].rearrange("s (b e) -> s b e", b=B)
                if biases:
                    dve.tensor_tensor(t.logits[:], logits, br[:].unsqueeze(1).broadcast_to([S, B, NE]), ALU.add)
                else:
                    dve.tensor_copy(t.logits[:], logits)
                dve.drain()
                top_two_vector(dve, net, t, sem["gap_ready"], sem["exp_ready"])
                if not biases:
                    for k in range(2):
                        dve.tensor_scalar(t.prob[k][:], t.prob[k][:], 1.0, None, ALU.is_ge)
                    dve.drain()
                dve.tensor_tensor(part[:], t.hot[0][:], t.prob[0][:].broadcast_to([S, B, NE]), ALU.mult)
                dve.tensor_tensor(t.hot[1][:], t.hot[1][:], t.prob[1][:].broadcast_to([S, B, NE]), ALU.mult)
                dve.memset(combine[:, NE:NEX, :], 1.0)
                dve.drain()
                dve.tensor_tensor(combine[:, 0:NE, :].rearrange("s e b -> s b e"), part[:], t.hot[1][:], ALU.add).then_inc(sem["combine_ready"], 1)
                dve.drain()
                dve.memset(part[0:1, 0, 0:1], 0.0).then_inc(sem["y_added"], 2)
                dve.drain()

                def add(b, e, scale):
                    dve.wait_ge(sem["y_psum"], e * B + b + 1)
                    dve.scalar_tensor_tensor(out=net.x[:, b, :], in0=summed[0:S, b % 2, 0:E], scalar=scale,
                                             in1=net.x[:, b, :], op0=ALU.mult, op1=ALU.add).then_inc(sem["y_added"], 1)

                with dve.Fori(0, NEX) as e:
                    dve.tensor_copy(weight[:], combine[:, e, :])
                    dve.drain()
                    for b in range(B):
                        add(b, e, weight[:, b:b + 1])
                    dve.drain()
                if biases:
                    for b in range(B):
                        add(b, NEX, 1.0)
                    dve.drain()


@sublayer
def l1_attn(net):
    nc, dram = net.nc, net.dram
    H, D, G = 16, 16, 4
    HP, NG = P // D, H // G
    with ExitStack() as ctx:
        def sb(n, shape, dt=F32):
            return ctx.enter_context(nc.sbuf_tensor("l1a_" + n, shape, dt))

        wqk, wv, wo = sb("wqk", [P, KC, 2 * E]), sb("wv", [P, KC, E]), sb("wo", [P, KC, E])
        bqk, bv, bo = sb("bqk", [S, 2 * E]), sb("bv", [S, E]), sb("bo", [S, E])
        headmask = sb("headmask", [P, HP])
        pairs = [(wqk[:], dram["l1a_wqk"]), (wv[:], dram["l1a_wv"]), (wo[:], dram["l1a_wo"]), (headmask[:], dram["headmask16"]),
                 (bqk[:], dram["l1a_bqk"].partition_broadcast(S)), (bv[:], dram["l1a_bv"].partition_broadcast(S)),
                 (bo[:], dram["l1a_bo"].partition_broadcast(S))]
        n_loaded = 16 * len(pairs)
        xn = sb("xn", [S, E])
        xt = sb("xt", [P, KC, S])
        qk = sb("qk", [S, 2 * H, D])
        sq = sb("sq", [S, 2 * H, D])
        norm = sb("norm", [S, 2 * H])
        qt, kt = sb("qt", [P, KC, S]), sb("kt", [P, KC, S])
        km = sb("km", [P, KC, HP, S])
        v1 = sb("v1", [S, H, D + 1])
        num, den, wt = sb("num", [S, H, S]), sb("den", [S, H, S]), sb("wt", [S, H, S])
        rs = sb("rs", [S, H])
        y = sb("y", [S, H, D])
        yt = sb("yt", [P, KC, S])
        delta = sb("delta", [S, E])
        sem = {n: net.sem("l1a_" + n) for n in (
            "loaded", "var_ready", "std_ready", "xn_ready", "xt_psum", "xt_ready", "qkv_psum", "sq_ready", "root_ready", "qk_ready",
            "qkt_psum", "heads_ready", "cos_psum", "num_ready", "wt_ready", "y_psum", "y_ready", "yt_psum", "yt_ready", "out_psum")}
        wide, turned, summed = net.wide, net.turned, net.summed

        with nc.Block() as block:
            @block.sync
            def _(sp):
                load_weights(sp, net, pairs, sem["loaded"])

            @block.tensor
            def _(pe):
                pe.wait_ge(sem["loaded"], n_loaded)
                with pe.Fori(0, B) as b:
                    pe.wait_ge(sem["xn_ready"], b + 1)
                    for k in range(KC):
                        last = pe.transpose(turned[:, 0, k * S:(k + 1) * S], xn[:, k * P:(k + 1) * P], net.ident[0:S, 0:S])
                    last.then_inc(sem["xt_psum"], 1)
                    pe.wait_ge(sem["xt_ready"], b + 1)
                    for w, out in ((wqk, wide[0:S, 0, :]), (wv, wide[0:S, 1, 0:E])):
                        for k in range(KC):
                            last = pe.matmul(out, xt[:, k, :], w[:, k, :], start=k == 0, stop=k == KC - 1)
                    last.then_inc(sem["qkv_psum"], 1)
                    pe.wait_ge(sem["qk_ready"], b + 1)
                    for c in range(2 * KC):
                        last = pe.transpose(turned[:, 0, c * S:(c + 1) * S],
                                            qk[:].rearrange("s h d -> s (h d)")[:, c * P:(c + 1) * P], net.ident[0:S, 0:S])
                    last.then_inc(sem["qkt_psum"], 1)
                    pe.wait_ge(sem["heads_ready"], b + 1)
                    for g in range(NG):
                        for j in range(G):
                            h = g * G + j
                            last = pe.matmul(wide[0:S, g, j * S:(j + 1) * S], km[:, h // HP, h % HP, :], qt[:, h // HP, :],
                                             start=True, stop=True)
                        last.then_inc(sem["cos_psum"], 1)
                    for g in range(NG):
                        pe.wait_ge(sem["wt_ready"], b * NG + g + 1)
                        for h in range(g * G, g * G + G):
                            last = pe.matmul(summed[0:S, 0, h * (D + 1):(h + 1) * (D + 1)], wt[:, h, :], v1[:, h, :],
                                             start=True, stop=True)
                    last.then_inc(sem["y_psum"], 1)
                    pe.wait_ge(sem["y_ready"], b + 1)
                    for k in range(KC):
                        last = pe.transpose(turned[:, 0, k * S:(k + 1) * S],
                                            y[:].rearrange("s h d -> s (h d)")[:, k * P:(k + 1) * P], net.ident[0:S, 0:S])
                    last.then_inc(sem["yt_psum"], 1)
                    pe.wait_ge(sem["yt_ready"], b + 1)
                    for k in range(KC):
                        last = pe.matmul(summed[0:S, 1, 0:E], yt[:, k, :], wo[:, k, :], start=k == 0, stop=k == KC - 1)
                    last.then_inc(sem["out_psum"], 1)

            @block.scalar
            def _(act):
                norm_stats_scalar(act, net, sem["var_ready"], sem["std_ready"])
                with act.Fori(0, B) as b:
                    act.wait_ge(sem["xt_psum"], b + 1)
                    act.activation(xt[:], turned[:, 0, 0:KC * S].rearrange("p (k s) -> p k s", k=KC), ACT.Copy).then_inc(sem["xt_ready"], 1)
                    act.wait_ge(sem["sq_ready"], b + 1)
                    act.activation(norm[:], norm[:], ACT.Sqrt).then_inc(sem["root_ready"], 1)
                    for g in range(NG):
                        act.wait_ge(sem["cos_psum"], b * NG + g + 1)
                        act.activation(num[:, g * G:(g + 1) * G, :], wide[0:S, g, 0:G * S].rearrange("s (j t) -> s j t", j=G),
                                       ACT.Square, bias=1.0).then_inc(sem["num_ready"], 1)
                    act.wait_ge(sem["yt_psum"], b + 1)
                    act.activation(yt[:], turned[:, 0, 0:KC * S].rearrange("p (k s) -> p k s", k=KC), ACT.Copy).then_inc(sem["yt_ready"], 1)

            @block.vector
            def _(dve):
                dve.memset(v1[:, :, D:D + 1], 1.0)
                norm_stats_vector(dve, net, sem["var_ready"], sem["std_ready"])
                dve.wait_ge(sem["loaded"], n_loaded)
                with dve.Fori(0, B) as b:
                    normalise(dve, net, xn[:], b).then_inc(sem["xn_ready"], 1)
                    dve.wait_ge(sem["qkv_psum"], b + 1)
                    dve.tensor_tensor(qk[:].rearrange("s h d -> s (h d)"), wide[0:S, 0, :], bqk[:], ALU.add)
                    dve.tensor_tensor(v1[:, :, 0:D], wide[0:S, 1, 0:E].rearrange("s (h d) -> s h d", h=H),
                                      bv[:].rearrange("s (h d) -> s h d", h=H), ALU.add)
                    dve.drain()
                    dve.tensor_tensor(sq[:], qk[:], qk[:], ALU.mult)
                    dve.drain()
                    dve.tensor_reduce(norm[:], sq[:], X_AX, ALU.add).then_inc(sem["sq_ready"], 1)
                    dve.wait_ge(sem["root_ready"], b + 1)
                    dve.tensor_scalar(norm[:], norm[:], 1e-8, None, ALU.add)
                    dve.drain()
                    dve.reciprocal(norm[:], norm[:])
                    dve.drain()
                    dve.tensor_tensor(qk[:], qk[:], norm[:].unsqueeze(2).broadcast_to([S, 2 * H, D]), ALU.mult).then_inc(sem["qk_ready"], 1)
                    dve.wait_ge(sem["qkt_psum"], b + 1)
                    dve.tensor_copy(qt[:], turned[:, 0, 0:KC * S].rearrange("p (k s) -> p k s", k=KC))
                    dve.tensor_copy(kt[:], turned[:, 0, KC * S:2 * KC * S].rearrange("p (k s) -> p k s", k=KC))
                    dve.drain()
                    for m in range(KC):
                        last = dve.tensor_tensor(km[:, m], kt[:, m, :].unsqueeze(1).broadcast_to([P, HP, S]),
                                                 headmask[:].unsqueeze(2).broadcast_to([P, HP, S]), ALU.mult)
                    last.then_inc(sem["heads_ready"], 1)
                    for g in range(NG):
                        one = den[:, g * G:(g + 1) * G, :]
                        dve.wait_ge(sem["num_ready"], b * NG + g + 1)
                        dve.tensor_scalar(one, wide[0:S, g, 0:G * S].rearrange("s (j t) -> s j t", j=G), -1.0, 1.1, ALU.mult, ALU.add)
                        dve.drain()
                        dve.reciprocal(one, one)
                        dve.drain()
                        dve.tensor_tensor(wt[:, g * G:(g + 1) * G, :], one, num[:, g * G:(g + 1) * G, :], ALU.mult).then_inc(sem["wt_ready"], 1)
                    dve.wait_ge(sem["y_psum"], b + 1)
                    got = summed[0:S, 0, 0:H * (D + 1)].rearrange("s (h d) -> s h d", h=H)
                    dve.tensor_scalar(rs[:].unsqueeze(2), got[:, :, D:D + 1], 1e-6, None, ALU.add)
                    dve.drain()
                    dve.reciprocal(rs[:], rs[:])
                    dve.drain()
                    dve.tensor_tensor(y[:], got[:, :, 0:D], rs[:].unsqueeze(2).broadcast_to([S, H, D]), ALU.mult).then_inc(sem["y_ready"], 1)
                    dve.wait_ge(sem["out_psum"], b + 1)
                    dve.tensor_tensor(delta[:], summed[0:S, 1, 0:E], bo[:], ALU.add)
                    dve.drain()
                    dve.tensor_tensor(net.x[:, b, :], net.x[:, b, :], delta[:], ALU.add)
                    dve.drain()


@sublayer
def l2_attn(net):
    nc, dram = net.nc, net.dram
    N = 2
    with ExitStack() as ctx:
        def sb(n, shape, dt=F32):
            return ctx.enter_context(nc.sbuf_tensor("l2a_" + n, shape, dt))

        par = {n: sb(n, [P, KC, N]) for n in ("delta", "alpha", "beta", "gamma")}
        omega = sb("omega", [P, KC])
        pairs = [(par[n][:], dram["l2a_" + n]) for n in par] + [(omega[:], dram["l2a_omega"])]
        n_loaded = 16 * len(pairs)
        p_, a_ = sb("p", [P, KC, N]), sb("a", [P, KC, N])
        q_, c_ = sb("q", [P, KC, N]), sb("c", [P, KC, N])
        keep = sb("keep", [P, B, S])
        decay = sb("decay", [P, KC * N, B * S])
        fed = sb("fed", [P, KC * N, B * S])
        avg = sb("avg", [P, KC * N, B * S])
        xn = sb("xn", [S, 2, E])
        xt = sb("xt", [P, KC, B * S])
        z = sb("z", [P, KC, B * S])
        sem = {n: net.sem("l2a_" + n) for n in (
            "loaded", "var_ready", "std_ready", "xn_ready", "xt_psum", "xt_ready", "gates_ready", "z_ready", "silu_ready", "zt_psum", "zt_added")}
        turned, summed = net.turned, net.summed

        with nc.Block() as block:
            @block.sync
            def _(sp):
                load_weights(sp, net, pairs, sem["loaded"])

            @block.tensor
            def _(pe):
                for b in range(B):
                    pe.wait_ge(sem["xn_ready"], b + 1)
                    if b >= 2:
                        pe.wait_ge(sem["xt_ready"], b - 1)
                    for k in range(KC):
                        last = pe.transpose(turned[:, b % 2, k * S:(k + 1) * S], xn[:, b % 2, k * P:(k + 1) * P], net.ident[0:S, 0:S])
                    last.then_inc(sem["xt_psum"], 1)
                pe.wait_ge(sem["silu_ready"], KC)
                for b in range(B):
                    if b >= 2:
                        pe.wait_ge(sem["zt_added"], b - 1)
                    for k in range(KC):
                        last = pe.transpose(summed[0:S, b % 2, k * P:(k + 1) * P], z[:, k, b * S:(b + 1) * S], net.ident[:])
                    last.then_inc(sem["zt_psum"], 1)

            @block.scalar
            def _(act):
                norm_stats_scalar(act, net, sem["var_ready"], sem["std_ready"])
                for b in range(B):
                    act.wait_ge(sem["xt_psum"], b + 1)
                    act.activation(xt[:, :, b * S:(b + 1) * S], turned[:, b % 2, 0:KC * S].rearrange("p (k s) -> p k s", k=KC),
                                   ACT.Copy).then_inc(sem["xt_ready"], 1)
                act.wait_ge(sem["loaded"], n_loaded)
                act.activation(p_[:], par["delta"][:], ACT.Sigmoid)
                act.activation(a_[:], par["alpha"][:], ACT.Sigmoid).then_inc(sem["gates_ready"], 1)
                for k in range(KC):
                    act.wait_ge(sem["z_ready"], k + 1)
                    act.activation(z[:, k, :], avg[:, 2 * k, :], ACT.Silu).then_inc(sem["silu_ready"], 1)

            @block.vector
            def _(dve):
                norm_stats_vector(dve, net, sem["var_ready"], sem["std_ready"])
                for b in range(B):
                    if b >= 2:
                        dve.wait_ge(sem["xt_psum"], b - 1)
                    normalise(dve, net, xn[:, b % 2, :], b).then_inc(sem["xn_ready"], 1)
                dve.memset(keep[:], 1.0)
                dve.drain()
                dve.memset(keep[:, :, 0:1], 0.0)
                dve.wait_ge(sem["gates_ready"], 1)
                dve.tensor_tensor(q_[:], p_[:], a_[:], ALU.mult)
                dve.tensor_tensor(c_[:], p_[:], par["beta"][:], ALU.mult)
                dve.drain()
                dve.tensor_scalar(q_[:], q_[:], -1.0, 1.0, ALU.mult, ALU.add)
                dve.tensor_tensor(c_[:], c_[:], par["gamma"][:], ALU.mult)
                dve.drain()
                dve.tensor_scalar(c_[:], c_[:], float(np.sqrt(1.0 / N)), None, ALU.mult)
                dve.drain()
                for k in range(KC):
                    for n in range(N):
                        dve.tensor_scalar(decay[:, k * N + n, :], keep[:].rearrange("p b s -> p (b s)"), q_[:, k, n:n + 1], None, ALU.mult)
                dve.wait_ge(sem["xt_ready"], B)
                for k in range(KC):
                    for n in range(N):
                        dve.tensor_scalar(fed[:, k * N + n, :], xt[:, k, :], c_[:, k, n:n + 1], None, ALU.mult)
                dve.drain()
                for k in range(KC):
                    for n in range(N):
                        j = k * N + n
                        dve.tensor_tensor_scan(avg[:, j, :], decay[:, j, :], fed[:, j, :], 0.0, ALU.mult, ALU.add)
                    dve.drain()
                    dve.tensor_tensor(avg[:, k * N, :], avg[:, k * N, :], avg[:, k * N + 1, :], ALU.add)
                    dve.drain()
                    dve.scalar_tensor_tensor(out=avg[:, k * N, :], in0=xt[:, k, :], scalar=omega[:, k:k + 1],
                                             in1=avg[:, k * N, :], op0=ALU.mult, op1=ALU.add).then_inc(sem["z_ready"], 1)
                for b in range(B):
                    dve.wait_ge(sem["zt_psum"], b + 1)
                    dve.tensor_tensor(net.x[:, b, :], net.x[:, b, :], summed[0:S, b % 2, 0:E], ALU.add).then_inc(sem["zt_added"], 1)
                dve.drain()


@sublayer
def l2_ffn(net):
    nc, dram = net.nc, net.dram
    F = 1024
    FC = F // P
    TOP = 2
    ROWS = B * S * TOP
    RT = ROWS // NE // S
    CR = RT * S
    SLOTS = 2
    with ExitStack() as ctx:
        def sb(n, shape, dt=F32):
            return ctx.enter_context(nc.sbuf_tensor("l2f_" + n, shape, dt))

        w1 = sb("w1", [P, SLOTS, KC, F])
        w2 = sb("w2", [P, SLOTS, FC, E])
        wr = sb("wr", [P, KC, NE])
        before, ones = sb("before", [S, S]), sb("ones", [S, S])
        t = TopTwo(sb)
        pairs = [(wr[:], dram["l2f_wr"]), (t.iota[:], dram["iota8"]), (before[:], dram["before"])]
        n_loaded = 16 * len(pairs)
        xn = sb("xn", [S, B, E])
        xt = sb("xt", [P, KC, 2, S])
        both = sb("both", [S, B, NE])
        total = sb("total", [S, B, NE])
        start = sb("start", [S, B + 1, NE])
        base = sb("base", [S, NE])
        rank = sb("rank", [S, B, NE])
        mine = sb("mine", [S, B, NE])
        place = sb("place", [S, TOP, B])
        placei = sb("placei", [S, TOP * B], U32)
        rows = sb("rows", [S, SLOTS, RT, E])
        rt = sb("rt", [P, KC, CR])
        hidden = sb("hidden", [P, FC, CR])
        out = sb("out", [S, SLOTS, RT, E])
        back = sb("back", [S, TOP * B, E])
        sorted_x = nc.dram_tensor("sorted_x", (ROWS, E), F32).ap()
        sorted_y = nc.dram_tensor("sorted_y", (ROWS, E), F32).ap()
        sem = {n: net.sem("l2f_" + n) for n in (
            "loaded", "w0", "w1", "r0", "r1", "var_ready", "std_ready", "xn_ready", "xt_psum", "xt_ready", "l_psum", "gap_ready",
            "exp_ready", "both_ready", "count_psum", "place_ready", "scattered", "rt_psum", "rt_ready", "h_psum", "h_ready",
            "y_psum", "y_ready", "stored0", "stored1", "gathered")}
        wide, turned, summed = net.wide, net.turned, net.summed
        w_loaded, r_loaded = (sem["w0"], sem["w1"]), (sem["r0"], sem["r1"])
        stored = (sem["stored0"], sem["stored1"])

        with nc.Block() as block:
            @block.sync
            def _(sp):
                load_weights(sp, net, pairs, sem["loaded"])

                def load_expert(e, slot):
                    sp.dma_start(w1[:, slot], dram["l2f_w1"][e]).then_inc(w_loaded[slot], 16)
                    sp.dma_start(w2[:, slot], dram["l2f_w2"][e]).then_inc(w_loaded[slot], 16)

                def load_rows(e, slot):
                    sp.dma_start(rows[:, slot], sorted_x.rearrange("(e r s) d -> e s r d", r=RT, s=S)[e]).then_inc(r_loaded[slot], 16)

                for slot in range(SLOTS):
                    load_expert(slot, slot)
                sp.wait_ge(sem["scattered"], 16 * TOP * B)
                for slot in range(SLOTS):
                    load_rows(slot, slot)
                with sp.Fori(1, NE // SLOTS) as r:
                    for slot in range(SLOTS):
                        sp.wait_ge(sem["y_psum"], SLOTS * r + slot - 1)
                        load_expert(SLOTS * r + slot, slot)
                        load_rows(SLOTS * r + slot, slot)

            @block.gpsimd
            def _(pool):
                pool.wait_ge(sem["place_ready"], 1)
                for b in range(B):
                    for k in range(TOP):
                        pool.indirect_dma_start(out=sorted_x, out_offset=bass.IndirectOffsetOnAxis(ap=placei[:, k * B + b:k * B + b + 1], axis=0),
                                                in_=xn[:, b, :], in_offset=None).then_inc(sem["scattered"], 16)
                for slot in range(SLOTS):
                    pool.wait_ge(stored[slot], 16 * NE // SLOTS)
                for b in range(B):
                    for k in range(TOP):
                        pool.indirect_dma_start(out=back[:, k * B + b, :], out_offset=None, in_=sorted_y,
                                                in_offset=bass.IndirectOffsetOnAxis(ap=placei[:, k * B + b:k * B + b + 1], axis=0)
                                                ).then_inc(sem["gathered"], 16)

            @block.tensor
            def _(pe):
                pe.wait_ge(sem["loaded"], n_loaded)
                for b in range(B):
                    pe.wait_ge(sem["xn_ready"], b + 1)
                    if b >= 2:
                        pe.wait_ge(sem["xt_ready"], b - 1)
                    for k in range(KC):
                        last = pe.transpose(turned[:, b % 2, k * S:(k + 1) * S], xn[:, b, k * P:(k + 1) * P], net.ident[0:S, 0:S])
                    last.then_inc(sem["xt_psum"], 1)
                    pe.wait_ge(sem["xt_ready"], b + 1)
                    for k in range(KC):
                        last = pe.matmul(summed[0:S, 0, b * NE:(b + 1) * NE], xt[:, k, b % 2, :], wr[:, k, :], start=k == 0, stop=k == KC - 1)
                last.then_inc(sem["l_psum"], 1)
                pe.wait_ge(sem["both_ready"], 1)
                chosen = both[:].rearrange("s b e -> s (b e)")
                pe.matmul(summed[0:S, 1, 0:B * NE], before[:], chosen, start=True, stop=True)
                pe.matmul(summed[0:S, 1, B * NE:2 * B * NE], ones[:], chosen, start=True, stop=True).then_inc(sem["count_psum"], 1)
                with pe.Fori(0, NE // SLOTS) as r:
                    for slot in range(SLOTS):
                        e = SLOTS * r + slot
                        pe.wait_ge(r_loaded[slot], 16 * (r + 1))
                        for c in range(RT):
                            for k in range(KC):
                                last = pe.transpose(turned[:, c, k * S:(k + 1) * S], rows[:, slot, c, k * P:(k + 1) * P], net.ident[0:S, 0:S])
                        last.then_inc(sem["rt_psum"], 1)
                        pe.wait_ge(sem["rt_ready"], e + 1)
                        pe.wait_ge(w_loaded[slot], 32 * (r + 1))
                        for f in range(FC):
                            if f >= 4:
                                pe.wait_ge(sem["h_ready"], e * FC + f - 3)
                            for k in range(KC):
                                last = pe.matmul(wide[:, f % 4, 0:CR], w1[:, slot, k, f * P:(f + 1) * P], rt[:, k, :], start=k == 0, stop=k == KC - 1)
                            last.then_inc(sem["h_psum"], 1)
                        pe.wait_ge(sem["h_ready"], e * FC + FC)
                        for c in range(RT):
                            for f in range(FC):
                                last = pe.matmul(summed[0:S, c, 0:E], hidden[:, f, c * S:(c + 1) * S], w2[:, slot, f, :], start=f == 0, stop=f == FC - 1)
                        last.then_inc(sem["y_psum"], 1)

            @block.scalar
            def _(act):
                norm_stats_scalar(act, net, sem["var_ready"], sem["std_ready"])
                for b in range(B):
                    act.wait_ge(sem["xt_psum"], b + 1)
                    act.activation(xt[:, :, b % 2, :], turned[:, b % 2, 0:KC * S].rearrange("p (k s) -> p k s", k=KC), ACT.Copy).then_inc(sem["xt_ready"], 1)
                act.wait_ge(sem["gap_ready"], 1)
                act.activation(t.exp[:], t.gap[:], ACT.Exp).then_inc(sem["exp_ready"], 1)
                with act.Fori(0, NE // SLOTS) as r:
                    for slot in range(SLOTS):
                        e = SLOTS * r + slot
                        act.wait_ge(sem["rt_psum"], e + 1)
                        act.activation(rt[:].rearrange("p k (c s) -> p c k s", c=RT), turned[:, :, 0:KC * S].rearrange("p c (k s) -> p c k s", k=KC),
                                       ACT.Copy).then_inc(sem["rt_ready"], 1)
                        for f in range(FC):
                            act.wait_ge(sem["h_psum"], e * FC + f + 1)
                            act.activation(hidden[:, f, :], wide[:, f % 4, 0:CR], ACT.Gelu).then_inc(sem["h_ready"], 1)
                        act.wait_ge(sem["y_ready"], e + 1)
                        act.dma_start(sorted_y.rearrange("(e r s) d -> e s r d", r=RT, s=S)[e], out[:, slot]).then_inc(stored[slot], 16)

            @block.vector
            def _(dve):
                dve.memset(ones[:], 1.0)
                dve.memset(start[:, 0, :], 0.0)
                dve.memset(base[:, 0:1], 0.0)
                norm_stats_vector(dve, net, sem["var_ready"], sem["std_ready"])
                with dve.Fori(0, B) as b:
                    normalise(dve, net, xn[:, b, :], b).then_inc(sem["xn_ready"], 1)
                dve.wait_ge(sem["loaded"], n_loaded)
                dve.wait_ge(sem["l_psum"], 1)
                dve.tensor_copy(t.logits[:], summed[0:S, 0, 0:B * NE].rearrange("s (b e) -> s b e", b=B))
                dve.drain()
                top_two_vector(dve, net, t, sem["gap_ready"], sem["exp_ready"])
                dve.tensor_tensor(both[:], t.hot[0][:], t.hot[1][:], ALU.add).then_inc(sem["both_ready"], 1)
                dve.wait_ge(sem["count_psum"], 1)
                dve.tensor_copy(total[:], summed[0:S, 1, B * NE:2 * B * NE].rearrange("s (b e) -> s b e", b=B))
                dve.drain()
                for b in range(B):
                    dve.tensor_tensor(start[:, b + 1, :], start[:, b, :], total[:, b, :], ALU.add)
                    dve.drain()
                for e in range(NE - 1):
                    dve.tensor_tensor(base[:, e + 1:e + 2], base[:, e:e + 1], start[:, B, e:e + 1], ALU.add)
                    dve.drain()
                dve.tensor_tensor(rank[:], start[:, 0:B, :], summed[0:S, 1, 0:B * NE].rearrange("s (b e) -> s b e", b=B), ALU.add)
                dve.drain()
                dve.tensor_tensor(rank[:], rank[:], base[:].unsqueeze(1).broadcast_to([S, B, NE]), ALU.add)
                dve.drain()
                for k in range(TOP):
                    dve.tensor_tensor(mine[:], rank[:], t.hot[k][:], ALU.mult)
                    dve.drain()
                    dve.tensor_reduce(place[:, k, :], mine[:], X_AX, ALU.add)
                    dve.drain()
                dve.tensor_copy(placei[:], place[:].rearrange("s k b -> s (k b)")).then_inc(sem["place_ready"], 1)
                for slot in range(SLOTS):
                    dve.wait_ge(sem["y_psum"], slot + 1)
                    dve.tensor_copy(out[:, slot], summed[0:S, :, 0:E]).then_inc(sem["y_ready"], 1)
                with dve.Fori(1, NE // SLOTS) as r:
                    for slot in range(SLOTS):
                        dve.wait_ge(stored[slot], 16 * r)
                        dve.wait_ge(sem["y_psum"], SLOTS * r + slot + 1)
                        dve.tensor_copy(out[:, slot], summed[0:S, :, 0:E]).then_inc(sem["y_ready"], 1)
                dve.wait_ge(sem["gathered"], 16 * TOP * B)
                for k in range(TOP):
                    for b in range(B):
                        dve.scalar_tensor_tensor(out=net.x[:, b, :], in0=back[:, k * B + b, :], scalar=t.prob[k][:, b, :],
                                                 in1=net.x[:, b, :], op0=ALU.mult, op1=ALU.add)
                    dve.drain()


@sublayer
def l3_attn(net):
    nc, dram = net.nc, net.dram
    H, D, C, T = 16, 16, 64, B
    HC = H * C
    with ExitStack() as ctx:
        def sb(n, shape, dt=F32):
            return ctx.enter_context(nc.sbuf_tensor("l3a_" + n, shape, dt))

        wqk, wv, wo = sb("wqk", [P, KC, 2 * E]), sb("wv", [P, KC, E]), sb("wo", [P, KC, E])
        bqk, bv, bo = sb("bqk", [S, 2 * E]), sb("bv", [S, E]), sb("bo", [S, E])
        qc = sb("qc", [P, KC, HC // KC])
        beta = sb("beta", [S, H])
        pairs = [(wqk[:], dram["l3a_wqk"]), (wv[:], dram["l3a_wv"]), (wo[:], dram["l3a_wo"]), (qc[:], dram["l3a_qc"]),
                 (bqk[:], dram["l3a_bqk"].partition_broadcast(S)), (bv[:], dram["l3a_bv"].partition_broadcast(S)),
                 (bo[:], dram["l3a_bo"].partition_broadcast(S)), (beta[:], dram["l3a_beta"].partition_broadcast(S))]
        n_loaded = 16 * len(pairs)
        xn = sb("xn", [S, E])
        xt = sb("xt", [P, KC, S])
        qk1 = sb("qk1", [S, 2 * E])
        q = sb("q", [S, T, E])
        k_ = sb("k", [S, T, E])
        v = sb("v", [S, T, E])
        kt = sb("kt", [P, KC, S])
        cw = sb("cw", [S, T, HC])
        top = sb("top", [S, HC])
        norm = sb("norm", [S, HC])
        rnorm = sb("rnorm", [S, HC])
        prod = sb("prod", [S, T, HC])
        qkp = sb("qkp", [S, T, E])
        score = sb("score", [S, T, H])
        lg = sb("lg", [S, H, C])
        ex = sb("ex", [S, H, C])
        mx, sm = sb("mx", [S, H]), sb("sm", [S, H])
        qs = sb("qs", [S, H])
        o = sb("o", [S, E])
        ot = sb("ot", [P, KC, S])
        delta = sb("delta", [S, E])
        sem = {n: net.sem("l3a_" + n) for n in (
            "loaded", "var_ready", "std_ready", "beta_ready", "xn_ready", "xt_psum", "xt_ready", "qkv_psum", "k_ready", "kt_psum",
            "kt_ready", "cw_psum", "cw_copied", "shifted", "cw_ready", "lg_ready", "ex_ready", "o_ready", "ot_psum", "ot_ready", "out_psum")}
        wide, turned, summed = net.wide, net.turned, net.summed

        with nc.Block() as block:
            @block.sync
            def _(sp):
                load_weights(sp, net, pairs, sem["loaded"])

            @block.tensor
            def _(pe):
                pe.wait_ge(sem["loaded"], n_loaded)
                with pe.Fori(0, T) as t:
                    pe.wait_ge(sem["xn_ready"], t + 1)
                    for k in range(KC):
                        last = pe.transpose(turned[:, 0, k * S:(k + 1) * S], xn[:, k * P:(k + 1) * P], net.ident[0:S, 0:S])
                    last.then_inc(sem["xt_psum"], 1)
                    pe.wait_ge(sem["xt_ready"], t + 1)
                    for w, dst in ((wqk, wide[0:S, 0, :]), (wv, wide[0:S, 1, 0:E])):
                        for k in range(KC):
                            last = pe.matmul(dst, xt[:, k, :], w[:, k, :], start=k == 0, stop=k == KC - 1)
                    last.then_inc(sem["qkv_psum"], 1)
                    pe.wait_ge(sem["k_ready"], t + 1)
                    for k in range(KC):
                        last = pe.transpose(turned[:, 1, k * S:(k + 1) * S], qk1[:, E + k * P:E + (k + 1) * P], net.ident[0:S, 0:S])
                    last.then_inc(sem["kt_psum"], 1)
                    pe.wait_ge(sem["kt_ready"], t + 1)
                    for m in range(KC):
                        last = pe.matmul(wide[0:S, 2 + m, :], kt[:, m, :], qc[:, m, :], start=True, stop=True)
                    last.then_inc(sem["cw_psum"], 1)
                for t in range(T):
                    pe.wait_ge(sem["o_ready"], t + 1)
                    for k in range(KC):
                        last = pe.transpose(turned[:, 0, k * S:(k + 1) * S], o[:, k * P:(k + 1) * P], net.ident[0:S, 0:S])
                    last.then_inc(sem["ot_psum"], 1)
                    pe.wait_ge(sem["ot_ready"], t + 1)
                    for k in range(KC):
                        last = pe.matmul(summed[0:S, 0, 0:E], ot[:, k, :], wo[:, k, :], start=k == 0, stop=k == KC - 1)
                    last.then_inc(sem["out_psum"], 1)

            @block.scalar
            def _(act):
                norm_stats_scalar(act, net, sem["var_ready"], sem["std_ready"])
                act.wait_ge(sem["loaded"], n_loaded)
                act.activation(beta[:], beta[:], ACT.Exp).then_inc(sem["beta_ready"], 1)
                with act.Fori(0, T) as t:
                    act.wait_ge(sem["xt_psum"], t + 1)
                    act.activation(xt[:], turned[:, 0, 0:KC * S].rearrange("p (k s) -> p k s", k=KC), ACT.Copy).then_inc(sem["xt_ready"], 1)
                    act.wait_ge(sem["kt_psum"], t + 1)
                    act.activation(kt[:], turned[:, 1, 0:KC * S].rearrange("p (k s) -> p k s", k=KC), ACT.Copy).then_inc(sem["kt_ready"], 1)
                    act.wait_ge(sem["cw_psum"], t + 1)
                    act.activation(cw[:, t, :], wide[0:S, 2:4, :].rearrange("s a n -> s (a n)"), ACT.Copy).then_inc(sem["cw_copied"], 1)
                for t in range(T):
                    act.wait_ge(sem["shifted"], t + 1)
                    act.activation(cw[:, t, :], cw[:, t, :], ACT.Exp).then_inc(sem["cw_ready"], 1)
                for t in range(T):
                    act.wait_ge(sem["lg_ready"], t + 1)
                    act.activation(ex[:], lg[:], ACT.Exp).then_inc(sem["ex_ready"], 1)
                    act.wait_ge(sem["ot_psum"], t + 1)
                    act.activation(ot[:], turned[:, 0, 0:KC * S].rearrange("p (k s) -> p k s", k=KC), ACT.Copy).then_inc(sem["ot_ready"], 1)

            @block.vector
            def _(dve):
                norm_stats_vector(dve, net, sem["var_ready"], sem["std_ready"])
                dve.wait_ge(sem["beta_ready"], 1)
                dve.tensor_scalar(qs[:], beta[:], float(D) ** 0.5, None, ALU.mult)
                dve.drain()
                dve.reciprocal(qs[:], qs[:])
                dve.drain()
                with dve.Fori(0, T) as t:
                    normalise(dve, net, xn[:], t).then_inc(sem["xn_ready"], 1)
                    dve.wait_ge(sem["qkv_psum"], t + 1)
                    dve.tensor_tensor(qk1[:], wide[0:S, 0, :], bqk[:], ALU.add).then_inc(sem["k_ready"], 1)
                    dve.tensor_tensor(v[:, t, :], wide[0:S, 1, 0:E], bv[:], ALU.add)
                    dve.drain()
                    dve.tensor_copy(k_[:, t, :], qk1[:, E:2 * E])
                    dve.tensor_tensor(q[:, t, :].rearrange("s (h d) -> s h d", h=H), qk1[:, 0:E].rearrange("s (h d) -> s h d", h=H),
                                      qs[:].unsqueeze(2).broadcast_to([S, H, D]), ALU.mult)
                    dve.wait_ge(sem["cw_copied"], t + 1)
                dve.drain()
                dve.tensor_reduce(top[:], cw[:].rearrange("s t n -> s n t"), X_AX, ALU.max)
                dve.drain()
                for t in range(T):
                    dve.tensor_tensor(cw[:, t, :], cw[:, t, :], top[:], ALU.subtract).then_inc(sem["shifted"], 1)
                for t in range(T):
                    n = t + 1
                    dve.wait_ge(sem["cw_ready"], t + 1)
                    if t == 0:
                        dve.tensor_copy(norm[:], cw[:, 0, :])
                    else:
                        dve.tensor_tensor(norm[:], norm[:], cw[:, t, :], ALU.add)
                    dve.tensor_tensor(qkp[:, 0:n, :], k_[:, 0:n, :], q[:, t, :].unsqueeze(1).broadcast_to([S, n, E]), ALU.mult)
                    dve.drain()
                    dve.reciprocal(rnorm[:], norm[:])
                    dve.tensor_reduce(score[:, 0:n, :], qkp[:, 0:n, :].rearrange("s t (h d) -> s t h d", h=H), X_AX, ALU.add)
                    dve.drain()
                    dve.tensor_tensor(prod[:, 0:n, :].rearrange("s t (h c) -> s t h c", h=H), cw[:, 0:n, :].rearrange("s t (h c) -> s t h c", h=H),
                                      score[:, 0:n, :].unsqueeze(3).broadcast_to([S, n, H, C]), ALU.mult)
                    dve.drain()
                    flat = lg[:].rearrange("s h c -> s (h c)")
                    dve.tensor_reduce(flat, prod[:, 0:n, :].rearrange("s t n -> s n t"), X_AX, ALU.add)
                    dve.drain()
                    dve.tensor_tensor(flat, flat, rnorm[:], ALU.mult)
                    dve.drain()
                    dve.tensor_reduce(mx[:], lg[:], X_AX, ALU.max)
                    dve.drain()
                    dve.tensor_tensor(lg[:], lg[:], mx[:].unsqueeze(2).broadcast_to([S, H, C]), ALU.subtract).then_inc(sem["lg_ready"], 1)
                    dve.wait_ge(sem["ex_ready"], t + 1)
                    dve.tensor_reduce(sm[:], ex[:], X_AX, ALU.add)
                    dve.tensor_tensor(flat, ex[:].rearrange("s h c -> s (h c)"), rnorm[:], ALU.mult)
                    dve.drain()
                    dve.reciprocal(sm[:], sm[:])
                    dve.tensor_tensor(prod[:, 0:n, :], cw[:, 0:n, :], flat.unsqueeze(1).broadcast_to([S, n, HC]), ALU.mult)
                    dve.drain()
                    dve.tensor_reduce(score[:, 0:n, :], prod[:, 0:n, :].rearrange("s t (h c) -> s t h c", h=H), X_AX, ALU.add)
                    dve.drain()
                    dve.tensor_tensor(score[:, 0:n, :], score[:, 0:n, :], sm[:].unsqueeze(1).broadcast_to([S, n, H]), ALU.mult)
                    dve.drain()
                    dve.tensor_tensor(qkp[:, 0:n, :].rearrange("s t (h d) -> s t h d", h=H), v[:, 0:n, :].rearrange("s t (h d) -> s t h d", h=H),
                                      score[:, 0:n, :].unsqueeze(3).broadcast_to([S, n, H, D]), ALU.mult)
                    dve.drain()
                    dve.tensor_reduce(o[:], qkp[:, 0:n, :].rearrange("s t n -> s n t"), X_AX, ALU.add).then_inc(sem["o_ready"], 1)
                    dve.wait_ge(sem["out_psum"], t + 1)
                    dve.tensor_tensor(delta[:], summed[0:S, 0, 0:E], bo[:], ALU.add)
                    dve.drain()
                    dve.tensor_tensor(net.x[:, t, :], net.x[:, t, :], delta[:], ALU.add)
                    dve.drain()


@sublayer
def l3_ffn(net):
    nc, dram = net.nc, net.dram
    with ExitStack() as ctx:
        def sb(n, shape, dt=F32):
            return ctx.enter_context(nc.sbuf_tensor("l3f_" + n, shape, dt))

        wg, we = sb("wg", [P, KC, E]), sb("we", [P, KC, NE * E])
        bg, be = sb("bg", [S, E]), sb("be", [NE, E])
        iota = sb("iota", [S, B, NE])
        pairs = [(wg[:], dram["l3f_wg"]), (we[:], dram["l3f_we"]), (bg[:], dram["l3f_bg"].partition_broadcast(S)),
                 (be[:], dram["l3f_be"]), (iota[:], dram["iota8"])]
        n_loaded = 16 * len(pairs)
        xn = sb("xn", [S, E])
        xt = sb("xt", [P, KC, S])
        lg, ex = sb("lg", [S, E]), sb("ex", [S, E])
        top, ntop, sm, p = sb("top", [S, 8]), sb("ntop", [S, 1]), sb("sm", [S, 1]), sb("p", [S, 1])
        which, whichf = sb("which", [S, 8], U32), sb("whichf", [S, 1])
        hot = sb("hot", [S, NE])
        hot_t = sb("hot_t", [NE, S])
        acc = sb("acc", [S, E])
        sem = {n: net.sem("l3f_" + n) for n in (
            "loaded", "var_ready", "std_ready", "xn_ready", "xt_psum", "xt_ready", "g_psum", "z_psum", "top_ready", "ex_ready",
            "hot_ready", "ht_psum", "ht_ready", "b_psum")}
        wide, turned, summed = net.wide, net.turned, net.summed

        with nc.Block() as block:
            @block.sync
            def _(sp):
                load_weights(sp, net, pairs, sem["loaded"])

            @block.tensor
            def _(pe):
                pe.wait_ge(sem["loaded"], n_loaded)
                with pe.Fori(0, B) as b:
                    pe.wait_ge(sem["xn_ready"], b + 1)
                    for k in range(KC):
                        last = pe.transpose(turned[:, 0, k * S:(k + 1) * S], xn[:, k * P:(k + 1) * P], net.ident[0:S, 0:S])
                    last.then_inc(sem["xt_psum"], 1)
                    pe.wait_ge(sem["xt_ready"], b + 1)
                    for k in range(KC):
                        last = pe.matmul(summed[0:S, 0, 0:E], xt[:, k, :], wg[:, k, :], start=k == 0, stop=k == KC - 1)
                    last.then_inc(sem["g_psum"], 1)
                    for n in range(4):
                        for k in range(KC):
                            last = pe.matmul(wide[0:S, n, :], xt[:, k, :], we[:, k, n * 512:(n + 1) * 512], start=k == 0, stop=k == KC - 1)
                    last.then_inc(sem["z_psum"], 1)
                    pe.wait_ge(sem["hot_ready"], b + 1)
                    pe.transpose(turned[0:NE, 1, 0:S], hot[:], net.ident[0:S, 0:S]).then_inc(sem["ht_psum"], 1)
                    pe.wait_ge(sem["ht_ready"], b + 1)
                    pe.matmul(summed[0:S, 1, 0:E], hot_t[:], be[:], start=True, stop=True).then_inc(sem["b_psum"], 1)

            @block.scalar
            def _(act):
                norm_stats_scalar(act, net, sem["var_ready"], sem["std_ready"])
                with act.Fori(0, B) as b:
                    act.wait_ge(sem["xt_psum"], b + 1)
                    act.activation(xt[:], turned[:, 0, 0:KC * S].rearrange("p (k s) -> p k s", k=KC), ACT.Copy).then_inc(sem["xt_ready"], 1)
                    act.wait_ge(sem["top_ready"], b + 1)
                    act.activation(ex[:], lg[:], ACT.Exp, bias=ntop[:], accum_out=sm[:]).then_inc(sem["ex_ready"], 1)
                    act.wait_ge(sem["ht_psum"], b + 1)
                    act.activation(hot_t[:], turned[0:NE, 1, 0:S], ACT.Copy).then_inc(sem["ht_ready"], 1)

            @block.vector
            def _(dve):
                norm_stats_vector(dve, net, sem["var_ready"], sem["std_ready"])
                dve.wait_ge(sem["loaded"], n_loaded)
                with dve.Fori(0, B) as b:
                    normalise(dve, net, xn[:], b).then_inc(sem["xn_ready"], 1)
                    dve.wait_ge(sem["g_psum"], b + 1)
                    dve.tensor_tensor(lg[:], summed[0:S, 0, 0:E], bg[:], ALU.add)
                    dve.drain()
                    dve.max(top[:], lg[:])
                    dve.drain()
                    dve.tensor_scalar(ntop[:], top[:, 0:1], -1.0, None, ALU.mult).then_inc(sem["top_ready"], 1)
                    dve.wait_ge(sem["ex_ready"], b + 1)
                    dve.tensor_copy(p[:], sm[:])
                    dve.max(top[:], ex[:])
                    dve.drain()
                    dve.max_index(which[:], top[:], ex[:])
                    dve.reciprocal(p[:], p[:])
                    dve.drain()
                    dve.tensor_scalar(which[:, 0:1], which[:, 0:1], NE - 1, None, ALU.bitwise_and)
                    dve.tensor_tensor(p[:], p[:], top[:, 0:1], ALU.mult)
                    dve.drain()
                    dve.tensor_copy(whichf[:], which[:, 0:1])
                    dve.drain()
                    dve.tensor_tensor(hot[:], whichf[:].broadcast_to([S, NE]), iota[:, 0, :], ALU.is_equal).then_inc(sem["hot_ready"], 1)
                    dve.wait_ge(sem["b_psum"], b + 1)
                    dve.wait_ge(sem["z_psum"], b + 1)
                    dve.tensor_copy(acc[:], summed[0:S, 1, 0:E])
                    for e in range(NE):
                        dve.drain()
                        dve.scalar_tensor_tensor(out=acc[:], in0=wide[0:S, e // 2, (e % 2) * E:(e % 2 + 1) * E], scalar=hot[:, e:e + 1],
                                                 in1=acc[:], op0=ALU.mult, op1=ALU.add)
                    dve.drain()
                    dve.tensor_scalar(acc[:], acc[:], 0.0, p[:], ALU.max, ALU.mult)
                    dve.drain()
                    dve.tensor_tensor(net.x[:, b, :], net.x[:, b, :], acc[:], ALU.add)
                    dve.drain()


def more_layouts(a, d, wide, col):
    def experts(w):
        return w.reshape(w.shape[0], -1, P, w.shape[-1]).transpose(0, 2, 1, 3)

    d["iota8"] = np.broadcast_to(np.arange(NE, dtype=np.float32), (S, B, NE))
    d["before"] = (np.arange(S)[:, None] < np.arange(S)[None, :]).astype(np.float32)
    d["l0f_w1"] = experts(np.concatenate([a["L0_ffn_W1"], a["L0_ffn_Ws1"][None]]))
    d["l0f_w2"] = experts(np.concatenate([a["L0_ffn_W2"], a["L0_ffn_Ws2"][None]]))
    d["l0f_wr"] = wide(a["L0_ffn_Wr"])
    d["l1f_w1"] = experts(np.concatenate([a["L1_ffn_w1"], a["L1_ffn_ws1"][None]]))
    d["l1f_w2"] = experts(np.concatenate([a["L1_ffn_w2"], a["L1_ffn_ws2"][None]]))
    d["l1f_wr"] = wide(a["L1_ffn_gate_w"])
    d["l1f_br"] = a["L1_ffn_gate_b"]
    d["l1f_b1"] = np.concatenate([a["L1_ffn_b1"], a["L1_ffn_bs1"][None]]).reshape(NE + 1, -1, P).transpose(0, 2, 1)
    d["l1f_b2"] = np.concatenate([a["L1_ffn_b2"], a["L1_ffn_bs2"][None]])
    d["l1a_wqk"] = wide(np.concatenate([a["L1_attn_Wq"], a["L1_attn_Wk"]], axis=1))
    d["l1a_bqk"] = np.concatenate([a["L1_attn_bq"], a["L1_attn_bk"]])
    d["l1a_wv"], d["l1a_wo"] = wide(a["L1_attn_Wv"]), wide(a["L1_attn_Wo"])
    d["l1a_bv"], d["l1a_bo"] = a["L1_attn_bv"], a["L1_attn_bo"]
    for n in ("delta", "alpha", "beta", "gamma"):
        d["l2a_" + n] = a["L2_attn_" + n].reshape(KC, P, 2).transpose(1, 0, 2)
    d["l2a_omega"] = col(a["L2_attn_omega"])
    d["l2f_wr"] = wide(a["L2_ffn_Wr"].T)
    d["l2f_w1"], d["l2f_w2"] = experts(a["L2_ffn_W1"]), experts(a["L2_ffn_W2"])
    d["l3a_wqk"] = wide(np.concatenate([a["L3_attn_Wq"].T, a["L3_attn_Wk"].T], axis=1))
    d["l3a_bqk"] = np.concatenate([a["L3_attn_bq"], a["L3_attn_bk"]])
    d["l3a_wv"], d["l3a_wo"] = wide(a["L3_attn_Wv"].T), wide(a["L3_attn_Wo"].T)
    d["l3a_bv"], d["l3a_bo"], d["l3a_beta"] = a["L3_attn_bv"], a["L3_attn_bo"], a["L3_attn_beta"]
    H, D, C = 16, 16, 64
    blocks = np.zeros((H, D, H, C), np.float32)
    for h in range(H):
        blocks[h, :, h, :] = a["L3_attn_q_c"].reshape(C, H, D)[:, h, :].T
    half = H // KC
    d["l3a_qc"] = np.stack([blocks[m * half:(m + 1) * half, :, m * half:(m + 1) * half].reshape(P, half * C) for m in range(KC)], axis=1)
    d["l3f_wg"] = wide(a["L3_ffn_Wg"])
    d["l3f_we"] = wide(a["L3_ffn_We"].transpose(1, 0, 2).reshape(E, NE * E))
    d["l3f_bg"], d["l3f_be"] = a["L3_ffn_bg"], a["L3_ffn_be"]


def build(nc, dram):
    with ExitStack() as ctx:
        net = Net(nc, ctx, dram)
        setup(net)
        l0_attn(net)
        cross_attn(net, "l0x", 16, rope=True, biases=True, mask=("key_mask", I32))
        moe(net, "l0f", P)
        l1_attn(net)
        cross_attn(net, "l1x", 16, biases=True, gate=True)
        moe(net, "l1f", 1024, biases=True)
        l2_attn(net)
        cross_attn(net, "l2x", 4, mask=("query_mask", U8))
        l2_ffn(net)
        l3_attn(net)
        cross_attn(net, "l3x", 16)
        l3_ffn(net)
        store(net)


def _layouts(a):
    def wide(w):
        return w.reshape(-1, P, w.shape[-1]).transpose(1, 0, 2)

    def col(b):
        return b.reshape(-1, P).T

    d = {"x": a["x"], "ident": np.eye(P, dtype=np.float32)}
    d["causal"] = np.where(np.arange(S)[:, None] < np.arange(S)[None, :], np.float32(NEG), np.float32(0))
    d["ctxt"] = a["ctx_1024"].transpose(0, 2, 1).reshape(B, KC, P, SKV).transpose(0, 2, 1, 3)
    for D in (16, 64):
        d[f"headmask{D}"] = (np.arange(P)[:, None] // D == np.arange(P // D)[None, :]).astype(np.float32)
    for n in ("q", "k", "v"):
        d["l0a_w" + n] = wide(a["L0_attn_w_" + n].reshape(-1, E).T)
    d["l0a_wo"] = wide(a["L0_attn_w_o"])
    for k, n in (("l0x", "L0_xattn"), ("l1x", "L1_xattn")):
        for m in "qkvo":
            d[f"{k}_w{m}"] = wide(a[f"{n}_W{m}"])
        for m in "qk":
            d[f"{k}_b{m}"] = col(a[f"{n}_b{m}"])
        for m in "vo":
            d[f"{k}_b{m}"] = a[f"{n}_b{m}"]
    wkv = a["L2_xattn_Wkv"]
    for m, w in (("q", a["L2_xattn_Wq"]), ("k", wkv[:E]), ("v", wkv[E:]), ("o", a["L2_xattn_Wout"])):
        d["l2x_w" + m] = wide(w.T)
    for m in "qkvo":
        d["l3x_w" + m] = wide(a["L3_xattn_W" + m].T)
    d["l3x_bo"] = a["L3_xattn_bo"]
    d["key_mask"] = a["mask_Bx1x1xS2_if1"].reshape(B, SKV)
    bits = np.zeros((B, S, -(-SKV // 4) * 4), np.bool_)
    bits[:, :, 0:SKV] = a["mask_BxSxS2_bk0"]
    d["query_mask"] = bits.view(np.int32)
    D = 16
    r = np.arange(P) % D
    inv = (1.0 / np.float32(10000.0) ** (np.arange(0, D, 2, dtype=np.float32) / np.float32(D))).astype(np.float32)
    angle = (np.arange(SKV, dtype=np.float32)[None, :] * inv[r % (D // 2)][:, None]).astype(np.float32)
    d["rope_cos"], d["rope_sin"] = np.cos(angle), np.sin(angle)
    swap = np.zeros((P, P), np.float32)
    for p in range(P):
        lower = r[p] < D // 2
        swap[p + D // 2 if lower else p - D // 2, p] = -1.0 if lower else 1.0
    d["rope_swap"] = swap
    rows = np.minimum(np.arange(PADKV), SKV - 1)
    d["energy"] = a["ctxb_2048x8"][:, rows].reshape(B * NCH, CH, 8).transpose(1, 0, 2)
    more_layouts(a, d, wide, col)
    return {k: np.ascontiguousarray(v) for k, v in d.items()}


def kernel(**inputs):
    import concourse.bacc as bacc
    from concourse.bass_utils import run_bass_kernel_spmd

    nc = bacc.Bacc("TRN2", target_bir_lowering=False, num_devices=1)
    arrays = {k + "_dram": v for k, v in _layouts({k: np.asarray(v) for k, v in inputs.items()}).items()}
    dram = {k[:-5]: nc.dram_tensor(k, v.shape, mybir.dt.from_np(v.dtype), kind="ExternalInput").ap()
            for k, v in arrays.items()}
    dram["out"] = nc.dram_tensor("out_dram", (B, S, E), F32, kind="ExternalOutput").ap()
    build(nc, dram)
    return run_bass_kernel_spmd(nc, [arrays], core_ids=[0]).results[0]["out_dram"]
```

```python
from contextlib import ExitStack

import numpy as np

import concourse.bass as bass
from concourse import mybir

B, S, E = 8, 100, 256
P = 128
KC = E // P
SKV = 361
CH = 121
NCH = 3
PADKV = CH * NCH
LAST = SKV - CH * (NCH - 1)
EPS = 1e-5
NEG = -1e30
NE = 8

ALU = mybir.AluOpType
ACT = mybir.ActivationFunctionType
F32 = mybir.dt.float32
I32 = mybir.dt.int32
U32 = mybir.dt.uint32
U8 = mybir.dt.uint8
X_AX = mybir.AxisListType.X


class Net:

    def __init__(self, nc, ctx, dram):
        self.nc, self.ctx, self.dram = nc, ctx, dram
        self.x = ctx.enter_context(nc.sbuf_tensor("x", [S, B, E], F32))
        self.ident = ctx.enter_context(nc.sbuf_tensor("ident", [P, P], F32))
        self.stats = ctx.enter_context(nc.sbuf_tensor("stats", [S, B, 6], F32))
        self.moments = ctx.enter_context(nc.sbuf_tensor("moments", [S, B, 2], F32))
        self.std = ctx.enter_context(nc.sbuf_tensor("std", [S, B, 1], F32))
        self.rstd = ctx.enter_context(nc.sbuf_tensor("rstd", [S, B, 1], F32))
        self.wide = ctx.enter_context(nc.psum_tensor("wide", [P, 4, 512], F32))
        self.turned = ctx.enter_context(nc.psum_tensor("turned", [P, 2, 512], F32))
        self.summed = ctx.enter_context(nc.psum_tensor("summed", [P, 2, 512], F32))

        self.sems = []

    def sem(self, name):
        self.sems.append(self.nc.alloc_semaphore(name=name))
        return self.sems[-1]

    def end_sublayer(self):
        self.nc.clear_and_free_semaphores(self.sems)
        self.nc.all_engine_barrier()
        self.sems = []


def sublayer(emit):
    def whole(net, *args, **kwargs):
        emit(net, *args, **kwargs)
        net.end_sublayer()
    return whole


def load_weights(sp, net, pairs, loaded):
    for tile, source in pairs:
        sp.dma_start(tile, source).then_inc(loaded, 16)
    return 16 * len(pairs)


def norm_stats_vector(dve, net, var_ready, std_ready):
    with dve.Fori(0, B) as b:
        dve.bn_stats(net.stats[:, b, :], net.x[:, b, :])
    dve.drain()
    for b in range(B):
        dve.bn_aggr(net.moments[:, b, :], net.stats[:, b, :])
    dve.drain()
    dve.tensor_scalar(net.std[:], net.moments[:, :, 1:2], EPS, None, ALU.add).then_inc(var_ready, 1)
    dve.wait_ge(std_ready, 1)
    dve.reciprocal(net.rstd[:], net.std[:])
    dve.drain()


def norm_stats_scalar(act, net, var_ready, std_ready):
    act.wait_ge(var_ready, 1)
    act.activation(net.std[:], net.std[:], ACT.Sqrt).then_inc(std_ready, 1)


def normalise(dve, net, out, b):
    return dve.tensor_scalar(out, net.x[:, b, :], net.moments[:, b, 0:1], net.rstd[:, b, :],
                             ALU.subtract, ALU.mult)


def by_pairs(engine, count, body):
    for slot in range(2):
        body(slot, slot, True)
    with engine.Fori(1, count // 2) as r:
        for slot in range(2):
            body(2 * r + slot, slot, False)


@sublayer
def setup(net):
    nc = net.nc
    loaded = net.sem("setup_loaded")
    with nc.Block() as block:
        @block.sync
        def _(sp):
            sp.dma_start(net.x[:], net.dram["x"].rearrange("b s d -> s b d")).then_inc(loaded, 16)
            sp.dma_start(net.ident[:], net.dram["ident"]).then_inc(loaded, 16)
            sp.wait_ge(loaded, 32)


def store(net):
    nc = net.nc
    stored = net.sem("stored")
    with nc.Block() as block:
        @block.sync
        def _(sp):
            sp.dma_start(net.dram["out"].rearrange("b s d -> s b d"), net.x[:]).then_inc(stored, 16)
            sp.wait_ge(stored, 16)


@sublayer
def l0_attn(net):
    nc, dram = net.nc, net.dram
    H, D, G = 16, 64, 4
    HD = H * D
    MC = HD // P
    PER = MC // 2
    NG = H // G

    def first_head(g):
        return (g // 2) * 2 * G + g % 2

    with ExitStack() as ctx:
        def sb(name, shape, dt=F32):
            return ctx.enter_context(nc.sbuf_tensor("l0a_" + name, shape, dt))

        wq, wk, wv = (sb(n, [P, KC, HD]) for n in ("wq", "wk", "wv"))
        wo = sb("wo", [P, MC, E])
        causal = sb("causal", [S, S])
        xn = sb("xn", [S, E])
        xt = sb("xt", [P, KC, S])
        qt, kt = sb("qt", [P, MC, S]), sb("kt", [P, MC, S])
        v1 = sb("v1", [S, H, D + 1])
        sc = sb("sc", [S, 2, G, S])
        mx = sb("mx", [S, H])
        pr = sb("pr", [S, 2, G, S])
        pt = sb("pt", [S, 2, G, S])
        rs = sb("rs", [S, H])
        y = sb("y", [S, H, D])
        yt = sb("yt", [P, MC, S])

        loaded, var_ready, std_ready, v1_ones, xn_ready, xt_psum, xt_ready, qk_psum, v_psum, q_ready, k_ready, v_ready, \
            s_psum, s_ready, p_ready, pt_psum, pt_ready, y_psum, y_ready, yt_psum, yt_ready, out_psum = (
                net.sem("l0a_" + n) for n in (
                    "loaded", "var_ready", "std_ready", "v1_ones", "xn_ready", "xt_psum", "xt_ready", "qk_psum", "v_psum",
                    "q_ready", "k_ready", "v_ready", "s_psum", "s_ready", "p_ready", "pt_psum", "pt_ready",
                    "y_psum", "y_ready", "yt_psum", "yt_ready", "out_psum"))
        wide, turned, summed = net.wide, net.turned, net.summed

        with nc.Block() as block:
            @block.sync
            def _(sp):
                load_weights(sp, net, [(wq[:], dram["l0a_wq"]), (wk[:], dram["l0a_wk"]), (wv[:], dram["l0a_wv"]),
                                       (wo[:], dram["l0a_wo"]), (causal[:], dram["causal"])], loaded)

            @block.tensor
            def _(pe):
                pe.wait_ge(loaded, 80)
                with pe.Fori(0, B) as b:
                    pe.wait_ge(xn_ready, b + 1)
                    for k in range(KC):
                        last = pe.transpose(turned[:, 0, k * S:(k + 1) * S], xn[:, k * P:(k + 1) * P], net.ident[0:S, 0:S])
                    last.then_inc(xt_psum, 1)
                    pe.wait_ge(xt_ready, b + 1)
                    for w, bank in ((wq, 0), (wk, 2)):
                        for m in range(MC):
                            for k in range(KC):
                                last = pe.matmul(wide[:, bank + m // PER, (m % PER) * S:(m % PER + 1) * S],
                                                 w[:, k, m * P:(m + 1) * P], xt[:, k, :], start=k == 0, stop=k == KC - 1)
                        last.then_inc(qk_psum, 1)
                    for n in range(2):
                        for k in range(KC):
                            last = pe.matmul(summed[0:S, n, :], xt[:, k, :], wv[:, k, n * 512:(n + 1) * 512],
                                             start=k == 0, stop=k == KC - 1)
                    last.then_inc(v_psum, 1)

                    def scores(g):
                        r = (g % 2) * D
                        for j in range(G):
                            m = first_head(g) // 2 + j
                            last = pe.matmul(wide[0:S, g, j * S:(j + 1) * S], qt[r:r + D, m, :],
                                             kt[r:r + D, m, :], start=True, stop=True)
                        last.then_inc(s_psum, 1)

                    def turn(g):
                        pe.wait_ge(p_ready, b * NG + g + 1)
                        if g >= 2:
                            pe.wait_ge(pt_ready, b * NG + g - 1)
                        for j in range(G):
                            last = pe.transpose(turned[0:S, g % 2, j * S:(j + 1) * S], pr[:, g % 2, j, :],
                                                net.ident[0:S, 0:S])
                        last.then_inc(pt_psum, 1)

                    def weigh(g):
                        pe.wait_ge(pt_ready, b * NG + g + 1)
                        if g >= 2:
                            pe.wait_ge(y_ready, b * NG + g - 1)
                        for j in range(G):
                            last = pe.matmul(summed[0:S, g % 2, j * (D + 1):(j + 1) * (D + 1)], pt[:, g % 2, j, :],
                                             v1[:, first_head(g) + 2 * j, :], start=True, stop=True)
                        last.then_inc(y_psum, 1)

                    pe.wait_ge(q_ready, b + 1)
                    pe.wait_ge(k_ready, b + 1)
                    scores(0)
                    scores(1)
                    turn(0)
                    pe.wait_ge(v_ready, b + 1)
                    scores(2)
                    turn(1)
                    weigh(0)
                    scores(3)
                    turn(2)
                    weigh(1)
                    turn(3)
                    weigh(2)
                    weigh(3)
                    pe.wait_ge(y_ready, b * NG + NG)
                    for m in range(MC):
                        last = pe.transpose(wide[:, m // PER, (m % PER) * S:(m % PER + 1) * S],
                                            y[:, 2 * m:2 * m + 2, :].rearrange("s h d -> s (h d)"), net.ident[0:S, 0:S])
                    last.then_inc(yt_psum, 1)
                    pe.wait_ge(yt_ready, b + 1)
                    for m in range(MC):
                        last = pe.matmul(summed[0:S, 0, 0:E], yt[:, m, :], wo[:, m, :], start=m == 0, stop=m == MC - 1)
                    last.then_inc(out_psum, 1)

            @block.scalar
            def _(act):
                norm_stats_scalar(act, net, var_ready, std_ready)
                with act.Fori(0, B) as b:
                    act.wait_ge(xt_psum, b + 1)
                    act.activation(xt[:], turned[:, 0, 0:KC * S].rearrange("p (k s) -> p k s", k=KC), ACT.Copy).then_inc(xt_ready, 1)
                    act.wait_ge(qk_psum, 2 * b + 1)
                    act.activation(qt[:].rearrange("p (a m) s -> p a (m s)", a=2), wide[:, 0:2, 0:PER * S], ACT.Copy).then_inc(q_ready, 1)
                    act.wait_ge(v_psum, b + 1)
                    act.activation(v1[:, :, 0:D], summed[0:S, :, :].rearrange("s a (h d) -> s (a h) d", d=D), ACT.Copy).then_inc(v_ready, 1)

                    def exps(g):
                        act.wait_ge(s_ready, b * NG + g + 1)
                        if g >= 2:
                            act.wait_ge(pt_psum, b * NG + g - 1)
                        act.activation(pr[:, g % 2], sc[:, g % 2], ACT.Exp, scale=D ** -0.5).then_inc(p_ready, 1)

                    def copy_pt(g):
                        act.wait_ge(pt_psum, b * NG + g + 1)
                        if g >= 2:
                            act.wait_ge(y_psum, b * NG + g - 1)
                        act.activation(pt[:, g % 2], turned[0:S, g % 2, 0:G * S].rearrange("s (j t) -> s j t", j=G), ACT.Copy).then_inc(pt_ready, 1)

                    exps(0)
                    exps(1)
                    copy_pt(0)
                    exps(2)
                    copy_pt(1)
                    exps(3)
                    copy_pt(2)
                    copy_pt(3)
                    act.wait_ge(yt_psum, b + 1)
                    act.activation(yt[:].rearrange("p (a m) s -> p a (m s)", a=2), wide[:, 0:2, 0:PER * S], ACT.Copy).then_inc(yt_ready, 1)

            @block.vector
            def _(dve):
                dve.memset(v1[:, :, D:D + 1], 1.0)
                norm_stats_vector(dve, net, var_ready, std_ready)
                dve.wait_ge(loaded, 80)
                with dve.Fori(0, B) as b:
                    normalise(dve, net, xn[:], b).then_inc(xn_ready, 1)
                    dve.wait_ge(qk_psum, 2 * b + 2)
                    dve.tensor_copy(kt[:].rearrange("p (a m) s -> p a (m s)", a=2), wide[:, 2:4, 0:PER * S]).then_inc(k_ready, 1)

                    def shift(g):
                        dve.wait_ge(s_psum, b * NG + g + 1)
                        if g >= 2:
                            dve.wait_ge(p_ready, b * NG + g - 1)
                        one = sc[:, g % 2]
                        dve.tensor_tensor(one, wide[0:S, g, 0:G * S].rearrange("s (j t) -> s j t", j=G),
                                          causal[:].unsqueeze(1).broadcast_to([S, G, S]), ALU.add)
                        dve.drain()
                        dve.tensor_reduce(mx[:, g * G:(g + 1) * G], one, X_AX, ALU.max)
                        dve.drain()
                        dve.tensor_tensor(one, one, mx[:, g * G:(g + 1) * G].unsqueeze(2).broadcast_to([S, G, S]),
                                          ALU.subtract).then_inc(s_ready, 1)

                    def divide(g):
                        dve.wait_ge(y_psum, b * NG + g + 1)
                        got = summed[0:S, g % 2, 0:G * (D + 1)].rearrange("s (j d) -> s j d", j=G)
                        dve.reciprocal(rs[:, g * G:(g + 1) * G].unsqueeze(2), got[:, :, D:D + 1])
                        dve.drain()
                        dve.tensor_tensor(y[:, first_head(g):first_head(g) + 2 * G - 1:2, :], got[:, :, 0:D],
                                          rs[:, g * G:(g + 1) * G].unsqueeze(2).broadcast_to([S, G, D]), ALU.mult).then_inc(y_ready, 1)

                    for g in range(NG):
                        shift(g)
                        if g >= 3:
                            divide(g - 3)
                    for g in range(1, NG):
                        divide(g)
                    dve.wait_ge(out_psum, b + 1)
                    dve.tensor_tensor(net.x[:, b, :], net.x[:, b, :], summed[0:S, 0, 0:E], ALU.add)
                    dve.drain()


@sublayer
def cross_attn(net, name, H, rope=False, biases=False, mask=None, gate=False):
    nc, dram = net.nc, net.dram
    D = E // H
    HP = P // D
    SCALE = D ** -0.5
    FRONT = ["xt", "q", "k0", "k1", "v0", "v1"]
    if rope:
        FRONT = ["xt", "q", "qswap", "k0", "k0swap", "k1", "k1swap", "v0", "v1"]
    TAIL = ["yt", "out"]
    if H == 16:
        timetable = {4 + n: [piece] for n, piece in enumerate(TAIL + FRONT)}
    else:
        timetable = {0: FRONT[0:2], 1: FRONT[2:4], 2: FRONT[4:6], 3: TAIL}
    with ExitStack() as ctx:
        def sb(n, shape, dt=F32):
            return ctx.enter_context(nc.sbuf_tensor(name + "_" + n, shape, dt))

        w = {n: sb(n, [P, KC, E]) for n in ("wq", "wk", "wv", "wo")}
        pairs = [(w[n][:], dram[name + "_" + n]) for n in w]
        headmask = sb("headmask", [P, HP])
        pairs.append((headmask[:], dram[f"headmask{D}"]))
        bo = None
        if biases:
            bq, bk, bv = sb("bq", [P, KC]), sb("bk", [P, KC]), sb("bv", [P, E])
            pairs += [(bq[:], dram[name + "_bq"]), (bk[:], dram[name + "_bk"]),
                      (bv[:], dram[name + "_bv"].partition_broadcast(P))]
        if name + "_bo" in dram:
            bo = sb("bo", [P, E])
            pairs.append((bo[:], dram[name + "_bo"].partition_broadcast(P)))
        if rope:
            swap = sb("swap", [P, P])
            cos, sin = sb("cos", [P, SKV]), sb("sin", [P, SKV])
            pairs += [(swap[:], dram["rope_swap"]), (cos[:], dram["rope_cos"]), (sin[:], dram["rope_sin"])]
            kraw, qraw = sb("kraw", [P, KC, SKV]), sb("qraw", [P, KC, S])
            ksin, qsin = sb("ksin", [P, SKV]), sb("qsin", [P, KC, S])
        if gate:
            energy = sb("energy", [CH, B * NCH, 8])
            gates = sb("gates", [CH, B * NCH])
            gsum = sb("gsum", [CH, B * NCH])
            pairs.append((energy[:], dram["energy"]))
        n_loaded = 16 * len(pairs)
        if mask:
            words = sb("words", [S, 2, dram[mask[0]].shape[-1]], I32)
            bias = sb("bias", [S, 2, SKV])
            sc = sb("sc", [S, 4, SKV])
        ctxt = sb("ctxt", [P, 2, KC, SKV])
        xn = sb("xn", [S, E])
        xt = sb("xt", [P, KC, S])
        qt = sb("qt", [P, KC, S])
        qm = sb("qm", [P, 2, KC, HP, S])
        kt = sb("kt", [P, 2, KC, PADKV])
        v1 = sb("v1", [CH, 2, NCH, H, D + 1])
        mx, nmx = sb("mx", [S, H]), sb("nmx", [S, H])
        pr = sb("pr", [S, 4, PADKV])
        pt = sb("pt", [CH, 4, NCH, S])
        rs = sb("rs", [S, H])
        y = sb("y", [S, H, D])
        yt = sb("yt", [P, KC, S])
        delta = sb("delta", [S, E])

        sem = {n: net.sem(name + "_" + n) for n in (
            "loaded", "ctx0", "ctx1", "mask_used", "var_ready", "std_ready", "cleared", "gate_sum", "gate_ready", "xn_ready",
            "side_psum", "side_done", "front_ready", "s_psum", "m_ready", "p_ready", "pt_psum", "pt_ready", "y_psum",
            "y_ready")}
        side, summed = net.summed[:, 1, :], net.summed[:, 0, :]
        wide, turned = net.wide, net.turned
        ctx_loaded = (sem["ctx0"], sem["ctx1"])
        per_ctx = 32 if mask else 16
        PER = len(FRONT) + len(TAIL)

        def pieces(b, step):
            last = isinstance(b, int) and b == B - 1
            first = isinstance(b, int) and b == 0
            order = [x for i in sorted(timetable) for x in timetable[i]
                     if not (first and x in TAIL) and not (last and x in FRONT)]
            before = len(FRONT) if first else 2 * len(FRONT) + (b - 1) * PER
            return [(x, before + order.index(x)) for x in timetable.get(step, []) if x in order]

        def walk(engine, front, step, finish):
            front(0, 0, [(x, n) for n, x in enumerate(FRONT)])
            for i in range(H):
                step(0, 0, i)
            with engine.Fori(0, (B - 2) // 2) as r:
                for n in (1, 2):
                    for i in range(H):
                        step(2 * r + n, n % 2, i)
            for i in range(H):
                step(B - 1, 1, i)
            finish()

        with nc.Block() as block:
            @block.sync
            def _(sp):
                load_weights(sp, net, pairs, sem["loaded"])

                def load_ctx(b, slot):
                    sp.dma_start(ctxt[:, slot], dram["ctxt"][b]).then_inc(ctx_loaded[slot], 16)
                    if mask:
                        src = dram[mask[0]][b]
                        if mask[0] == "key_mask":
                            src = src.partition_broadcast(S)
                        sp.dma_start(words[:, slot], src).then_inc(ctx_loaded[slot], 16)

                load_ctx(0, 0)
                load_ctx(1, 1)
                with sp.Fori(1, B // 2) as i:
                    for slot in range(2):
                        sp.wait_ge(sem["front_ready"], 2 * i + slot - 1)
                        if mask:
                            sp.wait_ge(sem["mask_used"], 2 * i + slot - 1)
                        load_ctx(2 * i + slot, slot)

            @block.tensor
            def _(pe):
                pe.wait_ge(sem["loaded"], n_loaded)
                pe.wait_ge(sem["cleared"], 1)
                if gate:
                    pe.wait_ge(sem["gate_ready"], 1)

                def piece(what, n, b, slot):
                    pe.wait_ge(sem["side_done"], n)
                    if what == "xt":
                        pe.wait_ge(sem["xn_ready"], b + 1)
                        for k in range(KC):
                            last = pe.transpose(side[:, k * S:(k + 1) * S], xn[:, k * P:(k + 1) * P], net.ident[0:S, 0:S])
                    elif what == "q":
                        for m in range(KC):
                            for k in range(KC):
                                last = pe.matmul(side[:, m * S:(m + 1) * S], w["wq"][:, k, m * P:(m + 1) * P], xt[:, k, :],
                                                 start=k == 0, stop=k == KC - 1)
                    elif what == "qswap":
                        for m in range(KC):
                            last = pe.matmul(side[:, m * S:(m + 1) * S], swap[:], qraw[:, m, :], start=True, stop=True)
                    elif what in ("k0", "k1"):
                        m = int(what[1])
                        if m == 0:
                            pe.wait_ge(ctx_loaded[slot], (b - slot) * (per_ctx // 2) + per_ctx)
                        for k in range(KC):
                            last = pe.matmul(side[:, 0:SKV], w["wk"][:, k, m * P:(m + 1) * P], ctxt[:, slot, k, :],
                                             start=k == 0, stop=k == KC - 1)
                    elif what in ("k0swap", "k1swap"):
                        last = pe.matmul(side[:, 0:SKV], swap[:], kraw[:, int(what[1]), :], start=True, stop=True)
                    elif what in ("v0", "v1"):
                        for c in (0, 1) if what == "v0" else (2,):
                            n_rows = CH if c < NCH - 1 else LAST
                            for k in range(KC):
                                last = pe.matmul(side[0:n_rows, (c % 2) * E:(c % 2 + 1) * E],
                                                 ctxt[:, slot, k, c * CH:c * CH + n_rows], w["wv"][:, k, :],
                                                 start=k == 0, stop=k == KC - 1)
                    elif what == "yt":
                        pe.wait_ge(sem["y_ready"], b + 1)
                        for k in range(KC):
                            last = pe.transpose(side[:, k * S:(k + 1) * S], y[:].rearrange("s h d -> s (h d)")[:, k * P:(k + 1) * P],
                                                net.ident[0:S, 0:S])
                    elif what == "out":
                        for k in range(KC):
                            last = pe.matmul(side[0:S, 0:E], yt[:, k, :], w["wo"][:, k, :], start=k == 0, stop=k == KC - 1)
                    last.then_inc(sem["side_psum"], 1)

                def front(b, slot, listed):
                    for what, n in listed:
                        piece(what, n, b, slot)

                def turn(g, h, slot):
                    pe.wait_ge(sem["p_ready"], g + 1)
                    if not isinstance(g, int) or g >= 2:
                        pe.wait_ge(sem["pt_ready"], g - 1)
                    for c in range(NCH):
                        last = pe.transpose(turned[0:CH, h % 2, c * S:(c + 1) * S], pr[:, h % 4, c * CH:(c + 1) * CH], net.ident[0:S, 0:S])
                    last.then_inc(sem["pt_psum"], 1)

                def weigh(b, g, h, slot):
                    pe.wait_ge(sem["pt_ready"], g + 1)
                    if h == 0 and (not isinstance(b, int) or b >= 1):
                        pe.wait_ge(sem["y_ready"], b)
                    for c in range(NCH):
                        last = pe.matmul(summed[0:S, h * (D + 1):(h + 1) * (D + 1)], pt[:, h % 4, c, :], v1[:, slot, c, h, :],
                                         start=c == 0, stop=c == NCH - 1)
                    last.then_inc(sem["y_psum"], 1)

                def step(b, slot, i):
                    g = b * H + i
                    if i == 0:
                        pe.wait_ge(sem["front_ready"], b + 1)
                    if not isinstance(b, int) or g >= 4:
                        if mask:
                            pe.wait_ge(sem["m_ready"], g - 3)
                        else:
                            pe.wait_ge(sem["p_ready"], g - 3)
                    pe.matmul(wide[0:S, i % 4, 0:SKV], qm[:, slot, i // HP, i % HP, :], kt[:, slot, i // HP, 0:SKV],
                              start=True, stop=True).then_inc(sem["s_psum"], 1)
                    if i >= 2:
                        turn(g - 2, i - 2, slot)
                    elif not isinstance(b, int) or b >= 1:
                        turn(g - 2, H + i - 2, 1 - slot)
                    if i >= 3:
                        weigh(b, g - 3, i - 3, slot)
                    elif not isinstance(b, int) or b >= 1:
                        weigh(b - 1, g - 3, H + i - 3, 1 - slot)
                    for what, n in pieces(b, i):
                        if what in TAIL:
                            piece(what, n, b - 1, 1 - slot)
                        else:
                            piece(what, n, b + 1, 1 - slot)

                def finish():
                    g = B * H
                    for h in (H - 2, H - 1):
                        turn(B * H - H + h, h, 1)
                        weigh(B - 1, g - H + h - 1, h - 1, 1)
                    weigh(B - 1, g - 1, H - 1, 1)
                    for n, what in enumerate(TAIL):
                        piece(what, (PER * (B - 1) + len(FRONT)) + n, B - 1, 1)

                walk(pe, front, step, finish)

            @block.scalar
            def _(act):
                norm_stats_scalar(act, net, sem["var_ready"], sem["std_ready"])
                if gate:
                    act.wait_ge(sem["gate_sum"], 1)
                    act.activation(gates[:], gsum[:], ACT.Sigmoid).then_inc(sem["gate_ready"], 1)
                act.wait_ge(sem["loaded"], n_loaded)

                def piece(what, n, slot):
                    if what in ("xt", "yt"):
                        act.wait_ge(sem["side_psum"], n + 1)
                        act.activation((xt if what == "xt" else yt)[:], side[:, 0:KC * S].rearrange("p (k s) -> p k s", k=KC),
                                       ACT.Copy).then_inc(sem["side_done"], 1)
                    elif what in ("k0", "k1"):
                        m = int(what[1])
                        dst = kraw[:, m, :] if rope else kt[:, slot, m, 0:SKV]
                        act.wait_ge(sem["side_psum"], n + 1)
                        if biases:
                            last = act.activation(dst, side[:, 0:SKV], ACT.Identity, bias=bk[:, m:m + 1])
                        else:
                            last = act.activation(dst, side[:, 0:SKV], ACT.Copy)
                        last.then_inc(sem["side_done"], 1)

                def front(b, slot, listed):
                    for what, n in listed:
                        piece(what, n, slot)

                def step(b, slot, i):
                    g = b * H + i
                    act.wait_ge(sem["m_ready"], g + 1)
                    if not isinstance(b, int) or g >= 4:
                        act.wait_ge(sem["pt_psum"], g - 3)
                    src = sc[:, i % 4, :] if mask else wide[0:S, i % 4, 0:SKV]
                    act.activation(pr[:, i % 4, 0:SKV], src, ACT.Exp, bias=nmx[:, i:i + 1], scale=SCALE).then_inc(sem["p_ready"], 1)
                    for what, n in pieces(b, i):
                        piece(what, n, 1 - slot)

                def finish():
                    piece("yt", PER * (B - 1) + len(FRONT), 1)

                walk(act, front, step, finish)

            @block.vector
            def _(dve):
                dve.memset(v1[:], 0.0)
                dve.memset(kt[:, :, :, SKV:PADKV], 0.0)
                dve.memset(pr[:, :, SKV:PADKV], 0.0)
                dve.drain()
                dve.memset(v1[:, :, :, :, D:D + 1], 1.0).then_inc(sem["cleared"], 1)
                norm_stats_vector(dve, net, sem["var_ready"], sem["std_ready"])
                dve.wait_ge(sem["loaded"], n_loaded)
                if gate:
                    dve.tensor_reduce(gates[:], energy[:], X_AX, ALU.add, apply_absolute_value=True)
                    dve.drain()
                    dve.tensor_scalar(gsum[:], gates[:], 10.0 / 8, -10.0 * 0.1, ALU.mult, ALU.add).then_inc(sem["gate_sum"], 1)
                    dve.wait_ge(sem["gate_ready"], 1)

                def by_head(slot):
                    dve.drain()
                    for m in range(KC):
                        dve.tensor_tensor(qm[:, slot, m], qt[:, m, :].unsqueeze(1).broadcast_to([P, HP, S]),
                                          headmask[:].unsqueeze(2).broadcast_to([P, HP, S]), ALU.mult)

                def normal(b, slot):
                    normalise(dve, net, xn[:], b).then_inc(sem["xn_ready"], 1)
                    if mask:
                        dve.wait_ge(ctx_loaded[slot], (b - slot) * (per_ctx // 2) + per_ctx)
                        dve.tensor_scalar(bias[:, slot, :], words[:, slot, :].bitcast(mask[1])[:, 0:SKV], 0.0, NEG,
                                          ALU.is_equal, ALU.mult).then_inc(sem["mask_used"], 1)

                def piece(what, n, b, slot):
                    if what == "xt":
                        normal(b, slot)
                    elif what == "q":
                        dve.wait_ge(sem["side_psum"], n + 1)
                        out_q = qraw if rope else qt
                        for m in range(KC):
                            if biases:
                                last = dve.tensor_scalar(out_q[:, m, :], side[:, m * S:(m + 1) * S], bq[:, m:m + 1], None, ALU.add)
                            else:
                                last = dve.tensor_copy(out_q[:, m, :], side[:, m * S:(m + 1) * S])
                        last.then_inc(sem["side_done"], 1)
                        if not rope:
                            by_head(slot)
                    elif what == "qswap":
                        dve.drain()
                        for m in range(KC):
                            dve.tensor_tensor(qt[:, m, :], qraw[:, m, :], cos[:, 0:S], ALU.mult)
                        dve.wait_ge(sem["side_psum"], n + 1)
                        for m in range(KC):
                            last = dve.tensor_tensor(qsin[:, m, :], side[:, m * S:(m + 1) * S], sin[:, 0:S], ALU.mult)
                        last.then_inc(sem["side_done"], 1)
                        dve.drain()
                        dve.tensor_tensor(qt[:], qt[:], qsin[:], ALU.add)
                        by_head(slot)
                    elif what in ("k0swap", "k1swap"):
                        m = int(what[1])
                        dve.wait_ge(sem["side_psum"], n + 1)
                        dve.tensor_tensor(ksin[:], side[:, 0:SKV], sin[:], ALU.mult).then_inc(sem["side_done"], 1)
                        dve.tensor_tensor(kt[:, slot, m, 0:SKV], kraw[:, m, :], cos[:], ALU.mult)
                        dve.drain()
                        dve.tensor_tensor(kt[:, slot, m, 0:SKV], kt[:, slot, m, 0:SKV], ksin[:], ALU.add)
                        dve.drain()
                    elif what in ("v0", "v1"):
                        dve.wait_ge(sem["side_psum"], n + 1)
                        for c in (0, 1) if what == "v0" else (2,):
                            rows = CH if c < NCH - 1 else LAST
                            got = side[0:rows, (c % 2) * E:(c % 2 + 1) * E].rearrange("s (h d) -> s h d", h=H)
                            dst = v1[0:rows, slot, c, :, 0:D]
                            if biases:
                                last = dve.tensor_tensor(dst, got, bv[0:rows, :].rearrange("s (h d) -> s h d", h=H), ALU.add)
                            elif gate:
                                last = dve.tensor_copy(dst, got)
                            else:
                                last = dve.tensor_copy(dst, got)
                        last.then_inc(sem["side_done"], 1)
                        if gate:
                            dve.drain()
                            for c in (0, 1) if what == "v0" else (2,):
                                rows = CH if c < NCH - 1 else LAST
                                dst = v1[0:rows, slot, c, :, 0:D]
                                last = dve.tensor_scalar(dst, dst, gates[0:rows, bass.ds(b * NCH + c, 1)], None, ALU.mult)
                        if what == "v1":
                            dve.drain()
                            dve.tensor_copy(delta[0:1, 0:1], xn[0:1, 0:1]).then_inc(sem["front_ready"], 1)
                    elif what == "out":
                        dve.wait_ge(sem["side_psum"], n + 1)
                        if bo is not None:
                            dve.tensor_tensor(delta[:], side[0:S, 0:E], bo[0:S, :], ALU.add).then_inc(sem["side_done"], 1)
                            dve.drain()
                            dve.tensor_tensor(net.x[:, b, :], net.x[:, b, :], delta[:], ALU.add)
                        else:
                            dve.tensor_tensor(net.x[:, b, :], net.x[:, b, :], side[0:S, 0:E], ALU.add).then_inc(sem["side_done"], 1)
                        dve.drain()

                def front(b, slot, listed):
                    for what, n in listed:
                        piece(what, n, b, slot)

                def copy_pt(g, h):
                    dve.wait_ge(sem["pt_psum"], g + 1)
                    if not isinstance(g, int) or g >= 4:
                        dve.wait_ge(sem["y_psum"], g - 1)
                    dve.tensor_copy(pt[:, h % 4], turned[0:CH, h % 2, 0:NCH * S].rearrange("s (c t) -> s c t", c=NCH)).then_inc(sem["pt_ready"], 1)

                def divide(b):
                    dve.wait_ge(sem["y_psum"], (b + 1) * H)
                    got = summed[0:S, 0:H * (D + 1)].rearrange("s (h d) -> s h d", h=H)
                    dve.reciprocal(rs[:].unsqueeze(2), got[:, :, D:D + 1])
                    dve.drain()
                    dve.tensor_tensor(y[:], got[:, :, 0:D], rs[:].unsqueeze(2).broadcast_to([S, H, D]), ALU.mult).then_inc(sem["y_ready"], 1)

                def step(b, slot, i):
                    g = b * H + i
                    dve.wait_ge(sem["s_psum"], g + 1)
                    if mask:
                        if not isinstance(b, int) or g >= 4:
                            dve.wait_ge(sem["p_ready"], g - 3)
                        dve.memset(mx[0:1, i:i + 1], 0.0)
                        dve.drain()
                        dve.tensor_tensor_reduce(sc[:, i % 4, :], wide[0:S, i % 4, 0:SKV], bias[:, slot, :], 1.0, -3e38,
                                                 ALU.add, ALU.max, mx[:, i:i + 1])
                    else:
                        dve.tensor_reduce(mx[:, i:i + 1], wide[0:S, i % 4, 0:SKV], X_AX, ALU.max)
                    dve.drain()
                    dve.tensor_scalar(nmx[:, i:i + 1], mx[:, i:i + 1], -SCALE, None, ALU.mult).then_inc(sem["m_ready"], 1)
                    if i == 3 and (not isinstance(b, int) or b >= 1):
                        divide(b - 1)
                    if i >= 2:
                        copy_pt(g - 2, i - 2)
                    elif not isinstance(b, int) or b >= 1:
                        copy_pt(g - 2, H + i - 2)
                    for what, n in pieces(b, i):
                        if what in TAIL:
                            piece(what, n, b - 1, 1 - slot)
                        else:
                            piece(what, n, b + 1, 1 - slot)

                def finish():
                    for h in (H - 2, H - 1):
                        copy_pt(B * H - H + h, h)
                    divide(B - 1)
                    piece("out", PER * (B - 1) + len(FRONT) + 1, B - 1, 1)

                walk(dve, front, step, finish)


def top_two_vector(dve, net, t, gap_ready, exp_ready):
    for b in range(B):
        dve.max(t.top[:, b, :], t.logits[:, b, :])
    dve.drain()
    for b in range(B):
        dve.max_index(t.which[:, b, :], t.top[:, b, :], t.logits[:, b, :])
    dve.tensor_tensor(t.gap[:], t.top[:, :, 1:2], t.top[:, :, 0:1], ALU.subtract).then_inc(gap_ready, 1)
    dve.drain()
    dve.tensor_copy(t.whichf[:], t.which[:, :, 0:2])
    dve.drain()
    for k in range(2):
        dve.tensor_tensor(t.hot[k][:], t.whichf[:, :, k:k + 1].broadcast_to([S, B, NE]), t.iota[:], ALU.is_equal)
    dve.wait_ge(exp_ready, 1)
    dve.tensor_scalar(t.den[:], t.exp[:], 1.0, None, ALU.add)
    dve.drain()
    dve.reciprocal(t.prob[0][:], t.den[:])
    dve.drain()
    dve.tensor_tensor(t.prob[1][:], t.exp[:], t.prob[0][:], ALU.mult)
    dve.drain()


class TopTwo:

    def __init__(self, sb):
        self.logits = sb("logits", [S, B, NE])
        self.top = sb("top", [S, B, 8])
        self.which = sb("which", [S, B, 8], U32)
        self.whichf = sb("whichf", [S, B, 2])
        self.gap = sb("gap", [S, B, 1])
        self.exp = sb("exp", [S, B, 1])
        self.den = sb("den", [S, B, 1])
        self.prob = [sb(f"prob{k}", [S, B, 1]) for k in range(2)]
        self.hot = [sb(f"hot{k}", [S, B, NE]) for k in range(2)]
        self.iota = sb("iota", [S, B, NE])


@sublayer
def moe(net, name, F, biases=False):
    nc, dram = net.nc, net.dram
    FC = F // P
    NEX = NE + 1
    SLOTS = 3
    ROUNDS = NEX // SLOTS
    HALF = B * S // 2
    UNITS = 2 * FC
    LAG = 4 if SLOTS * UNITS % 4 == 0 else 2
    with ExitStack() as ctx:
        def sb(n, shape, dt=F32):
            return ctx.enter_context(nc.sbuf_tensor(name + "_" + n, shape, dt))

        w1 = sb("w1", [P, SLOTS, KC, F])
        w2 = sb("w2", [P, SLOTS, FC, E])
        wr = sb("wr", [P, KC, NE])
        t = TopTwo(sb)
        pairs = [(wr[:], dram[name + "_wr"]), (t.iota[:], dram["iota8"])]
        if biases:
            b1 = sb("b1", [P, SLOTS, FC])
            b2 = sb("b2", [NEX, E])
            br = sb("br", [S, NE])
            pairs += [(b2[:], dram[name + "_b2"]), (br[:], dram[name + "_br"].partition_broadcast(S))]
            combine_t = sb("combine_t", [NEX, B, S])
        else:
            relu = sb("relu", [P, HALF])
        n_loaded = 16 * len(pairs)
        per_expert = 48 if biases else 32
        xn = sb("xn", [S, 2, E])
        xt = sb("xt", [P, KC, B * S])
        combine = sb("combine", [S, NEX, B])
        part = sb("part", [S, B, NE])
        weight = sb("weight", [S, B])
        credit = sb("credit", [1, 1])
        hidden = sb("hidden", [P, FC, B * S])
        sem = {n: net.sem(name + "_" + n) for n in (
            "loaded", "w0", "w1", "w2", "var_ready", "std_ready", "xn_ready", "xt_psum", "xt_ready", "l_psum",
            "gap_ready", "exp_ready", "combine_ready", "ct_psum", "ct_ready", "h_psum", "h_ready", "y_psum", "y_added")}
        wide, turned, summed = net.wide, net.turned, net.summed
        w_loaded = [sem[f"w{i}"] for i in range(SLOTS)]

        with nc.Block() as block:
            @block.sync
            def _(sp):
                load_weights(sp, net, pairs, sem["loaded"])

                def load_expert(e, slot):
                    sp.dma_start(w1[:, slot], dram[name + "_w1"][e]).then_inc(w_loaded[slot], 16)
                    sp.dma_start(w2[:, slot], dram[name + "_w2"][e]).then_inc(w_loaded[slot], 16)
                    if biases:
                        sp.dma_start(b1[:, slot], dram[name + "_b1"][e]).then_inc(w_loaded[slot], 16)

                for slot in range(SLOTS):
                    load_expert(slot, slot)
                with sp.Fori(1, ROUNDS) as r:
                    for slot in range(SLOTS):
                        sp.wait_ge(sem["y_psum"], (SLOTS * r + slot - 2) * B)
                        load_expert(SLOTS * r + slot, slot)

            @block.tensor
            def _(pe):
                pe.wait_ge(sem["loaded"], n_loaded)
                for b in range(B):
                    pe.wait_ge(sem["xn_ready"], b + 1)
                    if b >= 2:
                        pe.wait_ge(sem["xt_ready"], b - 1)
                    for k in range(KC):
                        last = pe.transpose(turned[:, b % 2, k * S:(k + 1) * S], xn[:, b % 2, k * P:(k + 1) * P], net.ident[0:S, 0:S])
                    last.then_inc(sem["xt_psum"], 1)
                for b in range(B):
                    pe.wait_ge(sem["xt_ready"], b + 1)
                    for k in range(KC):
                        last = pe.matmul(summed[0:S, 0, b * NE:(b + 1) * NE], xt[:, k, b * S:(b + 1) * S], wr[:, k, :],
                                         start=k == 0, stop=k == KC - 1)
                last.then_inc(sem["l_psum"], 1)
                if biases:
                    pe.wait_ge(sem["combine_ready"], 1)
                    for b in range(B):
                        last = pe.transpose(turned[0:NEX, b // 4, (b % 4) * S:(b % 4 + 1) * S], combine[:, :, b], net.ident[0:S, 0:S])
                    last.then_inc(sem["ct_psum"], 1)
                with pe.Fori(0, ROUNDS) as r:
                    for slot in range(SLOTS):
                        e = SLOTS * r + slot
                        pe.wait_ge(w_loaded[slot], per_expert * (r + 1))
                        for f in range(FC):
                            for half in range(2):
                                u = 2 * f + half
                                pe.wait_ge(sem["h_ready"], e * UNITS + u + 1)
                                for k in range(KC):
                                    last = pe.matmul(wide[:, (slot * UNITS + u) % 4, 0:HALF], w1[:, slot, k, f * P:(f + 1) * P],
                                                     xt[:, k, half * HALF:(half + 1) * HALF], start=k == 0, stop=k == KC - 1)
                                last.then_inc(sem["h_psum"], 1)
                        pe.wait_ge(sem["h_ready"], LAG + (e + 1) * UNITS)
                        for b in range(B):
                            pe.wait_ge(sem["y_added"], e * B + b + 1)
                            for f in range(FC):
                                last = pe.matmul(summed[0:S, b % 2, 0:E], hidden[:, f, b * S:(b + 1) * S], w2[:, slot, f, :],
                                                 start=f == 0, stop=f == FC - 1)
                            last.then_inc(sem["y_psum"], 1)
                if biases:
                    pe.wait_ge(sem["ct_ready"], 1)
                    for b in range(B):
                        pe.wait_ge(sem["y_added"], NEX * B + b + 1)
                        pe.matmul(summed[0:S, b % 2, 0:E], combine_t[:, b, :], b2[:], start=True, stop=True).then_inc(sem["y_psum"], 1)

            @block.scalar
            def _(act):
                norm_stats_scalar(act, net, sem["var_ready"], sem["std_ready"])
                for b in range(B):
                    act.wait_ge(sem["xt_psum"], b + 1)
                    act.activation(xt[:, :, b * S:(b + 1) * S], turned[:, b % 2, 0:KC * S].rearrange("p (k s) -> p k s", k=KC),
                                   ACT.Copy).then_inc(sem["xt_ready"], 1)
                act.wait_ge(sem["gap_ready"], 1)
                act.activation(t.exp[:], t.gap[:], ACT.Exp).then_inc(sem["exp_ready"], 1)
                act.drain()
                if biases:
                    act.wait_ge(sem["ct_psum"], 1)
                    act.activation(combine_t[:].rearrange("e (a b) s -> e a (b s)", a=2), turned[0:NEX, :, 0:4 * S], ACT.Copy).then_inc(sem["ct_ready"], 1)
                act.activation(credit[:], t.exp[0:1, 0, :], ACT.Copy).then_inc(sem["h_ready"], LAG)
                with act.Fori(0, ROUNDS) as r:
                    for slot in range(SLOTS):
                        e = SLOTS * r + slot
                        if biases:
                            act.wait_ge(w_loaded[slot], per_expert * (r + 1))
                        for f in range(FC):
                            for half in range(2):
                                u = 2 * f + half
                                act.wait_ge(sem["h_psum"], e * UNITS + u + 1)
                                src = wide[:, (slot * UNITS + u) % 4, 0:HALF]
                                dst = hidden[:, f, half * HALF:(half + 1) * HALF]
                                if biases:
                                    act.activation(dst, src, ACT.Gelu, bias=b1[:, slot, f:f + 1]).then_inc(sem["h_ready"], 1)
                                else:
                                    act.activation(relu[:], src, ACT.Relu)
                                    act.drain()
                                    act.activation(dst, relu[:], ACT.Square).then_inc(sem["h_ready"], 1)
                                    act.drain()

            @block.vector
            def _(dve):
                norm_stats_vector(dve, net, sem["var_ready"], sem["std_ready"])
                for b in range(B):
                    if b >= 2:
                        dve.wait_ge(sem["xt_psum"], b - 1)
                    normalise(dve, net, xn[:, b % 2, :], b).then_inc(sem["xn_ready"], 1)
                dve.wait_ge(sem["loaded"], n_loaded)
                dve.wait_ge(sem["l_psum"], 1)
                logits = summed[0:S, 0, 0:B * NE].rearrange("s (b e) -> s b e", b=B)
                if biases:
                    dve.tensor_tensor(t.logits[:], logits, br[:].unsqueeze(1).broadcast_to([S, B, NE]), ALU.add)
                else:
                    dve.tensor_copy(t.logits[:], logits)
                dve.drain()
                top_two_vector(dve, net, t, sem["gap_ready"], sem["exp_ready"])
                if not biases:
                    for k in range(2):
                        dve.tensor_scalar(t.prob[k][:], t.prob[k][:], 1.0, None, ALU.is_ge)
                    dve.drain()
                dve.tensor_tensor(part[:], t.hot[0][:], t.prob[0][:].broadcast_to([S, B, NE]), ALU.mult)
                dve.tensor_tensor(t.hot[1][:], t.hot[1][:], t.prob[1][:].broadcast_to([S, B, NE]), ALU.mult)
                dve.memset(combine[:, NE:NEX, :], 1.0)
                dve.drain()
                dve.tensor_tensor(combine[:, 0:NE, :].rearrange("s e b -> s b e"), part[:], t.hot[1][:], ALU.add).then_inc(sem["combine_ready"], 1)
                dve.drain()
                dve.memset(part[0:1, 0, 0:1], 0.0).then_inc(sem["y_added"], 2)
                dve.drain()

                def add(b, e, scale):
                    dve.wait_ge(sem["y_psum"], e * B + b + 1)
                    dve.scalar_tensor_tensor(out=net.x[:, b, :], in0=summed[0:S, b % 2, 0:E], scalar=scale,
                                             in1=net.x[:, b, :], op0=ALU.mult, op1=ALU.add).then_inc(sem["y_added"], 1)

                with dve.Fori(0, NEX) as e:
                    dve.tensor_copy(weight[:], combine[:, e, :])
                    dve.drain()
                    for b in range(B):
                        add(b, e, weight[:, b:b + 1])
                    dve.drain()
                if biases:
                    for b in range(B):
                        add(b, NEX, 1.0)
                    dve.drain()


@sublayer
def l1_attn(net):
    nc, dram = net.nc, net.dram
    H, D, G = 16, 16, 4
    HP, NG = P // D, H // G
    with ExitStack() as ctx:
        def sb(n, shape, dt=F32):
            return ctx.enter_context(nc.sbuf_tensor("l1a_" + n, shape, dt))

        wqk, wv, wo = sb("wqk", [P, KC, 2 * E]), sb("wv", [P, KC, E]), sb("wo", [P, KC, E])
        bqk, bv, bo = sb("bqk", [S, 2 * E]), sb("bv", [S, E]), sb("bo", [S, E])
        headmask = sb("headmask", [P, HP])
        pairs = [(wqk[:], dram["l1a_wqk"]), (wv[:], dram["l1a_wv"]), (wo[:], dram["l1a_wo"]), (headmask[:], dram["headmask16"]),
                 (bqk[:], dram["l1a_bqk"].partition_broadcast(S)), (bv[:], dram["l1a_bv"].partition_broadcast(S)),
                 (bo[:], dram["l1a_bo"].partition_broadcast(S))]
        n_loaded = 16 * len(pairs)
        xn = sb("xn", [S, 2, E])
        xt = sb("xt", [P, KC, B, S])
        qk = sb("qk", [S, B, 2 * E])
        sq = sb("sq", [S, B, 2 * E])
        unit = sb("unit", [S, 2 * E])
        norm = sb("norm", [S, B, 2 * H])
        qkt = sb("qkt", [P, 2 * KC, S])
        km = sb("km", [P, KC, HP, S])
        v1 = sb("v1", [S, B, H, D + 1])
        shift = sb("shift", [S, 1])
        num, den, wt = sb("num", [S, H, S]), sb("den", [S, H, S]), sb("wt", [S, H, S])
        rs = sb("rs", [S, H])
        y = sb("y", [S, H, D])
        yt = sb("yt", [P, KC, S])
        delta = sb("delta", [S, E])
        sem = {n: net.sem("l1a_" + n) for n in (
            "loaded", "var_ready", "std_ready", "xn_ready", "xt_psum", "xt_ready", "qkv_psum", "qkv_ready", "sq_ready", "sum_ready",
            "root_ready", "qk_ready", "qkt_psum", "qkt_ready", "heads_ready", "cos_psum", "den_ready", "wt_ready", "y_psum", "y_ready",
            "yt_psum", "yt_ready", "out_psum")}
        wide, turned, summed = net.wide, net.turned, net.summed

        def in_order(engine, step):
            step(0)
            with engine.Fori(1, B - 1) as b:
                step(b)
            step(B - 1)

        with nc.Block() as block:
            @block.sync
            def _(sp):
                load_weights(sp, net, pairs, sem["loaded"])

            @block.tensor
            def _(pe):
                def turn_x(b, slot, first):
                    pe.wait_ge(sem["xn_ready"], b + 1)
                    if not first:
                        pe.wait_ge(sem["xt_ready"], b - 1)
                    for k in range(KC):
                        last = pe.transpose(turned[:, slot, k * S:(k + 1) * S], xn[:, slot, k * P:(k + 1) * P], net.ident[0:S, 0:S])
                    last.then_inc(sem["xt_psum"], 1)

                by_pairs(pe, B, turn_x)
                pe.wait_ge(sem["loaded"], n_loaded)
                for b in range(B):
                    pe.wait_ge(sem["xt_ready"], b + 1)
                    if b >= 2:
                        pe.wait_ge(sem["qkv_ready"], b - 1)
                    for w, out in ((wqk, wide[0:S, b % 2, :]), (wv, wide[0:S, 2 + b % 2, 0:E])):
                        for k in range(KC):
                            last = pe.matmul(out, xt[:, k, b, :], w[:, k, :], start=k == 0, stop=k == KC - 1)
                    last.then_inc(sem["qkv_psum"], 1)

                def turn_qk(b):
                    pe.wait_ge(sem["qk_ready"], b + 1)
                    for c in range(2 * KC):
                        last = pe.transpose(turned[:, 0, c * S:(c + 1) * S],
                                            unit[:, c * P:(c + 1) * P], net.ident[0:S, 0:S])
                    last.then_inc(sem["qkt_psum"], 1)

                def cosines(b):
                    pe.wait_ge(sem["heads_ready"], b + 1)
                    for g in range(NG):
                        for j in range(G):
                            h = g * G + j
                            last = pe.matmul(wide[0:S, g, j * S:(j + 1) * S], km[:, h // HP, h % HP, :], qkt[:, h // HP, :],
                                             start=True, stop=True)
                        last.then_inc(sem["cos_psum"], 1)

                def weigh(b, g):
                    pe.wait_ge(sem["wt_ready"], b * NG + g + 1)
                    for h in range(g * G, g * G + G):
                        last = pe.matmul(summed[0:S, 0, h * (D + 1):(h + 1) * (D + 1)], wt[:, h, :],
                                         v1[:, bass.ds(b, 1), h, :].rearrange("s o d -> s (o d)"), start=True, stop=True)
                    if g == NG - 1:
                        last.then_inc(sem["y_psum"], 1)

                def turn_y(b):
                    pe.wait_ge(sem["y_ready"], b + 1)
                    for k in range(KC):
                        last = pe.transpose(turned[:, 1, k * S:(k + 1) * S],
                                            y[:].rearrange("s h d -> s (h d)")[:, k * P:(k + 1) * P], net.ident[0:S, 0:S])
                    last.then_inc(sem["yt_psum"], 1)

                def project(b):
                    pe.wait_ge(sem["yt_ready"], b + 1)
                    for k in range(KC):
                        last = pe.matmul(summed[0:S, 1, 0:E], yt[:, k, :], wo[:, k, :], start=k == 0, stop=k == KC - 1)
                    last.then_inc(sem["out_psum"], 1)

                def step(b):
                    is_first, is_last = isinstance(b, int) and b == 0, isinstance(b, int) and b == B - 1
                    if not is_first:
                        turn_y(b - 1)
                    weigh(b, 0)
                    weigh(b, 1)
                    if not is_last:
                        turn_qk(b + 1)
                    weigh(b, 2)
                    if not is_first:
                        project(b - 1)
                    weigh(b, 3)
                    if not is_last:
                        cosines(b + 1)

                turn_qk(0)
                cosines(0)
                in_order(pe, step)
                turn_y(B - 1)
                project(B - 1)

            @block.scalar
            def _(act):
                norm_stats_scalar(act, net, sem["var_ready"], sem["std_ready"])

                def copy_xt(b, slot, first):
                    act.wait_ge(sem["xt_psum"], b + 1)
                    act.activation(xt[:, :, bass.ds(b, 1), :].rearrange("p k o s -> p k (o s)"),
                                   turned[:, slot, 0:KC * S].rearrange("p (k s) -> p k s", k=KC), ACT.Copy).then_inc(sem["xt_ready"], 1)

                by_pairs(act, B, copy_xt)
                with act.Fori(0, B) as b:
                    act.wait_ge(sem["qkv_ready"], b + 1)
                    act.activation(sq[:, b, :], qk[:, b, :], ACT.Square).then_inc(sem["sq_ready"], 1)
                act.wait_ge(sem["sum_ready"], 1)
                act.activation(norm[:], norm[:], ACT.Sqrt).then_inc(sem["root_ready"], 1)

                def copy_qkt(b):
                    act.wait_ge(sem["qkt_psum"], b + 1)
                    act.activation(qkt[:], turned[:, 0, 0:2 * KC * S].rearrange("p (k s) -> p k s", k=2 * KC), ACT.Copy).then_inc(sem["qkt_ready"], 1)

                def scores(b):
                    for g in range(NG):
                        got = wide[0:S, g, 0:G * S].rearrange("s (j t) -> s j t", j=G)
                        one = den[:, g * G:(g + 1) * G, :]
                        act.wait_ge(sem["cos_psum"], b * NG + g + 1)
                        act.activation(one, got, ACT.Ln, bias=shift[:], scale=-1.0)
                    act.drain()
                    for g in range(NG):
                        got = wide[0:S, g, 0:G * S].rearrange("s (j t) -> s j t", j=G)
                        one = den[:, g * G:(g + 1) * G, :]
                        act.activation(num[:, g * G:(g + 1) * G, :], got, ACT.Square, bias=1.0)
                        act.activation(one, one, ACT.Exp, scale=-1.0).then_inc(sem["den_ready"], 1)

                def copy_yt(b):
                    act.wait_ge(sem["yt_psum"], b + 1)
                    act.activation(yt[:], turned[:, 1, 0:KC * S].rearrange("p (k s) -> p k s", k=KC), ACT.Copy).then_inc(sem["yt_ready"], 1)

                def step(b):
                    if not (isinstance(b, int) and b == 0):
                        copy_yt(b - 1)
                    if not (isinstance(b, int) and b == B - 1):
                        copy_qkt(b + 1)
                    if not (isinstance(b, int) and b == B - 1):
                        scores(b + 1)

                copy_qkt(0)
                scores(0)
                in_order(act, step)
                copy_yt(B - 1)

            @block.gpsimd
            def _(pool):
                pool.wait_ge(sem["loaded"], n_loaded)
                with pool.Fori(0, B) as b:
                    pool.wait_ge(sem["qkt_ready"], b + 1)
                    for m in range(KC):
                        last = pool.tensor_tensor(km[:, m], qkt[:, KC + m, :].unsqueeze(1).broadcast_to([P, HP, S]),
                                                  headmask[:].unsqueeze(2).broadcast_to([P, HP, S]), ALU.mult)
                    last.then_inc(sem["heads_ready"], 1)

            @block.vector
            def _(dve):
                dve.memset(v1[:, :, :, D:D + 1], 1.0)
                dve.memset(shift[:], 1.1)
                norm_stats_vector(dve, net, sem["var_ready"], sem["std_ready"])

                def normal(b, slot, first):
                    if not first:
                        dve.wait_ge(sem["xt_psum"], b - 1)
                    normalise(dve, net, xn[:, slot, :], b).then_inc(sem["xn_ready"], 1)

                def take(b, slot, first):
                    dve.wait_ge(sem["qkv_psum"], b + 1)
                    dve.tensor_tensor(qk[:, bass.ds(b, 1), :].rearrange("s o n -> s (o n)"), wide[0:S, slot, :], bqk[:], ALU.add)
                    dve.tensor_tensor(v1[:, bass.ds(b, 1), :, 0:D].rearrange("s o h d -> s (o h) d"),
                                      wide[0:S, 2 + slot, 0:E].rearrange("s (h d) -> s h d", h=H),
                                      bv[:].rearrange("s (h d) -> s h d", h=H), ALU.add).then_inc(sem["qkv_ready"], 1)

                by_pairs(dve, B, normal)
                dve.wait_ge(sem["loaded"], n_loaded)
                by_pairs(dve, B, take)
                with dve.Fori(0, B) as b:
                    dve.wait_ge(sem["sq_ready"], b + 1)
                    last = dve.tensor_reduce(norm[:, b, :], sq[:, b, :].rearrange("s (h d) -> s h d", d=D), X_AX, ALU.add)
                dve.drain()
                dve.memset(delta[0:1, 0:1], 0.0).then_inc(sem["sum_ready"], 1)
                dve.wait_ge(sem["root_ready"], 1)
                dve.tensor_scalar(norm[:], norm[:], 1e-8, None, ALU.add)
                dve.drain()
                dve.reciprocal(norm[:], norm[:])
                dve.drain()

                def shorten(b):
                    if not (isinstance(b, int) and b == 0):
                        dve.wait_ge(sem["qkt_psum"], b)
                    dve.tensor_tensor(unit[:].rearrange("s (h d) -> s h d", d=D), qk[:, bass.ds(b, 1), :].rearrange("s o (h d) -> s (o h) d", d=D),
                                      norm[:, bass.ds(b, 1), :].rearrange("s o h -> s (o h)").unsqueeze(2).broadcast_to([S, 2 * H, D]),
                                      ALU.mult).then_inc(sem["qk_ready"], 1)

                def weights(b):
                    for g in range(NG):
                        dve.wait_ge(sem["den_ready"], b * NG + g + 1)
                        dve.tensor_tensor(wt[:, g * G:(g + 1) * G, :], den[:, g * G:(g + 1) * G, :], num[:, g * G:(g + 1) * G, :],
                                          ALU.mult).then_inc(sem["wt_ready"], 1)

                def divide(b):
                    dve.wait_ge(sem["y_psum"], b + 1)
                    got = summed[0:S, 0, 0:H * (D + 1)].rearrange("s (h d) -> s h d", h=H)
                    dve.tensor_scalar(rs[:].unsqueeze(2), got[:, :, D:D + 1], 1e-6, None, ALU.add)
                    dve.drain()
                    dve.reciprocal(rs[:], rs[:])
                    dve.drain()
                    dve.tensor_tensor(y[:], got[:, :, 0:D], rs[:].unsqueeze(2).broadcast_to([S, H, D]), ALU.mult).then_inc(sem["y_ready"], 1)

                def add(b):
                    dve.wait_ge(sem["out_psum"], b + 1)
                    dve.tensor_tensor(delta[:], summed[0:S, 1, 0:E], bo[:], ALU.add)
                    dve.drain()
                    dve.tensor_tensor(net.x[:, b, :], net.x[:, b, :], delta[:], ALU.add)
                    dve.drain()

                def step(b):
                    if not (isinstance(b, int) and b == B - 1):
                        shorten(b + 1)
                    if not (isinstance(b, int) and b == 0):
                        add(b - 1)
                    divide(b)
                    if not (isinstance(b, int) and b == B - 1):
                        weights(b + 1)

                shorten(0)
                weights(0)
                in_order(dve, step)
                add(B - 1)


@sublayer
def l2_attn(net):
    nc, dram = net.nc, net.dram
    N = 2
    with ExitStack() as ctx:
        def sb(n, shape, dt=F32):
            return ctx.enter_context(nc.sbuf_tensor("l2a_" + n, shape, dt))

        par = {n: sb(n, [P, KC, N]) for n in ("delta", "alpha", "beta", "gamma")}
        omega = sb("omega", [P, KC])
        pairs = [(par[n][:], dram["l2a_" + n]) for n in par] + [(omega[:], dram["l2a_omega"])]
        n_loaded = 16 * len(pairs)
        p_, a_ = sb("p", [P, KC, N]), sb("a", [P, KC, N])
        q_, c_ = sb("q", [P, KC, N]), sb("c", [P, KC, N])
        keep = sb("keep", [P, B, S])
        decay = sb("decay", [P, KC * N, B * S])
        fed = sb("fed", [P, KC * N, B * S])
        avg = sb("avg", [P, KC * N, B * S])
        xn = sb("xn", [S, 2, E])
        xt = sb("xt", [P, KC, B * S])
        z = sb("z", [P, KC, B * S])
        sem = {n: net.sem("l2a_" + n) for n in (
            "loaded", "var_ready", "std_ready", "xn_ready", "xt_psum", "xt_ready", "gates_ready", "z_ready", "silu_ready", "zt_psum", "zt_added")}
        turned, summed = net.turned, net.summed

        with nc.Block() as block:
            @block.sync
            def _(sp):
                load_weights(sp, net, pairs, sem["loaded"])

            @block.tensor
            def _(pe):
                for b in range(B):
                    pe.wait_ge(sem["xn_ready"], b + 1)
                    if b >= 2:
                        pe.wait_ge(sem["xt_ready"], b - 1)
                    for k in range(KC):
                        last = pe.transpose(turned[:, b % 2, k * S:(k + 1) * S], xn[:, b % 2, k * P:(k + 1) * P], net.ident[0:S, 0:S])
                    last.then_inc(sem["xt_psum"], 1)
                pe.wait_ge(sem["silu_ready"], KC)
                for b in range(B):
                    if b >= 2:
                        pe.wait_ge(sem["zt_added"], b - 1)
                    for k in range(KC):
                        last = pe.transpose(summed[0:S, b % 2, k * P:(k + 1) * P], z[:, k, b * S:(b + 1) * S], net.ident[:])
                    last.then_inc(sem["zt_psum"], 1)

            @block.scalar
            def _(act):
                norm_stats_scalar(act, net, sem["var_ready"], sem["std_ready"])
                for b in range(B):
                    act.wait_ge(sem["xt_psum"], b + 1)
                    act.activation(xt[:, :, b * S:(b + 1) * S], turned[:, b % 2, 0:KC * S].rearrange("p (k s) -> p k s", k=KC),
                                   ACT.Copy).then_inc(sem["xt_ready"], 1)
                act.wait_ge(sem["loaded"], n_loaded)
                act.activation(p_[:], par["delta"][:], ACT.Sigmoid)
                act.activation(a_[:], par["alpha"][:], ACT.Sigmoid).then_inc(sem["gates_ready"], 1)
                for k in range(KC):
                    act.wait_ge(sem["z_ready"], k + 1)
                    act.activation(z[:, k, :], avg[:, 2 * k, :], ACT.Silu).then_inc(sem["silu_ready"], 1)

            @block.vector
            def _(dve):
                norm_stats_vector(dve, net, sem["var_ready"], sem["std_ready"])
                for b in range(B):
                    if b >= 2:
                        dve.wait_ge(sem["xt_psum"], b - 1)
                    normalise(dve, net, xn[:, b % 2, :], b).then_inc(sem["xn_ready"], 1)
                dve.memset(keep[:], 1.0)
                dve.drain()
                dve.memset(keep[:, :, 0:1], 0.0)
                dve.wait_ge(sem["gates_ready"], 1)
                dve.tensor_tensor(q_[:], p_[:], a_[:], ALU.mult)
                dve.tensor_tensor(c_[:], p_[:], par["beta"][:], ALU.mult)
                dve.drain()
                dve.tensor_scalar(q_[:], q_[:], -1.0, 1.0, ALU.mult, ALU.add)
                dve.tensor_tensor(c_[:], c_[:], par["gamma"][:], ALU.mult)
                dve.drain()
                dve.tensor_scalar(c_[:], c_[:], float(np.sqrt(1.0 / N)), None, ALU.mult)
                dve.drain()
                for k in range(KC):
                    for n in range(N):
                        dve.tensor_scalar(decay[:, k * N + n, :], keep[:].rearrange("p b s -> p (b s)"), q_[:, k, n:n + 1], None, ALU.mult)
                dve.wait_ge(sem["xt_ready"], B)
                for k in range(KC):
                    for n in range(N):
                        dve.tensor_scalar(fed[:, k * N + n, :], xt[:, k, :], c_[:, k, n:n + 1], None, ALU.mult)
                dve.drain()
                for k in range(KC):
                    for n in range(N):
                        j = k * N + n
                        dve.tensor_tensor_scan(avg[:, j, :], decay[:, j, :], fed[:, j, :], 0.0, ALU.mult, ALU.add)
                    dve.drain()
                    dve.tensor_tensor(avg[:, k * N, :], avg[:, k * N, :], avg[:, k * N + 1, :], ALU.add)
                    dve.drain()
                    dve.scalar_tensor_tensor(out=avg[:, k * N, :], in0=xt[:, k, :], scalar=omega[:, k:k + 1],
                                             in1=avg[:, k * N, :], op0=ALU.mult, op1=ALU.add).then_inc(sem["z_ready"], 1)
                for b in range(B):
                    dve.wait_ge(sem["zt_psum"], b + 1)
                    dve.tensor_tensor(net.x[:, b, :], net.x[:, b, :], summed[0:S, b % 2, 0:E], ALU.add).then_inc(sem["zt_added"], 1)
                dve.drain()


@sublayer
def l2_ffn(net):
    nc, dram = net.nc, net.dram
    F = 1024
    FC = F // P
    TOP = 2
    ROWS = B * S * TOP
    RT = ROWS // NE // S
    CR = RT * S
    SLOTS = 2
    with ExitStack() as ctx:
        def sb(n, shape, dt=F32):
            return ctx.enter_context(nc.sbuf_tensor("l2f_" + n, shape, dt))

        w1 = sb("w1", [P, SLOTS, KC, F])
        w2 = sb("w2", [P, SLOTS, FC, E])
        wr = sb("wr", [P, KC, NE])
        before, ones = sb("before", [S, S]), sb("ones", [S, S])
        t = TopTwo(sb)
        pairs = [(wr[:], dram["l2f_wr"]), (t.iota[:], dram["iota8"]), (before[:], dram["before"])]
        n_loaded = 16 * len(pairs)
        xn = sb("xn", [S, B, E])
        xt = sb("xt", [P, KC, 2, S])
        both = sb("both", [S, B, NE])
        total = sb("total", [S, B, NE])
        start = sb("start", [S, B + 1, NE])
        base = sb("base", [S, NE])
        rank = sb("rank", [S, B, NE])
        mine = sb("mine", [S, B, NE])
        place = sb("place", [S, TOP, B])
        placei = sb("placei", [S, TOP * B], U32)
        rows = sb("rows", [S, SLOTS, RT, E])
        rt = sb("rt", [P, KC, CR])
        hidden = sb("hidden", [P, FC, CR])
        out = sb("out", [S, SLOTS, RT, E])
        back = sb("back", [S, TOP * B, E])
        sorted_x = nc.dram_tensor("sorted_x", (ROWS, E), F32).ap()
        sorted_y = nc.dram_tensor("sorted_y", (ROWS, E), F32).ap()
        sem = {n: net.sem("l2f_" + n) for n in (
            "loaded", "w0", "w1", "r0", "r1", "var_ready", "std_ready", "xn_ready", "xt_psum", "xt_ready", "l_psum", "gap_ready",
            "exp_ready", "both_ready", "count_psum", "place_ready", "scattered", "rt_psum", "rt_ready", "h_psum", "h_ready",
            "y_psum", "y_ready", "stored0", "stored1", "gathered")}
        wide, turned, summed = net.wide, net.turned, net.summed
        w_loaded, r_loaded = (sem["w0"], sem["w1"]), (sem["r0"], sem["r1"])
        stored = (sem["stored0"], sem["stored1"])

        with nc.Block() as block:
            @block.sync
            def _(sp):
                load_weights(sp, net, pairs, sem["loaded"])

                def load_expert(e, slot):
                    sp.dma_start(w1[:, slot], dram["l2f_w1"][e]).then_inc(w_loaded[slot], 16)
                    sp.dma_start(w2[:, slot], dram["l2f_w2"][e]).then_inc(w_loaded[slot], 16)

                def load_rows(e, slot):
                    sp.dma_start(rows[:, slot], sorted_x.rearrange("(e r s) d -> e s r d", r=RT, s=S)[e]).then_inc(r_loaded[slot], 16)

                for slot in range(SLOTS):
                    load_expert(slot, slot)
                sp.wait_ge(sem["scattered"], 16 * TOP * B)
                for slot in range(SLOTS):
                    load_rows(slot, slot)
                with sp.Fori(1, NE // SLOTS) as r:
                    for slot in range(SLOTS):
                        sp.wait_ge(sem["y_psum"], SLOTS * r + slot - 1)
                        load_expert(SLOTS * r + slot, slot)
                        load_rows(SLOTS * r + slot, slot)

            @block.gpsimd
            def _(pool):
                pool.wait_ge(sem["place_ready"], 1)
                for b in range(B):
                    for k in range(TOP):
                        pool.indirect_dma_start(out=sorted_x, out_offset=bass.IndirectOffsetOnAxis(ap=placei[:, k * B + b:k * B + b + 1], axis=0),
                                                in_=xn[:, b, :], in_offset=None).then_inc(sem["scattered"], 16)
                for slot in range(SLOTS):
                    pool.wait_ge(stored[slot], 16 * NE // SLOTS)
                for b in range(B):
                    for k in range(TOP):
                        pool.indirect_dma_start(out=back[:, k * B + b, :], out_offset=None, in_=sorted_y,
                                                in_offset=bass.IndirectOffsetOnAxis(ap=placei[:, k * B + b:k * B + b + 1], axis=0)
                                                ).then_inc(sem["gathered"], 16)

            @block.tensor
            def _(pe):
                pe.wait_ge(sem["loaded"], n_loaded)
                for b in range(B):
                    pe.wait_ge(sem["xn_ready"], b + 1)
                    if b >= 2:
                        pe.wait_ge(sem["xt_ready"], b - 1)
                    for k in range(KC):
                        last = pe.transpose(turned[:, b % 2, k * S:(k + 1) * S], xn[:, b, k * P:(k + 1) * P], net.ident[0:S, 0:S])
                    last.then_inc(sem["xt_psum"], 1)
                    pe.wait_ge(sem["xt_ready"], b + 1)
                    for k in range(KC):
                        last = pe.matmul(summed[0:S, 0, b * NE:(b + 1) * NE], xt[:, k, b % 2, :], wr[:, k, :], start=k == 0, stop=k == KC - 1)
                last.then_inc(sem["l_psum"], 1)
                pe.wait_ge(sem["both_ready"], 1)
                chosen = both[:].rearrange("s b e -> s (b e)")
                pe.matmul(summed[0:S, 1, 0:B * NE], before[:], chosen, start=True, stop=True)
                pe.matmul(summed[0:S, 1, B * NE:2 * B * NE], ones[:], chosen, start=True, stop=True).then_inc(sem["count_psum"], 1)
                with pe.Fori(0, NE // SLOTS) as r:
                    for slot in range(SLOTS):
                        e = SLOTS * r + slot
                        pe.wait_ge(r_loaded[slot], 16 * (r + 1))
                        for c in range(RT):
                            for k in range(KC):
                                last = pe.transpose(turned[:, c, k * S:(k + 1) * S], rows[:, slot, c, k * P:(k + 1) * P], net.ident[0:S, 0:S])
                        last.then_inc(sem["rt_psum"], 1)
                        pe.wait_ge(sem["rt_ready"], e + 1)
                        pe.wait_ge(w_loaded[slot], 32 * (r + 1))
                        for f in range(FC):
                            if f >= 4:
                                pe.wait_ge(sem["h_ready"], e * FC + f - 3)
                            for k in range(KC):
                                last = pe.matmul(wide[:, f % 4, 0:CR], w1[:, slot, k, f * P:(f + 1) * P], rt[:, k, :], start=k == 0, stop=k == KC - 1)
                            last.then_inc(sem["h_psum"], 1)
                        pe.wait_ge(sem["h_ready"], e * FC + FC)
                        for c in range(RT):
                            for f in range(FC):
                                last = pe.matmul(summed[0:S, c, 0:E], hidden[:, f, c * S:(c + 1) * S], w2[:, slot, f, :], start=f == 0, stop=f == FC - 1)
                        last.then_inc(sem["y_psum"], 1)

            @block.scalar
            def _(act):
                norm_stats_scalar(act, net, sem["var_ready"], sem["std_ready"])
                for b in range(B):
                    act.wait_ge(sem["xt_psum"], b + 1)
                    act.activation(xt[:, :, b % 2, :], turned[:, b % 2, 0:KC * S].rearrange("p (k s) -> p k s", k=KC), ACT.Copy).then_inc(sem["xt_ready"], 1)
                act.wait_ge(sem["gap_ready"], 1)
                act.activation(t.exp[:], t.gap[:], ACT.Exp).then_inc(sem["exp_ready"], 1)
                with act.Fori(0, NE // SLOTS) as r:
                    for slot in range(SLOTS):
                        e = SLOTS * r + slot
                        act.wait_ge(sem["rt_psum"], e + 1)
                        act.activation(rt[:].rearrange("p k (c s) -> p c k s", c=RT), turned[:, :, 0:KC * S].rearrange("p c (k s) -> p c k s", k=KC),
                                       ACT.Copy).then_inc(sem["rt_ready"], 1)
                        for f in range(FC):
                            act.wait_ge(sem["h_psum"], e * FC + f + 1)
                            act.activation(hidden[:, f, :], wide[:, f % 4, 0:CR], ACT.Gelu).then_inc(sem["h_ready"], 1)
                        act.wait_ge(sem["y_ready"], e + 1)
                        act.dma_start(sorted_y.rearrange("(e r s) d -> e s r d", r=RT, s=S)[e], out[:, slot]).then_inc(stored[slot], 16)

            @block.vector
            def _(dve):
                dve.memset(ones[:], 1.0)
                dve.memset(start[:, 0, :], 0.0)
                dve.memset(base[:, 0:1], 0.0)
                norm_stats_vector(dve, net, sem["var_ready"], sem["std_ready"])
                with dve.Fori(0, B) as b:
                    normalise(dve, net, xn[:, b, :], b).then_inc(sem["xn_ready"], 1)
                dve.wait_ge(sem["loaded"], n_loaded)
                dve.wait_ge(sem["l_psum"], 1)
                dve.tensor_copy(t.logits[:], summed[0:S, 0, 0:B * NE].rearrange("s (b e) -> s b e", b=B))
                dve.drain()
                top_two_vector(dve, net, t, sem["gap_ready"], sem["exp_ready"])
                dve.tensor_tensor(both[:], t.hot[0][:], t.hot[1][:], ALU.add).then_inc(sem["both_ready"], 1)
                dve.wait_ge(sem["count_psum"], 1)
                dve.tensor_copy(total[:], summed[0:S, 1, B * NE:2 * B * NE].rearrange("s (b e) -> s b e", b=B))
                dve.drain()
                for b in range(B):
                    dve.tensor_tensor(start[:, b + 1, :], start[:, b, :], total[:, b, :], ALU.add)
                    dve.drain()
                for e in range(NE - 1):
                    dve.tensor_tensor(base[:, e + 1:e + 2], base[:, e:e + 1], start[:, B, e:e + 1], ALU.add)
                    dve.drain()
                dve.tensor_tensor(rank[:], start[:, 0:B, :], summed[0:S, 1, 0:B * NE].rearrange("s (b e) -> s b e", b=B), ALU.add)
                dve.drain()
                dve.tensor_tensor(rank[:], rank[:], base[:].unsqueeze(1).broadcast_to([S, B, NE]), ALU.add)
                dve.drain()
                for k in range(TOP):
                    dve.tensor_tensor(mine[:], rank[:], t.hot[k][:], ALU.mult)
                    dve.drain()
                    dve.tensor_reduce(place[:, k, :], mine[:], X_AX, ALU.add)
                    dve.drain()
                dve.tensor_copy(placei[:], place[:].rearrange("s k b -> s (k b)")).then_inc(sem["place_ready"], 1)
                for slot in range(SLOTS):
                    dve.wait_ge(sem["y_psum"], slot + 1)
                    dve.tensor_copy(out[:, slot], summed[0:S, :, 0:E]).then_inc(sem["y_ready"], 1)
                with dve.Fori(1, NE // SLOTS) as r:
                    for slot in range(SLOTS):
                        dve.wait_ge(stored[slot], 16 * r)
                        dve.wait_ge(sem["y_psum"], SLOTS * r + slot + 1)
                        dve.tensor_copy(out[:, slot], summed[0:S, :, 0:E]).then_inc(sem["y_ready"], 1)
                dve.wait_ge(sem["gathered"], 16 * TOP * B)
                for k in range(TOP):
                    for b in range(B):
                        dve.scalar_tensor_tensor(out=net.x[:, b, :], in0=back[:, k * B + b, :], scalar=t.prob[k][:, b, :],
                                                 in1=net.x[:, b, :], op0=ALU.mult, op1=ALU.add)
                    dve.drain()


@sublayer
def l3_attn(net):
    nc, dram = net.nc, net.dram
    H, D, C, T = 16, 16, 64, B
    HC = H * C
    HALF = HC // 2
    PAIRS = T * (T + 1) // 2
    RING = 4
    TB = 4
    AHEAD = 3

    def pairs_before(t):
        return t * (t + 1) // 2

    def gpsimd_share(n):
        return n // 3

    with ExitStack() as ctx:
        def sb(n, shape, dt=F32):
            return ctx.enter_context(nc.sbuf_tensor("l3a_" + n, shape, dt))

        wqk, wv, wo = sb("wqk", [P, KC, 2 * E]), sb("wv", [P, KC, E]), sb("wo", [P, KC, E])
        bqk, bv, bo = sb("bqk", [S, 2 * E]), sb("bv", [S, E]), sb("bo", [S, E])
        bkt = sb("bkt", [P, KC])
        qc = sb("qc", [P, KC, HC // KC])
        beta = sb("beta", [S, H])
        pairs = [(wqk[:], dram["l3a_wqk"]), (wv[:], dram["l3a_wv"]), (wo[:], dram["l3a_wo"]), (qc[:], dram["l3a_qc"]),
                 (bqk[:], dram["l3a_bqk"].partition_broadcast(S)), (bv[:], dram["l3a_bv"].partition_broadcast(S)),
                 (bkt[:], dram["l3a_bkt"]),
                 (bo[:], dram["l3a_bo"].partition_broadcast(S)), (beta[:], dram["l3a_beta"].partition_broadcast(S))]
        n_loaded = 16 * len(pairs)
        xn = sb("xn", [S, 2, E])
        xt = sb("xt", [P, KC, T, S])
        kt = sb("kt", [P, KC, T, S])
        qk = sb("qk", [S, T, 2 * E])
        ring = qk[:].rearrange("s (a t) n -> s a (t n)", a=RING)
        v = sb("v", [S, T, E])
        cw = sb("cw", [S, T, HC])
        top = sb("top", [S, HC])
        rnorm = sb("rnorm", [S, T, HC])
        prod = sb("prod", [S, T, HC])
        small = sb("small", [S, T, E])
        score = sb("score", [S, PAIRS, H])
        share = sb("share", [S, T, H])
        ex = sb("ex", [S, 2, H, C])
        exr = sb("exr", [S, 2, HC])
        mx, sm = sb("mx", [S, H]), sb("sm", [S, H])
        qs = sb("qs", [S, H])
        o = sb("o", [S, 2, E])
        ot = sb("ot", [P, KC, S])
        delta = sb("delta", [S, E])
        mark = sb("mark", [1, 1])
        sem = {n: net.sem("l3a_" + n) for n in (
            "loaded", "var_ready", "std_ready", "beta_ready", "xn_ready", "xt_psum", "xt_ready", "kt_psum", "kt_ready",
            "cw_psum", "cw_copied", "qkv_psum", "qkv_ready", "shifted", "cw_ready", "norm_ready", "rnorm_ready",
            "scored", "ring_ready", "ring_summed", "lg_ready", "ex_ready", "exr_ready", "prod_ready", "weighed",
            "o_ready", "ot_psum", "ot_ready", "out_psum", "added")}
        wide, turned, summed = net.wide, net.turned, net.summed
        kt_banks = [turned[:, 0, :], turned[:, 1, :], summed[:, 0, :], summed[:, 1, :]]

        with nc.Block() as block:
            @block.sync
            def _(sp):
                load_weights(sp, net, pairs, sem["loaded"])

            @block.tensor
            def _(pe):
                def turn_x(t, slot, first):
                    pe.wait_ge(sem["xn_ready"], t + 1)
                    if not first:
                        pe.wait_ge(sem["xt_ready"], t - 1)
                    for k in range(KC):
                        last = pe.transpose(turned[:, slot, k * S:(k + 1) * S], xn[:, slot, k * P:(k + 1) * P], net.ident[0:S, 0:S])
                    last.then_inc(sem["xt_psum"], 1)

                by_pairs(pe, T, turn_x)
                pe.wait_ge(sem["loaded"], n_loaded)
                pe.wait_ge(sem["xt_ready"], T)
                for m in range(KC):
                    for half in range(T // TB):
                        for k in range(KC):
                            last = pe.matmul(kt_banks[m * (T // TB) + half][:, 0:TB * S], wqk[:, k, E + m * P:E + (m + 1) * P],
                                             xt[:, k, half * TB:(half + 1) * TB, :].rearrange("p t s -> p (t s)"),
                                             start=k == 0, stop=k == KC - 1)
                        last.then_inc(sem["kt_psum"], 1)
                pe.wait_ge(sem["kt_ready"], 2 * T // TB)

                for t in range(T):
                    if t >= 2:
                        pe.wait_ge(sem["cw_copied"], t - 1)
                    for m in range(KC):
                        last = pe.matmul(wide[0:S, 2 * (t % 2) + m, :], kt[:, m, t, :], qc[:, m, :], start=True, stop=True)
                    last.then_inc(sem["cw_psum"], 1)
                    if t >= 2:
                        pe.wait_ge(sem["qkv_ready"], t - 1)
                    for w, dst in ((wqk, turned[0:S, t % 2, :]), (wv, summed[0:S, t % 2, 0:E])):
                        for k in range(KC):
                            last = pe.matmul(dst, xt[:, k, t, :], w[:, k, :], start=k == 0, stop=k == KC - 1)
                    last.then_inc(sem["qkv_psum"], 1)

                def average(t):
                    if t >= 2:
                        pe.wait_ge(sem["lg_ready"], t - 1)
                    for u in range(t + 1):
                        n = pairs_before(t) + u
                        pe.wait_ge(sem["ring_ready"], n + 1)
                        for half in range(2):
                            last = pe.matmul(wide[0:S, 2 * (t % 2) + half, :], net.ident[0:S, 0:S],
                                             ring[:, n % RING, half * HALF:(half + 1) * HALF], start=u == 0, stop=u == t)
                        last.then_inc(sem["ring_summed"], 1)

                for t in range(AHEAD):
                    average(t)
                for t in range(T):
                    if t + AHEAD < T:
                        average(t + AHEAD)
                    pe.wait_ge(sem["o_ready"], t + 1)
                    for k in range(KC):
                        last = pe.transpose(turned[:, t % 2, k * S:(k + 1) * S], o[:, t % 2, k * P:(k + 1) * P], net.ident[0:S, 0:S])
                    last.then_inc(sem["ot_psum"], 1)
                    pe.wait_ge(sem["ot_ready"], t + 1)
                    if t >= 2:
                        pe.wait_ge(sem["added"], t - 1)
                    for k in range(KC):
                        last = pe.matmul(summed[0:S, t % 2, 0:E], ot[:, k, :], wo[:, k, :], start=k == 0, stop=k == KC - 1)
                    last.then_inc(sem["out_psum"], 1)

            @block.scalar
            def _(act):
                norm_stats_scalar(act, net, sem["var_ready"], sem["std_ready"])

                def copy_xt(t, slot, first):
                    act.wait_ge(sem["xt_psum"], t + 1)
                    act.activation(xt[:, :, bass.ds(t, 1), :].rearrange("p k o s -> p k (o s)"),
                                   turned[:, slot, 0:KC * S].rearrange("p (k s) -> p k s", k=KC), ACT.Copy).then_inc(sem["xt_ready"], 1)

                by_pairs(act, T, copy_xt)
                act.wait_ge(sem["loaded"], n_loaded)
                for m in range(KC):
                    for half in range(T // TB):
                        n = m * (T // TB) + half
                        act.wait_ge(sem["kt_psum"], n + 1)
                        act.activation(kt[:, m, half * TB:(half + 1) * TB, :].rearrange("p t s -> p (t s)"), kt_banks[n][:, 0:TB * S],
                                       ACT.Identity, bias=bkt[:, m:m + 1]).then_inc(sem["kt_ready"], 1)
                act.activation(beta[:], beta[:], ACT.Exp).then_inc(sem["beta_ready"], 1)

                def copy_cw(t, slot, first):
                    act.wait_ge(sem["cw_psum"], t + 1)
                    act.activation(cw[:, bass.ds(t, 1), :].rearrange("s o n -> s (o n)"), wide[0:S, 2 * slot:2 * slot + 2, :].rearrange("s a n -> s (a n)"),
                                   ACT.Copy).then_inc(sem["cw_copied"], 1)

                by_pairs(act, T, copy_cw)
                with act.Fori(0, T) as t:
                    act.wait_ge(sem["shifted"], t + 1)
                    act.activation(cw[:, t, :], cw[:, t, :], ACT.Exp).then_inc(sem["cw_ready"], 1)
                act.drain()
                act.activation(rnorm[:, 0, :], cw[:, 0, :], ACT.Ln)
                with act.Fori(1, T) as t:
                    act.wait_ge(sem["norm_ready"], t)
                    act.activation(rnorm[:, t, :], rnorm[:, t, :], ACT.Ln)
                act.drain()
                with act.Fori(0, T) as t:
                    act.activation(rnorm[:, t, :], rnorm[:, t, :], ACT.Exp, scale=-1.0).then_inc(sem["rnorm_ready"], 1)

                def exps(t):
                    act.wait_ge(sem["lg_ready"], t + 1)
                    act.activation(ex[:, t % 2], ex[:, t % 2], ACT.Exp).then_inc(sem["ex_ready"], 1)

                exps(0)
                exps(1)
                for t in range(T):
                    if t + 2 < T:
                        exps(t + 2)
                    act.wait_ge(sem["ot_psum"], t + 1)
                    act.activation(ot[:], turned[:, t % 2, 0:KC * S].rearrange("p (k s) -> p k s", k=KC), ACT.Copy).then_inc(sem["ot_ready"], 1)

            @block.gpsimd
            def _(pool):
                for t in range(1, T):
                    pool.wait_ge(sem["cw_ready"], t + 1)
                    if t >= 2:
                        pool.drain()
                    pool.tensor_tensor(rnorm[:, t, :], cw[:, 0, :] if t == 1 else rnorm[:, t - 1, :], cw[:, t, :], ALU.add)
                    if t >= 2:
                        pool.drain()
                        pool.memset(mark[:], 0.0).then_inc(sem["norm_ready"], 1)
                pool.drain()
                pool.memset(mark[:], 0.0).then_inc(sem["norm_ready"], 1)

                def products(t):
                    for u in range(t + 1):
                        n = pairs_before(t) + u
                        if n >= RING:
                            pool.wait_ge(sem["ring_summed"], n - RING + 1)
                        pool.tensor_tensor(ring[:, n % RING, :].rearrange("s (h c) -> s h c", h=H), cw[:, u, :].rearrange("s (h c) -> s h c", h=H),
                                           score[:, n, :].unsqueeze(2).broadcast_to([S, H, C]), ALU.mult).then_inc(sem["ring_ready"], 1)

                def weigh(t):
                    pool.wait_ge(sem["ex_ready"], t + 1)
                    pool.wait_ge(sem["rnorm_ready"], t + 1)
                    if t >= 2:
                        pool.wait_ge(sem["weighed"], t - 1)
                    pool.tensor_tensor(exr[:, t % 2, :], ex[:, t % 2].rearrange("s h c -> s (h c)"), rnorm[:, t, :],
                                       ALU.mult).then_inc(sem["exr_ready"], 1)
                    n, mine = t + 1, gpsimd_share(t + 1)
                    if mine:
                        pool.drain()
                        if t >= 1:
                            pool.wait_ge(sem["weighed"], t)
                        pool.tensor_tensor(prod[:, n - mine:n, :], cw[:, n - mine:n, :],
                                           exr[:, t % 2, :].unsqueeze(1).broadcast_to([S, mine, HC]), ALU.mult).then_inc(sem["prod_ready"], 1)

                pool.wait_ge(sem["scored"], 1)
                for t in range(AHEAD):
                    products(t)
                for t in range(T):
                    weigh(t)
                    if t + AHEAD < T:
                        products(t + AHEAD)

            @block.vector
            def _(dve):
                norm_stats_vector(dve, net, sem["var_ready"], sem["std_ready"])

                def normal(t, slot, first):
                    if not first:
                        dve.wait_ge(sem["xt_psum"], t - 1)
                    normalise(dve, net, xn[:, slot, :], t).then_inc(sem["xn_ready"], 1)

                by_pairs(dve, T, normal)
                dve.wait_ge(sem["beta_ready"], 1)
                dve.tensor_scalar(qs[:], beta[:], float(D) ** 0.5, None, ALU.mult)
                dve.drain()
                dve.reciprocal(qs[:], qs[:])
                dve.drain()

                def take(t, slot, first):
                    one = qk[:, bass.ds(t, 1), :].rearrange("s o n -> s (o n)")
                    dve.wait_ge(sem["qkv_psum"], t + 1)
                    dve.tensor_tensor(one, turned[0:S, slot, :], bqk[:], ALU.add)
                    dve.tensor_tensor(v[:, bass.ds(t, 1), :].rearrange("s o n -> s (o n)"), summed[0:S, slot, 0:E], bv[:],
                                      ALU.add).then_inc(sem["qkv_ready"], 1)
                    dve.wait_ge(sem["cw_copied"], t + 1)
                    here = cw[:, bass.ds(t, 1), :].rearrange("s o n -> s (o n)")
                    if isinstance(t, int) and t == 0:
                        dve.tensor_copy(top[:], here)
                    else:
                        dve.tensor_tensor(top[:], top[:], here, ALU.max)
                    dve.drain()
                    dve.tensor_tensor(one[:, 0:E].rearrange("s (h d) -> s h d", h=H), one[:, 0:E].rearrange("s (h d) -> s h d", h=H),
                                      qs[:].unsqueeze(2).broadcast_to([S, H, D]), ALU.mult)

                by_pairs(dve, T, take)
                dve.drain()
                with dve.Fori(0, T) as t:
                    dve.tensor_tensor(cw[:, t, :], cw[:, t, :], top[:], ALU.subtract).then_inc(sem["shifted"], 1)
                for t in range(T):
                    n, at = t + 1, pairs_before(t)
                    dve.tensor_tensor(small[:, 0:n, :], qk[:, 0:n, E:2 * E], qk[:, t, 0:E].unsqueeze(1).broadcast_to([S, n, E]), ALU.mult)
                    dve.drain()
                    last = dve.tensor_reduce(score[:, at:at + n, :], small[:, 0:n, :].rearrange("s t (h d) -> s t h d", h=H), X_AX, ALU.add)
                    if t == T - 1:
                        last.then_inc(sem["scored"], 1)
                    dve.drain()

                def shift(t):
                    one = ex[:, t % 2]
                    dve.wait_ge(sem["ring_summed"], pairs_before(t + 1))
                    dve.wait_ge(sem["rnorm_ready"], t + 1)
                    dve.tensor_tensor(one.rearrange("s h c -> s (h c)"), wide[0:S, 2 * (t % 2):2 * (t % 2) + 2, :].rearrange("s a n -> s (a n)"),
                                      rnorm[:, t, :], ALU.mult)
                    dve.drain()
                    dve.tensor_reduce(mx[:], one, X_AX, ALU.max)
                    dve.drain()
                    dve.tensor_tensor(one, one, mx[:].unsqueeze(2).broadcast_to([S, H, C]), ALU.subtract).then_inc(sem["lg_ready"], 1)

                def values(t):
                    n, mine = t + 1, t + 1 - gpsimd_share(t + 1)
                    dve.wait_ge(sem["ex_ready"], t + 1)
                    dve.tensor_reduce(sm[:], ex[:, t % 2], X_AX, ALU.add)
                    dve.wait_ge(sem["exr_ready"], t + 1)
                    dve.tensor_tensor(prod[:, 0:mine, :], cw[:, 0:mine, :], exr[:, t % 2, :].unsqueeze(1).broadcast_to([S, mine, HC]), ALU.mult)
                    dve.drain()
                    dve.reciprocal(sm[:], sm[:])
                    dve.tensor_reduce(share[:, 0:mine, :], prod[:, 0:mine, :].rearrange("s t (h c) -> s t h c", h=H), X_AX, ALU.add)
                    if mine < n:
                        dve.wait_ge(sem["prod_ready"], sum(gpsimd_share(u + 1) > 0 for u in range(n)))
                        dve.tensor_reduce(share[:, mine:n, :], prod[:, mine:n, :].rearrange("s t (h c) -> s t h c", h=H), X_AX, ALU.add)
                    dve.drain()
                    dve.tensor_tensor(share[:, 0:n, :], share[:, 0:n, :], sm[:].unsqueeze(1).broadcast_to([S, n, H]), ALU.mult).then_inc(sem["weighed"], 1)
                    dve.drain()
                    dve.tensor_tensor(small[:, 0:n, :].rearrange("s t (h d) -> s t h d", h=H), v[:, 0:n, :].rearrange("s t (h d) -> s t h d", h=H),
                                      share[:, 0:n, :].unsqueeze(3).broadcast_to([S, n, H, D]), ALU.mult)
                    dve.drain()
                    if t >= 2:
                        dve.wait_ge(sem["ot_psum"], t - 1)
                    dve.tensor_reduce(o[:, t % 2, :], small[:, 0:n, :].rearrange("s t n -> s n t"), X_AX, ALU.add).then_inc(sem["o_ready"], 1)

                def add(t):
                    dve.drain()
                    dve.wait_ge(sem["out_psum"], t + 1)
                    dve.tensor_tensor(delta[:], summed[0:S, t % 2, 0:E], bo[:], ALU.add).then_inc(sem["added"], 1)
                    dve.drain()
                    dve.tensor_tensor(net.x[:, t, :], net.x[:, t, :], delta[:], ALU.add)

                shift(0)
                shift(1)
                for t in range(T):
                    values(t)
                    if t + 2 < T:
                        shift(t + 2)
                    if t >= 1:
                        add(t - 1)
                add(T - 1)
                dve.drain()


@sublayer
def l3_ffn(net):
    nc, dram = net.nc, net.dram
    with ExitStack() as ctx:
        def sb(n, shape, dt=F32):
            return ctx.enter_context(nc.sbuf_tensor("l3f_" + n, shape, dt))

        wg, we = sb("wg", [P, KC, E]), sb("we", [P, KC, NE * E])
        bg, be = sb("bg", [S, E]), sb("be", [NE, E])
        iota = sb("iota", [S, B, NE])
        pairs = [(wg[:], dram["l3f_wg"]), (we[:], dram["l3f_we"]), (bg[:], dram["l3f_bg"].partition_broadcast(S)),
                 (be[:], dram["l3f_be"]), (iota[:], dram["iota8"])]
        n_loaded = 16 * len(pairs)
        xn = sb("xn", [S, E])
        xt = sb("xt", [P, KC, S])
        lg, ex = sb("lg", [S, E]), sb("ex", [S, E])
        top, ntop, sm, p = sb("top", [S, 8]), sb("ntop", [S, 1]), sb("sm", [S, 1]), sb("p", [S, 1])
        which, whichf = sb("which", [S, 8], U32), sb("whichf", [S, 1])
        hot = sb("hot", [S, NE])
        hot_t = sb("hot_t", [NE, S])
        acc = sb("acc", [S, E])
        sem = {n: net.sem("l3f_" + n) for n in (
            "loaded", "var_ready", "std_ready", "xn_ready", "xt_psum", "xt_ready", "g_psum", "z_psum", "top_ready", "ex_ready",
            "hot_ready", "ht_psum", "ht_ready", "b_psum")}
        wide, turned, summed = net.wide, net.turned, net.summed

        with nc.Block() as block:
            @block.sync
            def _(sp):
                load_weights(sp, net, pairs, sem["loaded"])

            @block.tensor
            def _(pe):
                pe.wait_ge(sem["loaded"], n_loaded)
                with pe.Fori(0, B) as b:
                    pe.wait_ge(sem["xn_ready"], b + 1)
                    for k in range(KC):
                        last = pe.transpose(turned[:, 0, k * S:(k + 1) * S], xn[:, k * P:(k + 1) * P], net.ident[0:S, 0:S])
                    last.then_inc(sem["xt_psum"], 1)
                    pe.wait_ge(sem["xt_ready"], b + 1)
                    for k in range(KC):
                        last = pe.matmul(summed[0:S, 0, 0:E], xt[:, k, :], wg[:, k, :], start=k == 0, stop=k == KC - 1)
                    last.then_inc(sem["g_psum"], 1)
                    for n in range(4):
                        for k in range(KC):
                            last = pe.matmul(wide[0:S, n, :], xt[:, k, :], we[:, k, n * 512:(n + 1) * 512], start=k == 0, stop=k == KC - 1)
                    last.then_inc(sem["z_psum"], 1)
                    pe.wait_ge(sem["hot_ready"], b + 1)
                    pe.transpose(turned[0:NE, 1, 0:S], hot[:], net.ident[0:S, 0:S]).then_inc(sem["ht_psum"], 1)
                    pe.wait_ge(sem["ht_ready"], b + 1)
                    pe.matmul(summed[0:S, 1, 0:E], hot_t[:], be[:], start=True, stop=True).then_inc(sem["b_psum"], 1)

            @block.scalar
            def _(act):
                norm_stats_scalar(act, net, sem["var_ready"], sem["std_ready"])
                with act.Fori(0, B) as b:
                    act.wait_ge(sem["xt_psum"], b + 1)
                    act.activation(xt[:], turned[:, 0, 0:KC * S].rearrange("p (k s) -> p k s", k=KC), ACT.Copy).then_inc(sem["xt_ready"], 1)
                    act.wait_ge(sem["top_ready"], b + 1)
                    act.activation(ex[:], lg[:], ACT.Exp, bias=ntop[:], accum_out=sm[:]).then_inc(sem["ex_ready"], 1)
                    act.wait_ge(sem["ht_psum"], b + 1)
                    act.activation(hot_t[:], turned[0:NE, 1, 0:S], ACT.Copy).then_inc(sem["ht_ready"], 1)

            @block.vector
            def _(dve):
                norm_stats_vector(dve, net, sem["var_ready"], sem["std_ready"])
                dve.wait_ge(sem["loaded"], n_loaded)
                with dve.Fori(0, B) as b:
                    normalise(dve, net, xn[:], b).then_inc(sem["xn_ready"], 1)
                    dve.wait_ge(sem["g_psum"], b + 1)
                    dve.tensor_tensor(lg[:], summed[0:S, 0, 0:E], bg[:], ALU.add)
                    dve.drain()
                    dve.max(top[:], lg[:])
                    dve.drain()
                    dve.tensor_scalar(ntop[:], top[:, 0:1], -1.0, None, ALU.mult).then_inc(sem["top_ready"], 1)
                    dve.wait_ge(sem["ex_ready"], b + 1)
                    dve.tensor_copy(p[:], sm[:])
                    dve.max(top[:], ex[:])
                    dve.drain()
                    dve.max_index(which[:], top[:], ex[:])
                    dve.reciprocal(p[:], p[:])
                    dve.drain()
                    dve.tensor_scalar(which[:, 0:1], which[:, 0:1], NE - 1, None, ALU.bitwise_and)
                    dve.tensor_tensor(p[:], p[:], top[:, 0:1], ALU.mult)
                    dve.drain()
                    dve.tensor_copy(whichf[:], which[:, 0:1])
                    dve.drain()
                    dve.tensor_tensor(hot[:], whichf[:].broadcast_to([S, NE]), iota[:, 0, :], ALU.is_equal).then_inc(sem["hot_ready"], 1)
                    dve.wait_ge(sem["b_psum"], b + 1)
                    dve.wait_ge(sem["z_psum"], b + 1)
                    dve.tensor_copy(acc[:], summed[0:S, 1, 0:E])
                    for e in range(NE):
                        dve.drain()
                        dve.scalar_tensor_tensor(out=acc[:], in0=wide[0:S, e // 2, (e % 2) * E:(e % 2 + 1) * E], scalar=hot[:, e:e + 1],
                                                 in1=acc[:], op0=ALU.mult, op1=ALU.add)
                    dve.drain()
                    dve.tensor_scalar(acc[:], acc[:], 0.0, p[:], ALU.max, ALU.mult)
                    dve.drain()
                    dve.tensor_tensor(net.x[:, b, :], net.x[:, b, :], acc[:], ALU.add)
                    dve.drain()


def more_layouts(a, d, wide, col):
    def experts(w):
        return w.reshape(w.shape[0], -1, P, w.shape[-1]).transpose(0, 2, 1, 3)

    d["iota8"] = np.broadcast_to(np.arange(NE, dtype=np.float32), (S, B, NE))
    d["before"] = (np.arange(S)[:, None] < np.arange(S)[None, :]).astype(np.float32)
    d["l0f_w1"] = experts(np.concatenate([a["L0_ffn_W1"], a["L0_ffn_Ws1"][None]]))
    d["l0f_w2"] = experts(np.concatenate([a["L0_ffn_W2"], a["L0_ffn_Ws2"][None]]))
    d["l0f_wr"] = wide(a["L0_ffn_Wr"])
    d["l1f_w1"] = experts(np.concatenate([a["L1_ffn_w1"], a["L1_ffn_ws1"][None]]))
    d["l1f_w2"] = experts(np.concatenate([a["L1_ffn_w2"], a["L1_ffn_ws2"][None]]))
    d["l1f_wr"] = wide(a["L1_ffn_gate_w"])
    d["l1f_br"] = a["L1_ffn_gate_b"]
    d["l1f_b1"] = np.concatenate([a["L1_ffn_b1"], a["L1_ffn_bs1"][None]]).reshape(NE + 1, -1, P).transpose(0, 2, 1)
    d["l1f_b2"] = np.concatenate([a["L1_ffn_b2"], a["L1_ffn_bs2"][None]])
    d["l1a_wqk"] = wide(np.concatenate([a["L1_attn_Wq"], a["L1_attn_Wk"]], axis=1))
    d["l1a_bqk"] = np.concatenate([a["L1_attn_bq"], a["L1_attn_bk"]])
    d["l1a_wv"], d["l1a_wo"] = wide(a["L1_attn_Wv"]), wide(a["L1_attn_Wo"])
    d["l1a_bv"], d["l1a_bo"] = a["L1_attn_bv"], a["L1_attn_bo"]
    for n in ("delta", "alpha", "beta", "gamma"):
        d["l2a_" + n] = a["L2_attn_" + n].reshape(KC, P, 2).transpose(1, 0, 2)
    d["l2a_omega"] = col(a["L2_attn_omega"])
    d["l2f_wr"] = wide(a["L2_ffn_Wr"].T)
    d["l2f_w1"], d["l2f_w2"] = experts(a["L2_ffn_W1"]), experts(a["L2_ffn_W2"])
    d["l3a_wqk"] = wide(np.concatenate([a["L3_attn_Wq"].T, a["L3_attn_Wk"].T], axis=1))
    d["l3a_bqk"] = np.concatenate([a["L3_attn_bq"], a["L3_attn_bk"]])
    d["l3a_bkt"] = col(a["L3_attn_bk"])
    d["l3a_wv"], d["l3a_wo"] = wide(a["L3_attn_Wv"].T), wide(a["L3_attn_Wo"].T)
    d["l3a_bv"], d["l3a_bo"], d["l3a_beta"] = a["L3_attn_bv"], a["L3_attn_bo"], a["L3_attn_beta"]
    H, D, C = 16, 16, 64
    blocks = np.zeros((H, D, H, C), np.float32)
    for h in range(H):
        blocks[h, :, h, :] = a["L3_attn_q_c"].reshape(C, H, D)[:, h, :].T
    half = H // KC
    d["l3a_qc"] = np.stack([blocks[m * half:(m + 1) * half, :, m * half:(m + 1) * half].reshape(P, half * C) for m in range(KC)], axis=1)
    d["l3f_wg"] = wide(a["L3_ffn_Wg"])
    d["l3f_we"] = wide(a["L3_ffn_We"].transpose(1, 0, 2).reshape(E, NE * E))
    d["l3f_bg"], d["l3f_be"] = a["L3_ffn_bg"], a["L3_ffn_be"]


def build(nc, dram):
    with ExitStack() as ctx:
        net = Net(nc, ctx, dram)
        setup(net)
        l0_attn(net)
        cross_attn(net, "l0x", 16, rope=True, biases=True, mask=("key_mask", I32))
        moe(net, "l0f", P)
        l1_attn(net)
        cross_attn(net, "l1x", 16, biases=True, gate=True)
        moe(net, "l1f", 1024, biases=True)
        l2_attn(net)
        cross_attn(net, "l2x", 4, mask=("query_mask", U8))
        l2_ffn(net)
        l3_attn(net)
        cross_attn(net, "l3x", 16)
        l3_ffn(net)
        store(net)


def _layouts(a):
    def wide(w):
        return w.reshape(-1, P, w.shape[-1]).transpose(1, 0, 2)

    def col(b):
        return b.reshape(-1, P).T

    d = {"x": a["x"], "ident": np.eye(P, dtype=np.float32)}
    d["causal"] = np.where(np.arange(S)[:, None] < np.arange(S)[None, :], np.float32(NEG), np.float32(0))
    d["ctxt"] = a["ctx_1024"].transpose(0, 2, 1).reshape(B, KC, P, SKV).transpose(0, 2, 1, 3)
    for D in (16, 64):
        d[f"headmask{D}"] = (np.arange(P)[:, None] // D == np.arange(P // D)[None, :]).astype(np.float32)
    for n in ("q", "k", "v"):
        d["l0a_w" + n] = wide(a["L0_attn_w_" + n].reshape(-1, E).T)
    d["l0a_wo"] = wide(a["L0_attn_w_o"])
    for k, n in (("l0x", "L0_xattn"), ("l1x", "L1_xattn")):
        for m in "qkvo":
            d[f"{k}_w{m}"] = wide(a[f"{n}_W{m}"])
        for m in "qk":
            d[f"{k}_b{m}"] = col(a[f"{n}_b{m}"])
        for m in "vo":
            d[f"{k}_b{m}"] = a[f"{n}_b{m}"]
    wkv = a["L2_xattn_Wkv"]
    for m, w in (("q", a["L2_xattn_Wq"]), ("k", wkv[:E]), ("v", wkv[E:]), ("o", a["L2_xattn_Wout"])):
        d["l2x_w" + m] = wide(w.T)
    for m in "qkvo":
        d["l3x_w" + m] = wide(a["L3_xattn_W" + m].T)
    d["l3x_bo"] = a["L3_xattn_bo"]
    d["key_mask"] = a["mask_Bx1x1xS2_if1"].reshape(B, SKV)
    bits = np.zeros((B, S, -(-SKV // 4) * 4), np.bool_)
    bits[:, :, 0:SKV] = a["mask_BxSxS2_bk0"]
    d["query_mask"] = bits.view(np.int32)
    D = 16
    r = np.arange(P) % D
    inv = (1.0 / np.float32(10000.0) ** (np.arange(0, D, 2, dtype=np.float32) / np.float32(D))).astype(np.float32)
    angle = (np.arange(SKV, dtype=np.float32)[None, :] * inv[r % (D // 2)][:, None]).astype(np.float32)
    d["rope_cos"], d["rope_sin"] = np.cos(angle), np.sin(angle)
    swap = np.zeros((P, P), np.float32)
    for p in range(P):
        lower = r[p] < D // 2
        swap[p + D // 2 if lower else p - D // 2, p] = -1.0 if lower else 1.0
    d["rope_swap"] = swap
    rows = np.minimum(np.arange(PADKV), SKV - 1)
    d["energy"] = a["ctxb_2048x8"][:, rows].reshape(B * NCH, CH, 8).transpose(1, 0, 2)
    more_layouts(a, d, wide, col)
    return {k: np.ascontiguousarray(v) for k, v in d.items()}


def kernel(**inputs):
    import concourse.bacc as bacc
    from concourse.bass_utils import run_bass_kernel_spmd

    nc = bacc.Bacc("TRN2", target_bir_lowering=False, num_devices=1)
    arrays = {k + "_dram": v for k, v in _layouts({k: np.asarray(v) for k, v in inputs.items()}).items()}
    dram = {k[:-5]: nc.dram_tensor(k, v.shape, mybir.dt.from_np(v.dtype), kind="ExternalInput").ap()
            for k, v in arrays.items()}
    dram["out"] = nc.dram_tensor("out_dram", (B, S, E), F32, kind="ExternalOutput").ap()
    build(nc, dram)
    return run_bass_kernel_spmd(nc, [arrays], core_ids=[0]).results[0]["out_dram"]
```

```python
from contextlib import ExitStack

import numpy as np

import concourse.bass as bass
from concourse import mybir

B, S, E = 8, 100, 256
P = 128
KC = E // P
SKV = 361
CH = 121
NCH = 3
PADKV = CH * NCH
LAST = SKV - CH * (NCH - 1)
EPS = 1e-5
NEG = -1e30
NE = 8

ALU = mybir.AluOpType
ACT = mybir.ActivationFunctionType
F32 = mybir.dt.float32
I32 = mybir.dt.int32
U32 = mybir.dt.uint32
U8 = mybir.dt.uint8
X_AX = mybir.AxisListType.X


class Net:

    def __init__(self, nc, ctx, dram):
        self.nc, self.ctx, self.dram = nc, ctx, dram
        self.x = ctx.enter_context(nc.sbuf_tensor("x", [S, B, E], F32))
        self.ident = ctx.enter_context(nc.sbuf_tensor("ident", [P, P], F32))
        self.stats = ctx.enter_context(nc.sbuf_tensor("stats", [S, B, 6], F32))
        self.moments = ctx.enter_context(nc.sbuf_tensor("moments", [S, B, 2], F32))
        self.std = ctx.enter_context(nc.sbuf_tensor("std", [S, B, 1], F32))
        self.rstd = ctx.enter_context(nc.sbuf_tensor("rstd", [S, B, 1], F32))
        self.wide = ctx.enter_context(nc.psum_tensor("wide", [P, 4, 512], F32))
        self.turned = ctx.enter_context(nc.psum_tensor("turned", [P, 2, 512], F32))
        self.summed = ctx.enter_context(nc.psum_tensor("summed", [P, 2, 512], F32))

        self.sems = []

    def sem(self, name):
        self.sems.append(self.nc.alloc_semaphore(name=name))
        return self.sems[-1]

    def end_sublayer(self):
        self.nc.clear_and_free_semaphores(self.sems)
        self.nc.all_engine_barrier()
        self.sems = []


def sublayer(emit):
    def whole(net, *args, **kwargs):
        emit(net, *args, **kwargs)
        net.end_sublayer()
    return whole


def load_weights(sp, net, pairs, loaded):
    for tile, source in pairs:
        sp.dma_start(tile, source).then_inc(loaded, 16)
    return 16 * len(pairs)


def norm_stats_vector(dve, net, var_ready, std_ready):
    for b in range(B):
        dve.bn_stats(net.stats[:, b, :], net.x[:, b, :])
    dve.drain()
    for b in range(B):
        dve.bn_aggr(net.moments[:, b, :], net.stats[:, b, :])
    dve.drain()
    dve.tensor_scalar(net.std[:], net.moments[:, :, 1:2], EPS, None, ALU.add).then_inc(var_ready, 1)
    dve.wait_ge(std_ready, 1)
    dve.reciprocal(net.rstd[:], net.std[:])
    dve.drain()


def norm_stats_scalar(act, net, var_ready, std_ready):
    act.wait_ge(var_ready, 1)
    act.activation(net.std[:], net.std[:], ACT.Sqrt).then_inc(std_ready, 1)


def normalise(dve, net, out, b):
    return dve.tensor_scalar(out, net.x[:, b, :], net.moments[:, b, 0:1], net.rstd[:, b, :],
                             ALU.subtract, ALU.mult)


def by_pairs(engine, count, body):
    for slot in range(2):
        body(slot, slot, True)
    with engine.Fori(1, count // 2) as r:
        for slot in range(2):
            body(2 * r + slot, slot, False)


@sublayer
def setup(net):
    nc = net.nc
    loaded = net.sem("setup_loaded")
    with nc.Block() as block:
        @block.sync
        def _(sp):
            sp.dma_start(net.x[:], net.dram["x"].rearrange("b s d -> s b d")).then_inc(loaded, 16)
            sp.dma_start(net.ident[:], net.dram["ident"]).then_inc(loaded, 16)
            sp.wait_ge(loaded, 32)


def store(net):
    nc = net.nc
    stored = net.sem("stored")
    with nc.Block() as block:
        @block.sync
        def _(sp):
            sp.dma_start(net.dram["out"].rearrange("b s d -> s b d"), net.x[:]).then_inc(stored, 16)
            sp.wait_ge(stored, 16)


@sublayer
def l0_attn(net):
    nc, dram = net.nc, net.dram
    H, D, G = 16, 64, 4
    HD = H * D
    MC = HD // P
    PER = MC // 2
    NG = H // G
    FRONT = ["xt", "q0", "q1", "k0", "k1", "v0", "v1"]
    TAIL = ["yt0", "yt1", "out"]
    TIMETABLE = [(["xt"], [], ["q0"]), (["q1"], ["k0"], []), (["k1"], ["v0"], []), (["yt0"], ["yt1"], ["v1", "out"])]
    ORDER = [what for step in TIMETABLE for place in step for what in place]
    BY_VECTOR = ("k0", "k1", "v1", "out")

    def first_head(g):
        return (g // 2) * 2 * G + g % 2

    def number(what, b):
        if isinstance(b, int):
            if what in FRONT and b < 2:
                n = b * len(FRONT) + FRONT.index(what)
            elif what in TAIL and b >= B - 2:
                n = 2 * len(FRONT) + (B - 2) * len(ORDER) + (b - (B - 2)) * len(TAIL) + TAIL.index(what)
            else:
                n = 2 * len(FRONT) + (b - 2 if what in FRONT else b) * len(ORDER) + ORDER.index(what)
            return n % 2, n // 2
        half = len(FRONT) + (b - 2 if what in FRONT else b) * (len(ORDER) // 2)
        return ORDER.index(what) % 2, half + ORDER.index(what) // 2

    with ExitStack() as ctx:
        def sb(name, shape, dt=F32):
            return ctx.enter_context(nc.sbuf_tensor("l0a_" + name, shape, dt))

        wq, wk, wv = (sb(n, [P, KC, HD]) for n in ("wq", "wk", "wv"))
        wo = sb("wo", [P, MC, E])
        causal = sb("causal", [S, S])
        pairs = [(wq[:], dram["l0a_wq"]), (wk[:], dram["l0a_wk"]), (wv[:], dram["l0a_wv"]),
                 (wo[:], dram["l0a_wo"]), (causal[:], dram["causal"])]
        n_loaded = 16 * len(pairs)
        xn = sb("xn", [S, E])
        xt = sb("xt", [P, KC, S])
        qt, kt = sb("qt", [P, 2, MC, S]), sb("kt", [P, 2, MC, S])
        v1 = sb("v1", [S, 2, H, D + 1])
        sc = sb("sc", [S, 2, G, S])
        mx = sb("mx", [S, H])
        pr = sb("pr", [S, 2, G, S])
        pt = sb("pt", [S, 2, G, S])
        rs = sb("rs", [S, H])
        y = sb("y", [S, 2, H, D])
        yt = sb("yt", [P, MC, S])
        sem = {n: net.sem("l0a_" + n) for n in (
            "loaded", "var_ready", "std_ready", "xn_ready", "side_psum", "side_done0", "side_done1",
            "s_psum", "s_ready", "p_ready", "pt_psum", "pt_ready", "y_psum", "y_ready")}
        side_done = (sem["side_done0"], sem["side_done1"])
        scored, side, turned, summed = net.wide[:, 0:2, :], net.wide[:, 2:4, :], net.turned, net.summed

        def has(what, b):
            return not (isinstance(b, int) and (what in FRONT and b == B - 1 or what in TAIL and b == 0))

        def walk(engine, step):
            for b in (0, 1):
                for g in range(NG):
                    step(b, b % 2, g)
            with engine.Fori(1, B // 2 - 1) as r:
                for slot in range(2):
                    for g in range(NG):
                        step(2 * r + slot, slot, g)
            for b in (B - 2, B - 1):
                for g in range(NG):
                    step(b, b % 2, g)

        def wait_written(engine, what, b):
            bank, before = number(what, b)
            engine.wait_ge(sem["side_psum"], 2 * before + bank + 1)

        def wait_read(engine, what, b):
            bank, before = number(what, b)
            engine.wait_ge(side_done[bank], before + 1)

        with nc.Block() as block:
            @block.sync
            def _(sp):
                load_weights(sp, net, pairs, sem["loaded"])

            @block.tensor
            def _(pe):
                def piece(what, b, slot):
                    bank, before = number(what, b)
                    out = side[:, bank, :]
                    if not (isinstance(before, int) and before == 0):
                        pe.wait_ge(side_done[bank], before)
                    if what == "xt":
                        pe.wait_ge(sem["xn_ready"], b + 1)
                        for k in range(KC):
                            last = pe.transpose(out[:, k * S:(k + 1) * S], xn[:, k * P:(k + 1) * P], net.ident[0:S, 0:S])
                    elif what in ("q0", "q1", "k0", "k1"):
                        if what == "q0":
                            wait_read(pe, "xt", b)
                        w = wq if what[0] == "q" else wk
                        for j in range(PER):
                            m = int(what[1]) * PER + j
                            for k in range(KC):
                                last = pe.matmul(out[:, j * S:(j + 1) * S], w[:, k, m * P:(m + 1) * P], xt[:, k, :],
                                                 start=k == 0, stop=k == KC - 1)
                    elif what in ("v0", "v1"):
                        n = int(what[1])
                        for k in range(KC):
                            last = pe.matmul(out[0:S, :], xt[:, k, :], wv[:, k, n * 512:(n + 1) * 512], start=k == 0, stop=k == KC - 1)
                    elif what in ("yt0", "yt1"):
                        if what == "yt0":
                            pe.wait_ge(sem["y_ready"], (b + 1) * NG)
                        for j in range(PER):
                            m = int(what[2]) * PER + j
                            last = pe.transpose(out[:, j * S:(j + 1) * S], y[:, slot, 2 * m:2 * m + 2, :].rearrange("s h d -> s (h d)"),
                                                net.ident[0:S, 0:S])
                    elif what == "out":
                        for half in ("yt0", "yt1"):
                            if number(half, b)[0] != bank:
                                wait_read(pe, half, b)
                        for m in range(MC):
                            last = pe.matmul(out[0:S, 0:E], yt[:, m, :], wo[:, m, :], start=m == 0, stop=m == MC - 1)
                    last.then_inc(sem["side_psum"], 1)

                def turn(n, g):
                    pe.wait_ge(sem["p_ready"], n + 1)
                    if not isinstance(n, int) or n >= 2:
                        pe.wait_ge(sem["pt_ready"], n - 1)
                    for j in range(G):
                        last = pe.transpose(turned[0:S, g % 2, j * S:(j + 1) * S], pr[:, g % 2, j, :], net.ident[0:S, 0:S])
                    last.then_inc(sem["pt_psum"], 1)

                def weigh(b, n, g, slot):
                    if g == 0:
                        wait_read(pe, "v0", b)
                        wait_read(pe, "v1", b)
                    pe.wait_ge(sem["pt_ready"], n + 1)
                    if not isinstance(n, int) or n >= 2:
                        pe.wait_ge(sem["y_ready"], n - 1)
                    for j in range(G):
                        last = pe.matmul(summed[0:S, g % 2, j * (D + 1):(j + 1) * (D + 1)], pt[:, g % 2, j, :],
                                         v1[:, slot, first_head(g) + 2 * j, :], start=True, stop=True)
                    last.then_inc(sem["y_psum"], 1)

                def step(b, slot, g):
                    n = b * NG + g
                    if g == 0:
                        for what in ("k0", "k1"):
                            wait_read(pe, what, b)
                    if not isinstance(n, int) or n >= 2:
                        pe.wait_ge(sem["s_ready"], n - 1)
                    r = (g % 2) * D
                    for j in range(G):
                        m = first_head(g) // 2 + j
                        last = pe.matmul(scored[0:S, g % 2, j * S:(j + 1) * S], qt[r:r + D, slot, m, :], kt[r:r + D, slot, m, :],
                                         start=True, stop=True)
                    last.then_inc(sem["s_psum"], 1)
                    for place in range(3):
                        for what in TIMETABLE[g][place]:
                            if has(what, b):
                                piece(what, b + 1 if what in FRONT else b - 1, 1 - slot)
                        if place == 0 and (not isinstance(n, int) or n >= 1):
                            turn(n - 1, (g - 1) % NG)
                        if place == 1 and (not isinstance(n, int) or n >= 2):
                            weigh(b if g >= 2 else b - 1, n - 2, (g - 2) % NG, slot if g >= 2 else 1 - slot)

                pe.wait_ge(sem["loaded"], n_loaded)
                for what in FRONT:
                    piece(what, 0, 0)
                walk(pe, step)
                n = B * NG
                turn(n - 1, NG - 1)
                weigh(B - 1, n - 2, NG - 2, 1)
                weigh(B - 1, n - 1, NG - 1, 1)
                for what in TAIL:
                    piece(what, B - 1, 1)

            @block.scalar
            def _(act):
                def piece(what, b, slot):
                    src = side[:, number(what, b)[0], :]
                    if what == "xt":
                        dst, src = xt[:], src[:, 0:KC * S].rearrange("p (k s) -> p k s", k=KC)
                    elif what in ("q0", "q1"):
                        half = int(what[1])
                        dst, src = qt[:, slot, half * PER:(half + 1) * PER, :], src[:, 0:PER * S].rearrange("p (m s) -> p m s", m=PER)
                    elif what == "v0":
                        dst, src = v1[:, slot, 0:H // 2, 0:D], src[0:S, :].rearrange("s (h d) -> s h d", d=D)
                    else:
                        half = int(what[2])
                        dst, src = yt[:, half * PER:(half + 1) * PER, :], src[:, 0:PER * S].rearrange("p (m s) -> p m s", m=PER)
                    wait_written(act, what, b)
                    act.activation(dst, src, ACT.Copy).then_inc(side_done[number(what, b)[0]], 1)

                def copy_pt(n, g):
                    act.wait_ge(sem["pt_psum"], n + 1)
                    if not isinstance(n, int) or n >= 2:
                        act.wait_ge(sem["y_psum"], n - 1)
                    act.activation(pt[:, g % 2], turned[0:S, g % 2, 0:G * S].rearrange("s (j t) -> s j t", j=G), ACT.Copy).then_inc(sem["pt_ready"], 1)

                def step(b, slot, g):
                    n = b * NG + g
                    for place in range(3):
                        for what in TIMETABLE[g][place]:
                            if has(what, b) and what not in BY_VECTOR:
                                piece(what, b + 1 if what in FRONT else b - 1, 1 - slot)
                        if place == 0 and (not isinstance(n, int) or n >= 1):
                            copy_pt(n - 1, (g - 1) % NG)
                        if place == 1:
                            act.wait_ge(sem["s_ready"], n + 1)
                            if not isinstance(n, int) or n >= 2:
                                act.wait_ge(sem["pt_psum"], n - 1)
                            act.activation(pr[:, g % 2], sc[:, g % 2], ACT.Exp, scale=D ** -0.5).then_inc(sem["p_ready"], 1)

                norm_stats_scalar(act, net, sem["var_ready"], sem["std_ready"])
                for what in FRONT:
                    if what not in BY_VECTOR:
                        piece(what, 0, 0)
                walk(act, step)
                copy_pt(B * NG - 1, NG - 1)
                for what in ("yt0", "yt1"):
                    piece(what, B - 1, 1)

            @block.vector
            def _(dve):
                def piece(what, b, slot):
                    bank = number(what, b)[0]
                    src = side[:, bank, :]
                    wait_written(dve, what, b)
                    if what in ("k0", "k1"):
                        half = int(what[1])
                        last = dve.tensor_copy(kt[:, slot, half * PER:(half + 1) * PER, :], src[:, 0:PER * S].rearrange("p (m s) -> p m s", m=PER))
                    elif what == "v1":
                        last = dve.tensor_copy(v1[:, slot, H // 2:H, 0:D], src[0:S, :].rearrange("s (h d) -> s h d", d=D))
                    else:
                        last = dve.tensor_tensor(net.x[:, b, :], net.x[:, b, :], src[0:S, 0:E], ALU.add)
                    last.then_inc(side_done[bank], 1)

                def shift(n, g):
                    dve.wait_ge(sem["s_psum"], n + 1)
                    if not isinstance(n, int) or n >= 2:
                        dve.wait_ge(sem["p_ready"], n - 1)
                    one = sc[:, g % 2]
                    dve.tensor_tensor(one, scored[0:S, g % 2, 0:G * S].rearrange("s (j t) -> s j t", j=G),
                                      causal[:].unsqueeze(1).broadcast_to([S, G, S]), ALU.add)
                    dve.drain()
                    dve.tensor_reduce(mx[:, g * G:(g + 1) * G], one, X_AX, ALU.max)
                    dve.drain()
                    dve.tensor_tensor(one, one, mx[:, g * G:(g + 1) * G].unsqueeze(2).broadcast_to([S, G, S]),
                                      ALU.subtract).then_inc(sem["s_ready"], 1)

                def divide(n, g, slot):
                    dve.wait_ge(sem["y_psum"], n + 1)
                    got = summed[0:S, g % 2, 0:G * (D + 1)].rearrange("s (j d) -> s j d", j=G)
                    dve.reciprocal(rs[:, g * G:(g + 1) * G].unsqueeze(2), got[:, :, D:D + 1])
                    dve.drain()
                    dve.tensor_tensor(y[:, slot, first_head(g):first_head(g) + 2 * G - 1:2, :], got[:, :, 0:D],
                                      rs[:, g * G:(g + 1) * G].unsqueeze(2).broadcast_to([S, G, D]), ALU.mult).then_inc(sem["y_ready"], 1)

                def step(b, slot, g):
                    n = b * NG + g
                    if has("xt", b) and g == 0:
                        normalise(dve, net, xn[:], b + 1).then_inc(sem["xn_ready"], 1)
                    shift(n, g)
                    for place in range(3):
                        for what in TIMETABLE[g][place]:
                            if has(what, b) and what in BY_VECTOR:
                                piece(what, b + 1 if what in FRONT else b - 1, 1 - slot)
                        if place == 1 and (not isinstance(n, int) or n >= 2):
                            divide(n - 2, (g - 2) % NG, slot if g >= 2 else 1 - slot)

                dve.memset(v1[:, :, :, D:D + 1], 1.0)
                norm_stats_vector(dve, net, sem["var_ready"], sem["std_ready"])
                normalise(dve, net, xn[:], 0).then_inc(sem["xn_ready"], 1)
                dve.wait_ge(sem["loaded"], n_loaded)
                for what in FRONT:
                    if what in BY_VECTOR:
                        piece(what, 0, 0)
                walk(dve, step)
                n = B * NG
                divide(n - 2, NG - 2, 1)
                divide(n - 1, NG - 1, 1)
                piece("out", B - 1, 1)
                dve.drain()


@sublayer
def cross_attn(net, name, H, rope=False, biases=False, mask=None, gate=False):
    nc, dram = net.nc, net.dram
    D = E // H
    HP = P // D
    SCALE = D ** -0.5
    FRONT = ["xt", "q", "k0", "k1", "v0", "v1"]
    if rope:
        FRONT = ["xt", "q", "qswap", "k0", "k0swap", "k1", "k1swap", "v0", "v1"]
    upright = D == 16
    V = 32 if upright else D + 1
    TAIL = ["back", "yt", "out"] if upright else ["yt", "out"]
    if H == 16:
        timetable = {4 + n: [piece] for n, piece in enumerate(TAIL + FRONT)}
    else:
        timetable = {0: FRONT[0:2], 1: FRONT[2:4], 2: FRONT[4:6], 3: TAIL}
    with ExitStack() as ctx:
        def sb(n, shape, dt=F32):
            return ctx.enter_context(nc.sbuf_tensor(name + "_" + n, shape, dt))

        w = {n: sb(n, [P, KC, E]) for n in ("wq", "wk", "wv", "wo")}
        pairs = [(w[n][:], dram[name + "_" + n]) for n in w]
        headmask = sb("headmask", [P, HP])
        pairs.append((headmask[:], dram[f"headmask{D}"]))
        bo = None
        if biases:
            bq, bk, bv = sb("bq", [P, KC]), sb("bk", [P, KC]), sb("bv", [P, E])
            pairs += [(bq[:], dram[name + "_bq"]), (bk[:], dram[name + "_bk"]),
                      (bv[:], dram[name + "_bv"].partition_broadcast(P))]
        if name + "_bo" in dram:
            bo = sb("bo", [P, E])
            pairs.append((bo[:], dram[name + "_bo"].partition_broadcast(P)))
        if rope:
            swap = sb("swap", [P, P])
            cos, sin = sb("cos", [P, SKV]), sb("sin", [P, SKV])
            pairs += [(swap[:], dram["rope_swap"]), (cos[:], dram["rope_cos"]), (sin[:], dram["rope_sin"])]
            kraw, qraw = sb("kraw", [P, KC, SKV]), sb("qraw", [P, KC, S])
            ksin, qsin = sb("ksin", [P, SKV]), sb("qsin", [P, KC, S])
        if gate:
            energy = sb("energy", [CH, B * NCH, 8])
            gates = sb("gates", [CH, B * NCH])
            gsum = sb("gsum", [CH, B * NCH])
            pairs.append((energy[:], dram["energy"]))
        n_loaded = 16 * len(pairs)
        if mask:
            words = sb("words", [S, 2, dram[mask[0]].shape[-1]], I32)
            bias = sb("bias", [S, 2, SKV])
            sc = sb("sc", [S, 4, SKV])
        ctxt = sb("ctxt", [P, 2, KC, SKV])
        xn = sb("xn", [S, E])
        xt = sb("xt", [P, KC, S])
        qt = sb("qt", [P, KC, S])
        qm = sb("qm", [P, 2, KC, HP, S])
        kt = sb("kt", [P, 2, KC, PADKV])
        v1 = sb("v1", [CH, 2, NCH, H, V])
        mx, nmx = sb("mx", [S, H]), sb("nmx", [S, H])
        pr = sb("pr", [S, 4, PADKV])
        pt = sb("pt", [CH, 4, NCH, S])
        rs = sb("rs", [S, H])
        y = sb("y", [S, H, D])
        if upright:
            sums = sb("sums", [P, H // 4, S])
        yt = sb("yt", [P, KC, S])
        delta = sb("delta", [S, E])
        mark = sb("mark", [1, 1])

        sem = {n: net.sem(name + "_" + n) for n in (
            "loaded", "ctx0", "ctx1", "mask_used", "var_ready", "std_ready", "cleared", "gate_sum", "gate_ready", "xn_ready",
            "side_psum", "side_done", "front_ready", "s_psum", "m_ready", "p_ready", "pt_psum", "pt_even", "pt_odd",
            "y_psum", "y_ready", "q_ready", "qm_ready")}
        side, summed = net.summed[:, 1, :], net.summed[:, 0, :]
        wide, turned = net.wide, net.turned
        ctx_loaded = (sem["ctx0"], sem["ctx1"])
        pt_ready = (sem["pt_even"], sem["pt_odd"])
        per_ctx = 32 if mask else 16
        PER = len(FRONT) + len(TAIL)

        def pieces(b, step):
            last = isinstance(b, int) and b == B - 1
            first = isinstance(b, int) and b == 0
            order = [x for i in sorted(timetable) for x in timetable[i]
                     if not (first and x in TAIL) and not (last and x in FRONT)]
            before = len(FRONT) if first else 2 * len(FRONT) + (b - 1) * PER
            return [(x, before + order.index(x)) for x in timetable.get(step, []) if x in order]

        def copy_pt(engine, g, h):
            engine.wait_ge(sem["pt_psum"], g + 1)
            if not isinstance(g, int) or g >= 4:
                engine.wait_ge(sem["y_psum"], g - 1)
            src = turned[0:CH, h % 2, 0:NCH * S].rearrange("s (c t) -> s c t", c=NCH)
            if h % 2:
                last = engine.activation(pt[:, h % 4], src, ACT.Copy)
            else:
                last = engine.tensor_copy(pt[:, h % 4], src)
            last.then_inc(pt_ready[h % 2], 1)

        def walk(engine, front, step, finish):
            front(0, 0, [(x, n) for n, x in enumerate(FRONT)])
            for i in range(H):
                step(0, 0, i)
            with engine.Fori(0, (B - 2) // 2) as r:
                for n in (1, 2):
                    for i in range(H):
                        step(2 * r + n, n % 2, i)
            for i in range(H):
                step(B - 1, 1, i)
            finish()

        with nc.Block() as block:
            @block.sync
            def _(sp):
                load_weights(sp, net, pairs, sem["loaded"])

                def load_ctx(b, slot):
                    sp.dma_start(ctxt[:, slot], dram["ctxt"][b]).then_inc(ctx_loaded[slot], 16)
                    if mask:
                        src = dram[mask[0]][b]
                        if mask[0] == "key_mask":
                            src = src.partition_broadcast(S)
                        sp.dma_start(words[:, slot], src).then_inc(ctx_loaded[slot], 16)

                load_ctx(0, 0)
                load_ctx(1, 1)
                with sp.Fori(1, B // 2) as i:
                    for slot in range(2):
                        sp.wait_ge(sem["front_ready"], 2 * i + slot - 1)
                        if mask:
                            sp.wait_ge(sem["mask_used"], 2 * i + slot - 1)
                        load_ctx(2 * i + slot, slot)

            @block.tensor
            def _(pe):
                pe.wait_ge(sem["loaded"], n_loaded)
                pe.wait_ge(sem["cleared"], 1)
                if gate:
                    pe.wait_ge(sem["gate_ready"], 1)

                def piece(what, n, b, slot):
                    pe.wait_ge(sem["side_done"], n)
                    if what == "xt":
                        pe.wait_ge(sem["xn_ready"], b + 1)
                        for k in range(KC):
                            last = pe.transpose(side[:, k * S:(k + 1) * S], xn[:, k * P:(k + 1) * P], net.ident[0:S, 0:S])
                    elif what == "q":
                        for m in range(KC):
                            for k in range(KC):
                                last = pe.matmul(side[:, m * S:(m + 1) * S], w["wq"][:, k, m * P:(m + 1) * P], xt[:, k, :],
                                                 start=k == 0, stop=k == KC - 1)
                    elif what == "qswap":
                        for m in range(KC):
                            last = pe.matmul(side[:, m * S:(m + 1) * S], swap[:], qraw[:, m, :], start=True, stop=True)
                    elif what in ("k0", "k1"):
                        m = int(what[1])
                        if m == 0:
                            pe.wait_ge(ctx_loaded[slot], (b - slot) * (per_ctx // 2) + per_ctx)
                        for k in range(KC):
                            last = pe.matmul(side[:, 0:SKV], w["wk"][:, k, m * P:(m + 1) * P], ctxt[:, slot, k, :],
                                             start=k == 0, stop=k == KC - 1)
                    elif what in ("k0swap", "k1swap"):
                        last = pe.matmul(side[:, 0:SKV], swap[:], kraw[:, int(what[1]), :], start=True, stop=True)
                    elif what in ("v0", "v1"):
                        for c in (0, 1) if what == "v0" else (2,):
                            n_rows = CH if c < NCH - 1 else LAST
                            for k in range(KC):
                                last = pe.matmul(side[0:n_rows, (c % 2) * E:(c % 2 + 1) * E],
                                                 ctxt[:, slot, k, c * CH:c * CH + n_rows], w["wv"][:, k, :],
                                                 start=k == 0, stop=k == KC - 1)
                    elif what == "back":
                        pe.wait_ge(sem["y_ready"], b + 1)
                        for a in range(H // 4):
                            last = pe.transpose(side[0:S, a * P:(a + 1) * P], sums[:, a, :], net.ident[:])
                    elif what == "yt":
                        if not upright:
                            pe.wait_ge(sem["y_ready"], b + 1)
                        for k in range(KC):
                            last = pe.transpose(side[:, k * S:(k + 1) * S], y[:].rearrange("s h d -> s (h d)")[:, k * P:(k + 1) * P],
                                                net.ident[0:S, 0:S])
                    elif what == "out":
                        for k in range(KC):
                            last = pe.matmul(side[0:S, 0:E], yt[:, k, :], w["wo"][:, k, :], start=k == 0, stop=k == KC - 1)
                    last.then_inc(sem["side_psum"], 1)

                def front(b, slot, listed):
                    for what, n in listed:
                        piece(what, n, b, slot)

                def turn(b, g, h):
                    pe.wait_ge(sem["p_ready"], g + 1)
                    if not isinstance(g, int) or g >= 2:
                        pe.wait_ge(pt_ready[h % 2], b * (H // 2) + h // 2)
                    for c in range(NCH):
                        last = pe.transpose(turned[0:CH, h % 2, c * S:(c + 1) * S], pr[:, h % 4, c * CH:(c + 1) * CH], net.ident[0:S, 0:S])
                    last.then_inc(sem["pt_psum"], 1)

                def weigh(b, g, h, slot):
                    pe.wait_ge(pt_ready[h % 2], b * (H // 2) + h // 2 + 1)
                    if h == 0 and (not isinstance(b, int) or b >= 1):
                        pe.wait_ge(sem["y_ready"], b)
                    for c in range(NCH):
                        if upright:
                            last = pe.matmul(summed[(h % 4) * V:(h % 4 + 1) * V, (h // 4) * S:(h // 4 + 1) * S], v1[:, slot, c, h, :],
                                             pt[:, h % 4, c, :], start=c == 0, stop=c == NCH - 1)
                        else:
                            last = pe.matmul(summed[0:S, h * V:(h + 1) * V], pt[:, h % 4, c, :], v1[:, slot, c, h, :],
                                             start=c == 0, stop=c == NCH - 1)
                    last.then_inc(sem["y_psum"], 1)

                def step(b, slot, i):
                    g = b * H + i
                    if i == 0:
                        pe.wait_ge(sem["front_ready"], b + 1)
                        pe.wait_ge(sem["qm_ready"], b + 1)
                    if not isinstance(b, int) or g >= 4:
                        if mask:
                            pe.wait_ge(sem["m_ready"], g - 3)
                        else:
                            pe.wait_ge(sem["p_ready"], g - 3)
                    pe.matmul(wide[0:S, i % 4, 0:SKV], qm[:, slot, i // HP, i % HP, :], kt[:, slot, i // HP, 0:SKV],
                              start=True, stop=True).then_inc(sem["s_psum"], 1)
                    if i >= 2:
                        turn(b, g - 2, i - 2)
                    elif not isinstance(b, int) or b >= 1:
                        turn(b - 1, g - 2, H + i - 2)
                    if i >= 3:
                        weigh(b, g - 3, i - 3, slot)
                    elif not isinstance(b, int) or b >= 1:
                        weigh(b - 1, g - 3, H + i - 3, 1 - slot)
                    for what, n in pieces(b, i):
                        if what in TAIL:
                            piece(what, n, b - 1, 1 - slot)
                        else:
                            piece(what, n, b + 1, 1 - slot)

                def finish():
                    g = B * H
                    for h in (H - 2, H - 1):
                        turn(B - 1, B * H - H + h, h)
                        weigh(B - 1, g - H + h - 1, h - 1, 1)
                    weigh(B - 1, g - 1, H - 1, 1)
                    for n, what in enumerate(TAIL):
                        piece(what, (PER * (B - 1) + len(FRONT)) + n, B - 1, 1)

                walk(pe, front, step, finish)

            @block.scalar
            def _(act):
                norm_stats_scalar(act, net, sem["var_ready"], sem["std_ready"])
                if gate:
                    act.wait_ge(sem["gate_sum"], 1)
                    act.activation(gates[:], gsum[:], ACT.Sigmoid).then_inc(sem["gate_ready"], 1)
                act.wait_ge(sem["loaded"], n_loaded)
                act.wait_ge(sem["cleared"], 1)

                def piece(what, n, slot):
                    if what in ("xt", "yt"):
                        act.wait_ge(sem["side_psum"], n + 1)
                        act.activation((xt if what == "xt" else yt)[:], side[:, 0:KC * S].rearrange("p (k s) -> p k s", k=KC),
                                       ACT.Copy).then_inc(sem["side_done"], 1)
                    elif what in ("k0", "k1"):
                        m = int(what[1])
                        dst = kraw[:, m, :] if rope else kt[:, slot, m, 0:SKV]
                        act.wait_ge(sem["side_psum"], n + 1)
                        if biases:
                            last = act.activation(dst, side[:, 0:SKV], ACT.Identity, bias=bk[:, m:m + 1])
                        else:
                            last = act.activation(dst, side[:, 0:SKV], ACT.Copy)
                        last.then_inc(sem["side_done"], 1)

                def front(b, slot, listed):
                    for what, n in listed:
                        piece(what, n, slot)

                def take(b):
                    act.wait_ge(sem["y_psum"], (b + 1) * H)
                    act.activation(sums[:], summed[:, 0:H // 4 * S].rearrange("p (a s) -> p a s", s=S), ACT.Copy).then_inc(sem["y_ready"], 1)

                def step(b, slot, i):
                    g = b * H + i
                    if i % 2 == 1 and (i >= 2 or not isinstance(b, int) or b >= 1):
                        copy_pt(act, g - 2, (H + i - 2) % H)
                    if upright and i == 2 and (not isinstance(b, int) or b >= 1):
                        take(b - 1)
                    act.wait_ge(sem["m_ready"], g + 1)
                    if not isinstance(b, int) or g >= 4:
                        act.wait_ge(sem["pt_psum"], g - 3)
                    src = sc[:, i % 4, :] if mask else wide[0:S, i % 4, 0:SKV]
                    act.activation(pr[:, i % 4, 0:SKV], src, ACT.Exp, bias=nmx[:, i:i + 1], scale=SCALE).then_inc(sem["p_ready"], 1)
                    for what, n in pieces(b, i):
                        piece(what, n, 1 - slot)

                def finish():
                    copy_pt(act, B * H - 1, H - 1)
                    if upright:
                        take(B - 1)
                    piece("yt", PER * (B - 1) + len(FRONT) + TAIL.index("yt"), 1)

                walk(act, front, step, finish)

            @block.gpsimd
            def _(pool):
                def by_head(b, slot, first):
                    pool.wait_ge(sem["q_ready"], b + 1)
                    for m in range(KC):
                        last = pool.tensor_tensor(qm[:, slot, m], qt[:, m, :].unsqueeze(1).broadcast_to([P, HP, S]),
                                                  headmask[:].unsqueeze(2).broadcast_to([P, HP, S]), ALU.mult)
                    last.then_inc(sem["qm_ready"], 1)

                pool.memset(kt[:, :, :, SKV:PADKV], 0.0)
                pool.memset(pr[:, :, SKV:PADKV], 0.0)
                pool.memset(v1[:], 0.0)
                pool.drain()
                pool.memset(v1[:, :, :, :, D:D + 1], 1.0).then_inc(sem["cleared"], 1)
                pool.wait_ge(sem["loaded"], n_loaded)
                by_pairs(pool, B, by_head)

            @block.vector
            def _(dve):
                norm_stats_vector(dve, net, sem["var_ready"], sem["std_ready"])
                dve.wait_ge(sem["loaded"], n_loaded)
                dve.wait_ge(sem["cleared"], 1)
                if gate:
                    dve.tensor_reduce(gates[:], energy[:], X_AX, ALU.add, apply_absolute_value=True)
                    dve.drain()
                    dve.tensor_scalar(gsum[:], gates[:], 10.0 / 8, -10.0 * 0.1, ALU.mult, ALU.add).then_inc(sem["gate_sum"], 1)
                    dve.wait_ge(sem["gate_ready"], 1)

                def normal(b, slot):
                    normalise(dve, net, xn[:], b).then_inc(sem["xn_ready"], 1)
                    if mask:
                        dve.wait_ge(ctx_loaded[slot], (b - slot) * (per_ctx // 2) + per_ctx)
                        dve.tensor_scalar(bias[:, slot, :], words[:, slot, :].bitcast(mask[1])[:, 0:SKV], 0.0, NEG,
                                          ALU.is_equal, ALU.mult).then_inc(sem["mask_used"], 1)

                def piece(what, n, b, slot):
                    if what == "xt":
                        normal(b, slot)
                    elif what == "q":
                        dve.wait_ge(sem["side_psum"], n + 1)
                        out_q = qraw if rope else qt
                        for m in range(KC):
                            if biases:
                                last = dve.tensor_scalar(out_q[:, m, :], side[:, m * S:(m + 1) * S], bq[:, m:m + 1], None, ALU.add)
                            else:
                                last = dve.tensor_copy(out_q[:, m, :], side[:, m * S:(m + 1) * S])
                        last.then_inc(sem["side_done"], 1)
                        if not rope:
                            dve.drain()
                            dve.memset(mark[:], 0.0).then_inc(sem["q_ready"], 1)
                    elif what == "qswap":
                        dve.drain()
                        for m in range(KC):
                            dve.tensor_tensor(qt[:, m, :], qraw[:, m, :], cos[:, 0:S], ALU.mult)
                        dve.wait_ge(sem["side_psum"], n + 1)
                        for m in range(KC):
                            last = dve.tensor_tensor(qsin[:, m, :], side[:, m * S:(m + 1) * S], sin[:, 0:S], ALU.mult)
                        last.then_inc(sem["side_done"], 1)
                        dve.drain()
                        dve.tensor_tensor(qt[:], qt[:], qsin[:], ALU.add).then_inc(sem["q_ready"], 1)
                    elif what in ("k0swap", "k1swap"):
                        m = int(what[1])
                        dve.wait_ge(sem["side_psum"], n + 1)
                        dve.tensor_tensor(ksin[:], side[:, 0:SKV], sin[:], ALU.mult).then_inc(sem["side_done"], 1)
                        dve.tensor_tensor(kt[:, slot, m, 0:SKV], kraw[:, m, :], cos[:], ALU.mult)
                        dve.drain()
                        dve.tensor_tensor(kt[:, slot, m, 0:SKV], kt[:, slot, m, 0:SKV], ksin[:], ALU.add)
                        dve.drain()
                    elif what in ("v0", "v1"):
                        dve.wait_ge(sem["side_psum"], n + 1)
                        for c in (0, 1) if what == "v0" else (2,):
                            rows = CH if c < NCH - 1 else LAST
                            got = side[0:rows, (c % 2) * E:(c % 2 + 1) * E].rearrange("s (h d) -> s h d", h=H)
                            dst = v1[0:rows, slot, c, :, 0:D]
                            if biases:
                                last = dve.tensor_tensor(dst, got, bv[0:rows, :].rearrange("s (h d) -> s h d", h=H), ALU.add)
                            else:
                                last = dve.tensor_copy(dst, got)
                        last.then_inc(sem["side_done"], 1)
                        if gate:
                            dve.drain()
                            for c in (0, 1) if what == "v0" else (2,):
                                rows = CH if c < NCH - 1 else LAST
                                dst = v1[0:rows, slot, c, :, 0:D]
                                last = dve.tensor_scalar(dst, dst, gates[0:rows, bass.ds(b * NCH + c, 1)], None, ALU.mult)
                        if what == "v1":
                            dve.drain()
                            dve.tensor_copy(delta[0:1, 0:1], xn[0:1, 0:1]).then_inc(sem["front_ready"], 1)
                    elif what == "back":
                        dve.wait_ge(sem["side_psum"], n + 1)
                        divide(side[0:S, 0:H * V]).then_inc(sem["side_done"], 1)
                    elif what == "out":
                        dve.wait_ge(sem["side_psum"], n + 1)
                        if bo is not None:
                            dve.tensor_tensor(delta[:], side[0:S, 0:E], bo[0:S, :], ALU.add).then_inc(sem["side_done"], 1)
                            dve.drain()
                            dve.tensor_tensor(net.x[:, b, :], net.x[:, b, :], delta[:], ALU.add)
                        else:
                            dve.tensor_tensor(net.x[:, b, :], net.x[:, b, :], side[0:S, 0:E], ALU.add).then_inc(sem["side_done"], 1)
                        dve.drain()

                def front(b, slot, listed):
                    for what, n in listed:
                        piece(what, n, b, slot)

                def divide(bank):
                    got = bank.rearrange("s (h d) -> s h d", h=H)
                    dve.reciprocal(rs[:].unsqueeze(2), got[:, :, D:D + 1])
                    dve.drain()
                    return dve.tensor_tensor(y[:], got[:, :, 0:D], rs[:].unsqueeze(2).broadcast_to([S, H, D]), ALU.mult)

                def divide_batch(b):
                    dve.wait_ge(sem["y_psum"], (b + 1) * H)
                    divide(summed[0:S, 0:H * V]).then_inc(sem["y_ready"], 1)

                def step(b, slot, i):
                    g = b * H + i
                    dve.wait_ge(sem["s_psum"], g + 1)
                    if mask:
                        if not isinstance(b, int) or g >= 4:
                            dve.wait_ge(sem["p_ready"], g - 3)
                        dve.memset(mx[0:1, i:i + 1], 0.0)
                        dve.drain()
                        dve.tensor_tensor_reduce(sc[:, i % 4, :], wide[0:S, i % 4, 0:SKV], bias[:, slot, :], 1.0, -3e38,
                                                 ALU.add, ALU.max, mx[:, i:i + 1])
                    else:
                        dve.tensor_reduce(mx[:, i:i + 1], wide[0:S, i % 4, 0:SKV], X_AX, ALU.max)
                    dve.drain()
                    dve.tensor_scalar(nmx[:, i:i + 1], mx[:, i:i + 1], -SCALE, None, ALU.mult).then_inc(sem["m_ready"], 1)
                    if not upright and i == 3 and (not isinstance(b, int) or b >= 1):
                        divide_batch(b - 1)
                    if i % 2 == 0 and (i >= 2 or not isinstance(b, int) or b >= 1):
                        copy_pt(dve, g - 2, (H + i - 2) % H)
                    for what, n in pieces(b, i):
                        if what in TAIL:
                            piece(what, n, b - 1, 1 - slot)
                        else:
                            piece(what, n, b + 1, 1 - slot)

                def finish():
                    copy_pt(dve, B * H - 2, H - 2)
                    if upright:
                        piece("back", PER * (B - 1) + len(FRONT), B - 1, 1)
                    else:
                        divide_batch(B - 1)
                    piece("out", PER * (B - 1) + len(FRONT) + TAIL.index("out"), B - 1, 1)

                walk(dve, front, step, finish)


def top_two_vector(dve, net, t, gap_ready, exp_ready, both=None, both_ready=None):
    for b in range(B):
        dve.max(t.top[:, b, :], t.logits[:, b, :])
    dve.drain()
    for b in range(B):
        dve.max_index(t.which[:, b, :], t.top[:, b, :], t.logits[:, b, :])
    dve.tensor_tensor(t.gap[:], t.top[:, :, 1:2], t.top[:, :, 0:1], ALU.subtract).then_inc(gap_ready, 1)
    dve.drain()
    dve.tensor_copy(t.whichf[:], t.which[:, :, 0:2])
    dve.drain()
    for k in range(2):
        dve.tensor_tensor(t.hot[k][:], t.whichf[:, :, k:k + 1].broadcast_to([S, B, NE]), t.iota[:], ALU.is_equal)
    if both is not None:
        dve.drain()
        dve.tensor_tensor(both[:], t.hot[0][:], t.hot[1][:], ALU.add).then_inc(both_ready, 1)
    dve.wait_ge(exp_ready, 1)
    dve.tensor_scalar(t.den[:], t.exp[:], 1.0, None, ALU.add)
    dve.drain()
    dve.reciprocal(t.prob[0][:], t.den[:])
    dve.drain()
    dve.tensor_tensor(t.prob[1][:], t.exp[:], t.prob[0][:], ALU.mult)
    dve.drain()


class TopTwo:

    def __init__(self, sb):
        self.logits = sb("logits", [S, B, NE])
        self.top = sb("top", [S, B, 8])
        self.which = sb("which", [S, B, 8], U32)
        self.whichf = sb("whichf", [S, B, 2])
        self.gap = sb("gap", [S, B, 1])
        self.exp = sb("exp", [S, B, 1])
        self.den = sb("den", [S, B, 1])
        self.prob = [sb(f"prob{k}", [S, B, 1]) for k in range(2)]
        self.hot = [sb(f"hot{k}", [S, B, NE]) for k in range(2)]
        self.iota = sb("iota", [S, B, NE])


@sublayer
def l0_ffn(net):
    nc, dram = net.nc, net.dram
    NEX = NE + 1
    SLOTS = 3
    ROUNDS = NEX // SLOTS
    HALF = B * S // 2
    with ExitStack() as ctx:
        def sb(n, shape, dt=F32):
            return ctx.enter_context(nc.sbuf_tensor("l0f_" + n, shape, dt))

        w1 = sb("w1", [P, SLOTS, KC, P])
        w2 = sb("w2", [P, SLOTS, E])
        wr = sb("wr", [P, KC, NE])
        t = TopTwo(sb)
        pairs = [(wr[:], dram["l0f_wr"]), (t.iota[:], dram["iota8"])]
        n_loaded = 16 * len(pairs)
        per_expert = 32
        xn = sb("xn", [S, 2, E])
        xt = sb("xt", [P, KC, B * S])
        combine = sb("combine", [S, NEX, B])
        part = sb("part", [S, B, NE])
        weight = sb("weight", [S, B])
        relu = sb("relu", [P, 2, HALF])
        hidden = sb("hidden", [P, SLOTS, B * S])
        sem = {n: net.sem("l0f_" + n) for n in (
            "loaded", "w0", "w1", "w2", "var_ready", "std_ready", "xn_ready", "xt_psum", "xt_ready", "l_psum",
            "gap_ready", "exp_ready", "h_psum", "h_ready", "y_psum", "y_added")}
        wide, turned, summed = net.wide, net.turned, net.summed
        banks = [summed[0:S, 0, 0:E], summed[0:S, 1, 0:E], turned[0:S, 0, 0:E], turned[0:S, 1, 0:E]]
        w_loaded = [sem[f"w{i}"] for i in range(SLOTS)]

        with nc.Block() as block:
            @block.sync
            def _(sp):
                load_weights(sp, net, pairs, sem["loaded"])

                def load_expert(e, slot):
                    sp.dma_start(w1[:, slot], dram["l0f_w1"][e]).then_inc(w_loaded[slot], 16)
                    sp.dma_start(w2[:, slot], dram["l0f_w2"][e]).then_inc(w_loaded[slot], 16)

                for slot in range(SLOTS):
                    load_expert(slot, slot)
                with sp.Fori(1, ROUNDS) as r:
                    for slot in range(SLOTS):
                        sp.wait_ge(sem["y_psum"], (SLOTS * (r - 1) + slot + 1) * B)
                        load_expert(SLOTS * r + slot, slot)

            @block.tensor
            def _(pe):
                for b in range(B):
                    pe.wait_ge(sem["xn_ready"], b + 1)
                    if b >= 2:
                        pe.wait_ge(sem["xt_ready"], b - 1)
                    for k in range(KC):
                        last = pe.transpose(turned[:, b % 2, k * S:(k + 1) * S], xn[:, b % 2, k * P:(k + 1) * P], net.ident[0:S, 0:S])
                    last.then_inc(sem["xt_psum"], 1)
                pe.wait_ge(sem["loaded"], n_loaded)
                for b in range(B):
                    pe.wait_ge(sem["xt_ready"], b + 1)
                    for k in range(KC):
                        last = pe.matmul(summed[0:S, 0, b * NE:(b + 1) * NE], xt[:, k, b * S:(b + 1) * S], wr[:, k, :],
                                         start=k == 0, stop=k == KC - 1)
                last.then_inc(sem["l_psum"], 1)

                def first_layer(r, slot):
                    e = SLOTS * r + slot
                    pe.wait_ge(w_loaded[slot], per_expert * (r + 1))
                    for half in range(2):
                        pe.wait_ge(sem["h_ready"], 2 * e + half + 1)
                        for k in range(KC):
                            last = pe.matmul(wide[:, (2 * slot + half) % 4, 0:HALF], w1[:, slot, k, :],
                                             xt[:, k, half * HALF:(half + 1) * HALF], start=k == 0, stop=k == KC - 1)
                        last.then_inc(sem["h_psum"], 1)

                with pe.Fori(0, ROUNDS) as r:
                    first_layer(r, 0)
                    for slot in range(SLOTS):
                        e = SLOTS * r + slot
                        if slot + 1 < SLOTS:
                            first_layer(r, slot + 1)
                        pe.wait_ge(sem["h_ready"], 2 + 2 * (e + 1))
                        for b in range(B):
                            pe.wait_ge(sem["y_added"], e * B + b + 1)
                            pe.matmul(banks[b % 4], hidden[:, slot, b * S:(b + 1) * S], w2[:, slot, :],
                                      start=True, stop=True).then_inc(sem["y_psum"], 1)

            @block.scalar
            def _(act):
                norm_stats_scalar(act, net, sem["var_ready"], sem["std_ready"])
                for b in range(B):
                    act.wait_ge(sem["xt_psum"], b + 1)
                    act.activation(xt[:, :, b * S:(b + 1) * S], turned[:, b % 2, 0:KC * S].rearrange("p (k s) -> p k s", k=KC),
                                   ACT.Copy).then_inc(sem["xt_ready"], 1)
                act.wait_ge(sem["gap_ready"], 1)
                act.activation(t.exp[:], t.gap[:], ACT.Exp).then_inc(sem["exp_ready"], 1)

                act.drain()
                act.activation(relu[0:1, 0, 0:1], t.exp[0:1, 0, :], ACT.Copy).then_inc(sem["h_ready"], 2)
                act.drain()
                with act.Fori(0, ROUNDS) as r:
                    for slot in range(SLOTS):
                        for half in range(2):
                            act.wait_ge(sem["h_psum"], 2 * (SLOTS * r + slot) + half + 1)
                            act.activation(relu[:, half, :], wide[:, (2 * slot + half) % 4, 0:HALF], ACT.Relu)
                            act.drain()
                            act.activation(hidden[:, slot, half * HALF:(half + 1) * HALF], relu[:, half, :], ACT.Square).then_inc(sem["h_ready"], 1)

            @block.vector
            def _(dve):
                norm_stats_vector(dve, net, sem["var_ready"], sem["std_ready"])
                for b in range(B):
                    if b >= 2:
                        dve.wait_ge(sem["xt_psum"], b - 1)
                    normalise(dve, net, xn[:, b % 2, :], b).then_inc(sem["xn_ready"], 1)
                dve.wait_ge(sem["loaded"], n_loaded)
                dve.wait_ge(sem["l_psum"], 1)
                dve.tensor_copy(t.logits[:], summed[0:S, 0, 0:B * NE].rearrange("s (b e) -> s b e", b=B))
                dve.drain()
                top_two_vector(dve, net, t, sem["gap_ready"], sem["exp_ready"])
                for k in range(2):
                    dve.tensor_scalar(t.prob[k][:], t.prob[k][:], 1.0, None, ALU.is_ge)
                dve.drain()
                dve.tensor_tensor(part[:], t.hot[0][:], t.prob[0][:].broadcast_to([S, B, NE]), ALU.mult)
                dve.tensor_tensor(t.hot[1][:], t.hot[1][:], t.prob[1][:].broadcast_to([S, B, NE]), ALU.mult)
                dve.memset(combine[:, NE:NEX, :], 1.0)
                dve.drain()
                dve.tensor_tensor(combine[:, 0:NE, :].rearrange("s e b -> s b e"), part[:], t.hot[1][:], ALU.add)
                dve.drain()
                dve.memset(part[0:1, 0, 0:1], 0.0).then_inc(sem["y_added"], len(banks))
                dve.drain()

                with dve.Fori(0, ROUNDS) as r:
                    for slot in range(SLOTS):
                        e = SLOTS * r + slot
                        dve.tensor_copy(weight[:], combine[:, e, :])
                        dve.drain()
                        for b in range(B):
                            dve.wait_ge(sem["y_psum"], e * B + b + 1)
                            dve.scalar_tensor_tensor(out=net.x[:, b, :], in0=banks[b % 4], scalar=weight[:, b:b + 1],
                                                     in1=net.x[:, b, :], op0=ALU.mult, op1=ALU.add).then_inc(sem["y_added"], 1)
                        dve.drain()


@sublayer
def l1_attn(net):
    nc, dram = net.nc, net.dram
    H, D, G = 16, 16, 4
    HP, NG = P // D, H // G
    with ExitStack() as ctx:
        def sb(n, shape, dt=F32):
            return ctx.enter_context(nc.sbuf_tensor("l1a_" + n, shape, dt))

        wqk, wv, wo = sb("wqk", [P, KC, 2 * E]), sb("wv", [P, KC, E]), sb("wo", [P, KC, E])
        bqk, bv, bo = sb("bqk", [S, 2 * E]), sb("bv", [S, E]), sb("bo", [S, E])
        headmask = sb("headmask", [P, HP])
        pairs = [(wqk[:], dram["l1a_wqk"]), (wv[:], dram["l1a_wv"]), (wo[:], dram["l1a_wo"]), (headmask[:], dram["headmask16"]),
                 (bqk[:], dram["l1a_bqk"].partition_broadcast(S)), (bv[:], dram["l1a_bv"].partition_broadcast(S)),
                 (bo[:], dram["l1a_bo"].partition_broadcast(S))]
        n_loaded = 16 * len(pairs)
        xn = sb("xn", [S, 2, E])
        xt = sb("xt", [P, KC, B, S])
        qk = sb("qk", [S, B, 2 * E])
        sq = sb("sq", [S, B, 2 * E])
        unit = sb("unit", [S, 2 * E])
        norm = sb("norm", [S, B, 2 * H])
        qkt = sb("qkt", [P, 2 * KC, S])
        km = sb("km", [P, KC, HP, S])
        v1 = sb("v1", [S, B, H, D + 1])
        shift = sb("shift", [S, 1])
        num, den, wt = sb("num", [S, H, S]), sb("den", [S, H, S]), sb("wt", [S, H, S])
        rs = sb("rs", [S, H])
        y = sb("y", [S, H, D])
        yt = sb("yt", [P, KC, S])
        delta = sb("delta", [S, E])
        sem = {n: net.sem("l1a_" + n) for n in (
            "loaded", "var_ready", "std_ready", "xn_ready", "xt_psum", "xt_ready", "qkv_psum", "qkv_ready", "sq_ready", "sum_ready",
            "root_ready", "qk_ready", "qkt_psum", "qkt_ready", "heads0_ready", "heads1_ready", "cos_psum", "den_ready", "wt_ready", "y_psum", "y_ready",
            "yt_psum", "yt_ready", "out_psum")}
        wide, turned, summed = net.wide, net.turned, net.summed

        def in_order(engine, step):
            step(0)
            with engine.Fori(1, B - 2) as b:
                step(b)
            step(B - 2)
            step(B - 1)

        def exists(b):
            return not isinstance(b, int) or 0 <= b < B

        def by_head(engine, m):
            return engine.tensor_tensor(km[:, m], qkt[:, KC + m, :].unsqueeze(1).broadcast_to([P, HP, S]),
                                        headmask[:].unsqueeze(2).broadcast_to([P, HP, S]), ALU.mult)

        with nc.Block() as block:
            @block.sync
            def _(sp):
                load_weights(sp, net, pairs, sem["loaded"])

            @block.tensor
            def _(pe):
                def turn_x(b, slot, first):
                    pe.wait_ge(sem["xn_ready"], b + 1)
                    if not first:
                        pe.wait_ge(sem["xt_ready"], b - 1)
                    for k in range(KC):
                        last = pe.transpose(turned[:, slot, k * S:(k + 1) * S], xn[:, slot, k * P:(k + 1) * P], net.ident[0:S, 0:S])
                    last.then_inc(sem["xt_psum"], 1)

                by_pairs(pe, B, turn_x)
                pe.wait_ge(sem["loaded"], n_loaded)
                for b in range(B):
                    pe.wait_ge(sem["xt_ready"], b + 1)
                    if b >= 2:
                        pe.wait_ge(sem["qkv_ready"], b - 1)
                    for w, out in ((wqk, wide[0:S, b % 2, :]), (wv, wide[0:S, 2 + b % 2, 0:E])):
                        for k in range(KC):
                            last = pe.matmul(out, xt[:, k, b, :], w[:, k, :], start=k == 0, stop=k == KC - 1)
                    last.then_inc(sem["qkv_psum"], 1)

                def turn_qk(b):
                    pe.wait_ge(sem["qk_ready"], b + 1)
                    for c in range(2 * KC):
                        last = pe.transpose(turned[:, 0, c * S:(c + 1) * S],
                                            unit[:, c * P:(c + 1) * P], net.ident[0:S, 0:S])
                    last.then_inc(sem["qkt_psum"], 1)

                def cosines(b, g):
                    if g % (NG // KC) == 0:
                        pe.wait_ge(sem[f"heads{g // (NG // KC)}_ready"], b + 1)
                    for j in range(G):
                        h = g * G + j
                        last = pe.matmul(wide[0:S, g, j * S:(j + 1) * S], km[:, h // HP, h % HP, :], qkt[:, h // HP, :],
                                         start=True, stop=True)
                    last.then_inc(sem["cos_psum"], 1)

                def weigh(b, g):
                    if g == 0 and exists(b - 1):
                        pe.wait_ge(sem["y_ready"], b)
                    pe.wait_ge(sem["wt_ready"], b * NG + g + 1)
                    for h in range(g * G, g * G + G):
                        last = pe.matmul(summed[0:S, 0, h * (D + 1):(h + 1) * (D + 1)], wt[:, h, :],
                                         v1[:, bass.ds(b, 1), h, :].rearrange("s o d -> s (o d)"), start=True, stop=True)
                    if g == NG - 1:
                        last.then_inc(sem["y_psum"], 1)

                def turn_y(b):
                    pe.wait_ge(sem["y_ready"], b + 1)
                    for k in range(KC):
                        last = pe.transpose(turned[:, 1, k * S:(k + 1) * S],
                                            y[:].rearrange("s h d -> s (h d)")[:, k * P:(k + 1) * P], net.ident[0:S, 0:S])
                    last.then_inc(sem["yt_psum"], 1)

                def project(b):
                    pe.wait_ge(sem["yt_ready"], b + 1)
                    for k in range(KC):
                        last = pe.matmul(summed[0:S, 1, 0:E], yt[:, k, :], wo[:, k, :], start=k == 0, stop=k == KC - 1)
                    last.then_inc(sem["out_psum"], 1)

                def step(b):
                    for g in range(NG):
                        weigh(b, g)
                        if exists(b + 1):
                            cosines(b + 1, g)
                        if exists(b - 1) and g == 0:
                            turn_y(b - 1)
                        if exists(b - 1) and g == 2:
                            project(b - 1)
                    if exists(b + 2):
                        turn_qk(b + 2)

                turn_qk(0)
                for g in range(NG):
                    cosines(0, g)
                turn_qk(1)
                in_order(pe, step)
                turn_y(B - 1)
                project(B - 1)

            @block.scalar
            def _(act):
                norm_stats_scalar(act, net, sem["var_ready"], sem["std_ready"])

                def copy_xt(b, slot, first):
                    act.wait_ge(sem["xt_psum"], b + 1)
                    act.activation(xt[:, :, bass.ds(b, 1), :].rearrange("p k o s -> p k (o s)"),
                                   turned[:, slot, 0:KC * S].rearrange("p (k s) -> p k s", k=KC), ACT.Copy).then_inc(sem["xt_ready"], 1)

                by_pairs(act, B, copy_xt)
                with act.Fori(0, B) as b:
                    act.wait_ge(sem["qkv_ready"], b + 1)
                    act.activation(sq[:, b, :], qk[:, b, :], ACT.Square).then_inc(sem["sq_ready"], 1)
                act.wait_ge(sem["sum_ready"], 1)
                act.activation(norm[:], norm[:], ACT.Sqrt).then_inc(sem["root_ready"], 1)

                def copy_qkt(b):
                    act.wait_ge(sem["qkt_psum"], b + 1)
                    act.activation(qkt[:], turned[:, 0, 0:2 * KC * S].rearrange("p (k s) -> p k s", k=2 * KC), ACT.Copy).then_inc(sem["qkt_ready"], 1)

                def logarithm(b, g):
                    act.wait_ge(sem["cos_psum"], b * NG + g + 1)
                    act.activation(den[:, g * G:(g + 1) * G, :], wide[0:S, g, 0:G * S].rearrange("s (j t) -> s j t", j=G),
                                   ACT.Ln, bias=shift[:], scale=-1.0)

                def scores(groups):
                    act.drain()
                    for g in groups:
                        got = wide[0:S, g, 0:G * S].rearrange("s (j t) -> s j t", j=G)
                        one = den[:, g * G:(g + 1) * G, :]
                        act.activation(num[:, g * G:(g + 1) * G, :], got, ACT.Square, bias=1.0)
                        act.activation(one, one, ACT.Exp, scale=-1.0).then_inc(sem["den_ready"], 1)

                def copy_yt(b):
                    act.wait_ge(sem["yt_psum"], b + 1)
                    act.activation(yt[:], turned[:, 1, 0:KC * S].rearrange("p (k s) -> p k s", k=KC), ACT.Copy).then_inc(sem["yt_ready"], 1)

                def step(b):
                    for g in range(NG):
                        if exists(b + 1):
                            logarithm(b + 1, g)
                        if exists(b - 1) and g == 0:
                            copy_yt(b - 1)
                        if exists(b + 2) and g == NG - 1:
                            copy_qkt(b + 2)
                        if exists(b + 1) and g % 2:
                            scores((g - 1, g))

                copy_qkt(0)
                for g in range(NG):
                    logarithm(0, g)
                copy_qkt(1)
                scores(range(NG))
                in_order(act, step)
                copy_yt(B - 1)

            @block.gpsimd
            def _(pool):
                pool.wait_ge(sem["loaded"], n_loaded)
                with pool.Fori(0, B) as b:
                    pool.wait_ge(sem["qkt_ready"], b + 1)
                    by_head(pool, 1).then_inc(sem["heads1_ready"], 1)

            @block.vector
            def _(dve):
                dve.memset(v1[:, :, :, D:D + 1], 1.0)
                dve.memset(shift[:], 1.1)
                norm_stats_vector(dve, net, sem["var_ready"], sem["std_ready"])

                def normal(b, slot, first):
                    if not first:
                        dve.wait_ge(sem["xt_psum"], b - 1)
                    normalise(dve, net, xn[:, slot, :], b).then_inc(sem["xn_ready"], 1)

                def take(b, slot, first):
                    dve.wait_ge(sem["qkv_psum"], b + 1)
                    dve.tensor_tensor(qk[:, bass.ds(b, 1), :].rearrange("s o n -> s (o n)"), wide[0:S, slot, :], bqk[:], ALU.add)
                    dve.tensor_tensor(v1[:, bass.ds(b, 1), :, 0:D].rearrange("s o h d -> s (o h) d"),
                                      wide[0:S, 2 + slot, 0:E].rearrange("s (h d) -> s h d", h=H),
                                      bv[:].rearrange("s (h d) -> s h d", h=H), ALU.add).then_inc(sem["qkv_ready"], 1)

                by_pairs(dve, B, normal)
                dve.wait_ge(sem["loaded"], n_loaded)
                by_pairs(dve, B, take)
                with dve.Fori(0, B) as b:
                    dve.wait_ge(sem["sq_ready"], b + 1)
                    last = dve.tensor_reduce(norm[:, b, :], sq[:, b, :].rearrange("s (h d) -> s h d", d=D), X_AX, ALU.add)
                dve.drain()
                dve.memset(delta[0:1, 0:1], 0.0).then_inc(sem["sum_ready"], 1)
                dve.wait_ge(sem["root_ready"], 1)
                dve.tensor_scalar(norm[:], norm[:], 1e-8, None, ALU.add)
                dve.drain()
                dve.reciprocal(norm[:], norm[:])
                dve.drain()

                def shorten(b):
                    if not (isinstance(b, int) and b == 0):
                        dve.wait_ge(sem["qkt_psum"], b)
                    dve.tensor_tensor(unit[:].rearrange("s (h d) -> s h d", d=D), qk[:, bass.ds(b, 1), :].rearrange("s o (h d) -> s (o h) d", d=D),
                                      norm[:, bass.ds(b, 1), :].rearrange("s o h -> s (o h)").unsqueeze(2).broadcast_to([S, 2 * H, D]),
                                      ALU.mult).then_inc(sem["qk_ready"], 1)

                def lower_heads(b):
                    dve.wait_ge(sem["qkt_ready"], b + 1)
                    by_head(dve, 0).then_inc(sem["heads0_ready"], 1)

                def weights(b, groups):
                    for g in groups:
                        dve.wait_ge(sem["den_ready"], b * NG + g + 1)
                        dve.tensor_tensor(wt[:, g * G:(g + 1) * G, :], den[:, g * G:(g + 1) * G, :], num[:, g * G:(g + 1) * G, :],
                                          ALU.mult).then_inc(sem["wt_ready"], 1)

                def divide(b):
                    dve.wait_ge(sem["y_psum"], b + 1)
                    got = summed[0:S, 0, 0:H * (D + 1)].rearrange("s (h d) -> s h d", h=H)
                    dve.tensor_scalar(rs[:].unsqueeze(2), got[:, :, D:D + 1], 1e-6, None, ALU.add)
                    dve.drain()
                    dve.reciprocal(rs[:], rs[:])
                    dve.drain()
                    dve.tensor_tensor(y[:], got[:, :, 0:D], rs[:].unsqueeze(2).broadcast_to([S, H, D]), ALU.mult).then_inc(sem["y_ready"], 1)

                def add(b):
                    dve.wait_ge(sem["out_psum"], b + 1)
                    dve.tensor_tensor(delta[:], summed[0:S, 1, 0:E], bo[:], ALU.add)
                    dve.drain()
                    dve.tensor_tensor(net.x[:, b, :], net.x[:, b, :], delta[:], ALU.add)
                    dve.drain()

                def step(b):
                    if exists(b + 2):
                        shorten(b + 2)
                    if exists(b + 1):
                        weights(b + 1, range(NG // 2))
                    if exists(b - 1):
                        add(b - 1)
                    divide(b)
                    if exists(b + 2):
                        lower_heads(b + 2)
                    if exists(b + 1):
                        weights(b + 1, range(NG // 2, NG))

                for b in range(2):
                    shorten(b)
                    lower_heads(b)
                weights(0, range(NG))
                in_order(dve, step)
                add(B - 1)


@sublayer
def l1_ffn(net):
    nc, dram = net.nc, net.dram
    F = 1024
    FC = F // P
    TOP = 2
    RT = 2
    CR = RT * S
    MOST = B * S // CR
    NT = (TOP * B * S + NE * (CR - 1)) // CR
    SLOTS = 2
    W1, W2 = KC * F, FC * E
    WORDS = W1 + W2 + FC
    UNITS = B * S // CR
    with ExitStack() as ctx:
        def sb(n, shape, dt=F32):
            return ctx.enter_context(nc.sbuf_tensor("l1f_" + n, shape, dt))

        pack = sb("pack", [P, SLOTS, WORDS])
        shared = sb("shared", [P, WORDS])
        wr = sb("wr", [P, KC, NE])
        before, ones = sb("before", [S, S]), sb("ones", [S, P])
        br, b2s, b2 = sb("br", [S, NE]), sb("b2s", [S, E]), sb("b2", [S, SLOTS, E])
        tiles, partition = sb("tiles", [P, NT]), sb("partition", [P, NT])
        t = TopTwo(sb)
        pairs = [(wr[:], dram["l1f_wr"]), (t.iota[:], dram["iota8"]), (before[:], dram["before"]),
                 (br[:], dram["l1f_br"].partition_broadcast(S)), (b2s[:], dram["l1f_b2s"].partition_broadcast(S)),
                 (tiles[:], dram["l1f_tiles"]), (partition[:], dram["l1f_partition"])]
        n_loaded = 16 * len(pairs)
        zeros = sb("zeros", [S, E])
        xn = sb("xn", [S, B, E])
        xt = sb("xt", [P, KC, B * S])
        both = sb("both", [S, B, NE])
        total = sb("total", [P, B, NE])
        start = sb("start", [P, B + 1, NE])
        beyond = sb("beyond", [P, MOST, NE])
        held = sb("held", [P, NE])
        first = sb("first", [P, NE])
        first_row = sb("first_row", [S, NE])
        passed = sb("passed", [P, NT, NE - 1])
        expert = sb("expert", [P, NT])
        packi, experti = sb("packi", [P, NT], U32), sb("experti", [S, NT], U32)
        rank = sb("rank", [S, B, NE])
        mine = sb("mine", [S, B, NE])
        place = sb("place", [S, TOP, B])
        placei = sb("placei", [S, TOP * B], U32)
        rows = sb("rows", [S, SLOTS, RT, E])
        rt = sb("rt", [P, KC, CR])
        hidden = sb("hidden", [P, FC, CR])
        plus = sb("plus", [S, RT, E])
        out = sb("out", [S, SLOTS, RT, E])
        back = sb("back", [S, TOP * B, E])
        sorted_x = nc.dram_tensor("l1f_sorted_x", (NT * CR, E), F32).ap()
        sorted_y = nc.dram_tensor("l1f_sorted_y", (NT * CR, E), F32).ap()
        sem = {n: net.sem("l1f_" + n) for n in (
            "loaded", "shared_loaded", "w0", "w1", "r0", "r1", "zeros_ready", "cleared", "var_ready", "std_ready", "xn_ready",
            "xt_psum", "xt_ready", "l_psum", "gap_ready", "exp_ready", "both_ready", "count_psum", "tiles_ready", "place_ready",
            "scattered", "sh_psum", "sh_ready", "sy_psum", "sy_added", "rt_psum", "rt_ready", "h_psum", "h_ready",
            "y_psum", "y_ready", "stored0", "stored1", "gathered")}
        wide, turned, summed = net.wide, net.turned, net.summed
        w_loaded, r_loaded = (sem["w0"], sem["w1"]), (sem["r0"], sem["r1"])
        stored = (sem["stored0"], sem["stored1"])

        def by_tiles(engine, body):
            by_pairs(engine, NT // 2 * 2, body)
            if NT % 2:
                body(NT - 1, (NT - 1) % 2, False)

        def w1_of(w, k, f):
            return w[:, k * F + f * P:k * F + (f + 1) * P]

        def w2_of(w, f):
            return w[:, W1 + f * E:W1 + (f + 1) * E]

        def b1_of(w, f):
            return w[:, W1 + W2 + f:W1 + W2 + f + 1]

        with nc.Block() as block:
            @block.sync
            def _(sp):
                load_weights(sp, net, pairs, sem["loaded"])
                sp.dma_start(shared[:], dram["l1f_shared"]).then_inc(sem["shared_loaded"], 16)
                sp.wait_ge(sem["zeros_ready"], 1)
                with sp.Fori(0, NT) as n:
                    sp.dma_start(sorted_x.rearrange("(n r s) d -> n s r d", r=RT, s=S)[n],
                                 zeros[:].unsqueeze(1).broadcast_to([S, RT, E])).then_inc(sem["cleared"], 16)
                sp.wait_ge(sem["scattered"], 16 * TOP * B)

                def load_rows(n, slot, is_first):
                    if not is_first:
                        sp.wait_ge(sem["rt_psum"], n - 1)
                    sp.dma_start(rows[:, slot], sorted_x.rearrange("(n r s) d -> n s r d", r=RT, s=S)[n]).then_inc(r_loaded[slot], 16)

                by_tiles(sp, load_rows)

            @block.gpsimd
            def _(pool):
                def load_pack(n):
                    pool.indirect_dma_start(out=pack[:, n % 2, :], out_offset=None, in_=dram["l1f_pack"],
                                            in_offset=bass.IndirectOffsetOnAxis(ap=packi[:, n:n + 1], axis=0)).then_inc(w_loaded[n % 2], 16)
                    pool.indirect_dma_start(out=b2[:, n % 2, :], out_offset=None, in_=dram["l1f_b2"],
                                            in_offset=bass.IndirectOffsetOnAxis(ap=experti[:, n:n + 1], axis=0)).then_inc(w_loaded[n % 2], 16)

                pool.wait_ge(sem["tiles_ready"], 1)
                load_pack(0)
                pool.wait_ge(sem["place_ready"], 1)
                pool.wait_ge(sem["cleared"], 16 * NT)
                for b in range(B):
                    for k in range(TOP):
                        pool.indirect_dma_start(out=sorted_x, out_offset=bass.IndirectOffsetOnAxis(ap=placei[:, k * B + b:k * B + b + 1], axis=0),
                                                in_=xn[:, b, :], in_offset=None).then_inc(sem["scattered"], 16)
                load_pack(1)
                for n in range(2, NT):
                    pool.wait_ge(sem["y_ready"], n - 1)
                    load_pack(n)
                for slot in range(SLOTS):
                    pool.wait_ge(stored[slot], 16 * ((NT + 1 - slot) // 2))
                for b in range(B):
                    for k in range(TOP):
                        pool.indirect_dma_start(out=back[:, k * B + b, :], out_offset=None, in_=sorted_y,
                                                in_offset=bass.IndirectOffsetOnAxis(ap=placei[:, k * B + b:k * B + b + 1], axis=0)
                                                ).then_inc(sem["gathered"], 16)

            @block.tensor
            def _(pe):
                for b in range(B):
                    pe.wait_ge(sem["xn_ready"], b + 1)
                    if b >= 2:
                        pe.wait_ge(sem["xt_ready"], b - 1)
                    for k in range(KC):
                        last = pe.transpose(turned[:, b % 2, k * S:(k + 1) * S], xn[:, b, k * P:(k + 1) * P], net.ident[0:S, 0:S])
                    last.then_inc(sem["xt_psum"], 1)
                pe.wait_ge(sem["loaded"], n_loaded)
                for b in range(B):
                    pe.wait_ge(sem["xt_ready"], b + 1)
                    for k in range(KC):
                        last = pe.matmul(summed[0:S, 0, b * NE:(b + 1) * NE], xt[:, k, b * S:(b + 1) * S], wr[:, k, :], start=k == 0, stop=k == KC - 1)
                last.then_inc(sem["l_psum"], 1)

                def first_layer(w, cols, done, read, before_it):
                    for f in range(FC):
                        if f >= 4:
                            pe.wait_ge(read, before_it + f - 3)
                        for k in range(KC):
                            last = pe.matmul(wide[:, f % 4, 0:CR], w1_of(w, k, f), cols(k), start=k == 0, stop=k == KC - 1)
                        last.then_inc(done, 1)

                def second_layer(w, banks, done):
                    for c in range(RT):
                        for f in range(FC):
                            last = pe.matmul(banks[0:S, c, 0:E], hidden[:, f, c * S:(c + 1) * S], w2_of(w, f), start=f == 0, stop=f == FC - 1)
                    last.then_inc(done, 1)

                def turn(n, slot):
                    pe.wait_ge(r_loaded[slot], 8 * (n - slot) + 16)
                    for c in range(RT):
                        for k in range(KC):
                            last = pe.transpose(turned[:, c, k * S:(k + 1) * S], rows[:, slot, c, k * P:(k + 1) * P], net.ident[0:S, 0:S])
                    last.then_inc(sem["rt_psum"], 1)

                pe.wait_ge(sem["shared_loaded"], 16)
                for u in range(UNITS):
                    first_layer(shared, lambda k: xt[:, k, u * CR:(u + 1) * CR], sem["sh_psum"], sem["sh_ready"], u * FC)
                    if u == 0:
                        pe.wait_ge(sem["both_ready"], 1)
                        chosen = both[:].rearrange("s b e -> s (b e)")
                        pe.matmul(summed[0:S, 1, 0:B * NE], before[:], chosen, start=True, stop=True)
                        pe.matmul(summed[:, 1, B * NE:2 * B * NE], ones[:], chosen, start=True, stop=True).then_inc(sem["count_psum"], 1)
                    pe.wait_ge(sem["sh_ready"], (u + 1) * FC)
                    if u >= 1:
                        pe.wait_ge(sem["sy_added"], u)
                    second_layer(shared, turned, sem["sy_psum"])
                pe.wait_ge(sem["sy_added"], UNITS)
                turn(0, 0)

                def tile(n, slot, is_first):
                    pe.wait_ge(w_loaded[slot], 16 * (n - slot) + 32)
                    pe.wait_ge(sem["rt_ready"], n + 1)
                    first_layer(pack[:, slot, :], lambda k: rt[:, k, :], sem["h_psum"], sem["h_ready"], n * FC)
                    if not (isinstance(n, int) and n == NT - 1):
                        turn(n + 1, 1 - slot)
                    pe.wait_ge(sem["h_ready"], (n + 1) * FC)
                    if not (isinstance(n, int) and n == 0):
                        pe.wait_ge(sem["y_ready"], n)
                    second_layer(pack[:, slot, :], summed, sem["y_psum"])

                by_tiles(pe, tile)

            @block.scalar
            def _(act):
                norm_stats_scalar(act, net, sem["var_ready"], sem["std_ready"])
                for b in range(B):
                    act.wait_ge(sem["xt_psum"], b + 1)
                    act.activation(xt[:, :, b * S:(b + 1) * S], turned[:, b % 2, 0:KC * S].rearrange("p (k s) -> p k s", k=KC), ACT.Copy).then_inc(sem["xt_ready"], 1)
                act.wait_ge(sem["shared_loaded"], 16)

                def gelu(w, n, done, read):
                    for f in range(FC):
                        act.wait_ge(done, n * FC + f + 1)
                        act.activation(hidden[:, f, :], wide[:, f % 4, 0:CR], ACT.Gelu, bias=b1_of(w, f)).then_inc(read, 1)

                for u in range(UNITS):
                    gelu(shared, u, sem["sh_psum"], sem["sh_ready"])
                    if u == 0:
                        act.wait_ge(sem["gap_ready"], 1)
                        act.activation(t.exp[:], t.gap[:], ACT.Exp).then_inc(sem["exp_ready"], 1)

                def copy_rt(n):
                    act.wait_ge(sem["rt_psum"], n + 1)
                    act.activation(rt[:].rearrange("p k (c s) -> p c k s", c=RT), turned[:, :, 0:KC * S].rearrange("p c (k s) -> p c k s", k=KC),
                                   ACT.Copy).then_inc(sem["rt_ready"], 1)

                copy_rt(0)

                def tile(n, slot, is_first):
                    act.wait_ge(w_loaded[slot], 16 * (n - slot) + 32)
                    gelu(pack[:, slot, :], n, sem["h_psum"], sem["h_ready"])
                    if not (isinstance(n, int) and n == NT - 1):
                        copy_rt(n + 1)
                    act.wait_ge(sem["y_ready"], n + 1)
                    act.dma_start(sorted_y.rearrange("(n r s) d -> n s r d", r=RT, s=S)[n], out[:, slot]).then_inc(stored[slot], 16)

                by_tiles(act, tile)

            @block.vector
            def _(dve):
                dve.memset(zeros[:], 0.0).then_inc(sem["zeros_ready"], 1)
                dve.memset(ones[:], 1.0)
                dve.memset(start[:, 0, :], 0.0)
                dve.memset(first[:, 0:1], 0.0)
                norm_stats_vector(dve, net, sem["var_ready"], sem["std_ready"])
                for b in range(B):
                    normalise(dve, net, xn[:, b, :], b).then_inc(sem["xn_ready"], 1)
                dve.wait_ge(sem["loaded"], n_loaded)
                dve.wait_ge(sem["l_psum"], 1)
                dve.tensor_tensor(t.logits[:], summed[0:S, 0, 0:B * NE].rearrange("s (b e) -> s b e", b=B),
                                  br[:].unsqueeze(1).broadcast_to([S, B, NE]), ALU.add)
                dve.drain()
                top_two_vector(dve, net, t, sem["gap_ready"], sem["exp_ready"], both, sem["both_ready"])
                dve.wait_ge(sem["count_psum"], 1)
                dve.tensor_copy(total[:], summed[:, 1, B * NE:2 * B * NE].rearrange("s (b e) -> s b e", b=B))
                dve.drain()
                for b in range(B):
                    dve.tensor_tensor(start[:, b + 1, :], start[:, b, :], total[:, b, :], ALU.add)
                    dve.drain()
                for m in range(MOST):
                    dve.tensor_scalar(beyond[:, m, :], start[:, B, :], float(m * CR), None, ALU.is_gt)
                dve.drain()
                dve.tensor_reduce(held[:], beyond[:].rearrange("p m e -> p e m"), X_AX, ALU.add)
                dve.drain()
                for e in range(NE - 1):
                    dve.tensor_tensor(first[:, e + 1:e + 2], first[:, e:e + 1], held[:, e:e + 1], ALU.add)
                    dve.drain()
                dve.tensor_tensor(passed[:], tiles[:].unsqueeze(2).broadcast_to([P, NT, NE - 1]),
                                  first[:, 1:NE].unsqueeze(1).broadcast_to([P, NT, NE - 1]), ALU.is_ge)
                dve.tensor_scalar(first_row[:], first[0:S, :], float(CR), None, ALU.mult)
                dve.drain()
                dve.tensor_reduce(expert[:], passed[:], X_AX, ALU.add)
                dve.tensor_tensor(rank[:], start[0:S, 0:B, :], summed[0:S, 1, 0:B * NE].rearrange("s (b e) -> s b e", b=B), ALU.add)
                dve.drain()
                dve.tensor_copy(experti[:], expert[0:S, :])
                dve.scalar_tensor_tensor(out=packi[:], in0=expert[:], scalar=float(P), in1=partition[:], op0=ALU.mult, op1=ALU.add)
                dve.drain()
                dve.tensor_tensor(rank[:], rank[:], first_row[:].unsqueeze(1).broadcast_to([S, B, NE]), ALU.add).then_inc(sem["tiles_ready"], 1)
                dve.drain()
                for k in range(TOP):
                    dve.tensor_tensor(mine[:], rank[:], t.hot[k][:], ALU.mult)
                    dve.drain()
                    dve.tensor_reduce(place[:, k, :], mine[:], X_AX, ALU.add)
                    dve.drain()
                dve.tensor_copy(placei[:], place[:].rearrange("s k b -> s (k b)")).then_inc(sem["place_ready"], 1)
                for u in range(UNITS):
                    dve.wait_ge(sem["sy_psum"], u + 1)
                    dve.tensor_tensor(plus[:], turned[0:S, :, 0:E], b2s[:].unsqueeze(1).broadcast_to([S, RT, E]), ALU.add).then_inc(sem["sy_added"], 1)
                    dve.drain()
                    dve.tensor_tensor(net.x[:, u * RT:(u + 1) * RT, :], net.x[:, u * RT:(u + 1) * RT, :], plus[:], ALU.add)
                    dve.drain()

                def tile(n, slot, is_first):
                    dve.wait_ge(w_loaded[slot], 16 * (n - slot) + 32)
                    if not is_first:
                        dve.wait_ge(stored[slot], 8 * (n - slot))
                    dve.wait_ge(sem["y_psum"], n + 1)
                    dve.tensor_tensor(out[:, slot], summed[0:S, :, 0:E], b2[:, slot, :].unsqueeze(1).broadcast_to([S, RT, E]),
                                      ALU.add).then_inc(sem["y_ready"], 1)

                by_tiles(dve, tile)
                dve.wait_ge(sem["gathered"], 16 * TOP * B)
                for k in range(TOP):
                    for b in range(B):
                        dve.scalar_tensor_tensor(out=net.x[:, b, :], in0=back[:, k * B + b, :], scalar=t.prob[k][:, b, :],
                                                 in1=net.x[:, b, :], op0=ALU.mult, op1=ALU.add)
                    dve.drain()


@sublayer
def l2_attn(net):
    nc, dram = net.nc, net.dram
    N = 2
    with ExitStack() as ctx:
        def sb(n, shape, dt=F32):
            return ctx.enter_context(nc.sbuf_tensor("l2a_" + n, shape, dt))

        par = {n: sb(n, [P, KC, N]) for n in ("delta", "alpha", "beta", "gamma")}
        omega = sb("omega", [P, KC])
        pairs = [(par[n][:], dram["l2a_" + n]) for n in par] + [(omega[:], dram["l2a_omega"])]
        n_loaded = 16 * len(pairs)
        p_, a_ = sb("p", [P, KC, N]), sb("a", [P, KC, N])
        q_, c_ = sb("q", [P, KC, N]), sb("c", [P, KC, N])
        keep = sb("keep", [P, B, S])
        decay = sb("decay", [P, KC * N, B * S])
        fed = sb("fed", [P, KC * N, B * S])
        avg = sb("avg", [P, KC * N, B * S])
        xn = sb("xn", [S, 2, E])
        xt = sb("xt", [P, KC, B * S])
        z = sb("z", [P, KC, B * S])
        sem = {n: net.sem("l2a_" + n) for n in (
            "loaded", "var_ready", "std_ready", "xn_ready", "xt_psum", "xt_ready", "gates_ready", "z_ready", "silu_ready", "zt_psum", "zt_added")}
        turned, summed = net.turned, net.summed

        with nc.Block() as block:
            @block.sync
            def _(sp):
                load_weights(sp, net, pairs, sem["loaded"])

            @block.tensor
            def _(pe):
                for b in range(B):
                    pe.wait_ge(sem["xn_ready"], b + 1)
                    if b >= 2:
                        pe.wait_ge(sem["xt_ready"], b - 1)
                    for k in range(KC):
                        last = pe.transpose(turned[:, b % 2, k * S:(k + 1) * S], xn[:, b % 2, k * P:(k + 1) * P], net.ident[0:S, 0:S])
                    last.then_inc(sem["xt_psum"], 1)
                pe.wait_ge(sem["silu_ready"], KC)
                for b in range(B):
                    if b >= 2:
                        pe.wait_ge(sem["zt_added"], b - 1)
                    for k in range(KC):
                        last = pe.transpose(summed[0:S, b % 2, k * P:(k + 1) * P], z[:, k, b * S:(b + 1) * S], net.ident[:])
                    last.then_inc(sem["zt_psum"], 1)

            @block.scalar
            def _(act):
                norm_stats_scalar(act, net, sem["var_ready"], sem["std_ready"])
                for b in range(B):
                    act.wait_ge(sem["xt_psum"], b + 1)
                    act.activation(xt[:, :, b * S:(b + 1) * S], turned[:, b % 2, 0:KC * S].rearrange("p (k s) -> p k s", k=KC),
                                   ACT.Copy).then_inc(sem["xt_ready"], 1)
                act.wait_ge(sem["loaded"], n_loaded)
                act.activation(p_[:], par["delta"][:], ACT.Sigmoid)
                act.activation(a_[:], par["alpha"][:], ACT.Sigmoid).then_inc(sem["gates_ready"], 1)
                for k in range(KC):
                    act.wait_ge(sem["z_ready"], k + 1)
                    act.activation(z[:, k, :], avg[:, 2 * k, :], ACT.Silu).then_inc(sem["silu_ready"], 1)

            @block.vector
            def _(dve):
                norm_stats_vector(dve, net, sem["var_ready"], sem["std_ready"])
                for b in range(B):
                    if b >= 2:
                        dve.wait_ge(sem["xt_psum"], b - 1)
                    normalise(dve, net, xn[:, b % 2, :], b).then_inc(sem["xn_ready"], 1)
                dve.memset(keep[:], 1.0)
                dve.drain()
                dve.memset(keep[:, :, 0:1], 0.0)
                dve.wait_ge(sem["gates_ready"], 1)
                dve.tensor_tensor(q_[:], p_[:], a_[:], ALU.mult)
                dve.tensor_tensor(c_[:], p_[:], par["beta"][:], ALU.mult)
                dve.drain()
                dve.tensor_scalar(q_[:], q_[:], -1.0, 1.0, ALU.mult, ALU.add)
                dve.tensor_tensor(c_[:], c_[:], par["gamma"][:], ALU.mult)
                dve.drain()
                dve.tensor_scalar(c_[:], c_[:], float(np.sqrt(1.0 / N)), None, ALU.mult)
                dve.drain()
                for k in range(KC):
                    for n in range(N):
                        dve.tensor_scalar(decay[:, k * N + n, :], keep[:].rearrange("p b s -> p (b s)"), q_[:, k, n:n + 1], None, ALU.mult)
                dve.wait_ge(sem["xt_ready"], B)
                for k in range(KC):
                    for n in range(N):
                        dve.tensor_scalar(fed[:, k * N + n, :], xt[:, k, :], c_[:, k, n:n + 1], None, ALU.mult)
                dve.drain()
                for k in range(KC):
                    for n in range(N):
                        j = k * N + n
                        dve.tensor_tensor_scan(avg[:, j, :], decay[:, j, :], fed[:, j, :], 0.0, ALU.mult, ALU.add)
                    dve.drain()
                    dve.tensor_tensor(avg[:, k * N, :], avg[:, k * N, :], avg[:, k * N + 1, :], ALU.add)
                    dve.drain()
                    dve.scalar_tensor_tensor(out=avg[:, k * N, :], in0=xt[:, k, :], scalar=omega[:, k:k + 1],
                                             in1=avg[:, k * N, :], op0=ALU.mult, op1=ALU.add).then_inc(sem["z_ready"], 1)
                for b in range(B):
                    dve.wait_ge(sem["zt_psum"], b + 1)
                    dve.tensor_tensor(net.x[:, b, :], net.x[:, b, :], summed[0:S, b % 2, 0:E], ALU.add).then_inc(sem["zt_added"], 1)
                dve.drain()


@sublayer
def l2_ffn(net):
    nc, dram = net.nc, net.dram
    F = 1024
    FC = F // P
    TOP = 2
    ROWS = B * S * TOP
    RT = ROWS // NE // S
    CR = RT * S
    SLOTS = 4
    with ExitStack() as ctx:
        def sb(n, shape, dt=F32):
            return ctx.enter_context(nc.sbuf_tensor("l2f_" + n, shape, dt))

        w1 = sb("w1", [P, SLOTS, KC, F])
        w2 = sb("w2", [P, SLOTS, FC, E])
        wr = sb("wr", [P, KC, NE])
        before, ones = sb("before", [S, S]), sb("ones", [S, S])
        t = TopTwo(sb)
        pairs = [(wr[:], dram["l2f_wr"]), (t.iota[:], dram["iota8"]), (before[:], dram["before"])]
        n_loaded = 16 * len(pairs)
        xn = sb("xn", [S, B, E])
        xt = sb("xt", [P, KC, 2, S])
        both = sb("both", [S, B, NE])
        total = sb("total", [S, B, NE])
        start = sb("start", [S, B + 1, NE])
        base = sb("base", [S, NE])
        rank = sb("rank", [S, B, NE])
        mine = sb("mine", [S, B, NE])
        place = sb("place", [S, TOP, B])
        placei = sb("placei", [S, TOP * B], U32)
        rows = sb("rows", [S, SLOTS, RT, E])
        rt = sb("rt", [P, KC, CR])
        hidden = sb("hidden", [P, FC, CR])
        out = sb("out", [S, SLOTS, RT, E])
        back = sb("back", [S, TOP * B, E])
        sorted_x = nc.dram_tensor("sorted_x", (ROWS, E), F32).ap()
        sorted_y = nc.dram_tensor("sorted_y", (ROWS, E), F32).ap()
        sem = {n: net.sem("l2f_" + n) for n in (
            "loaded", "w0", "w1", "w2", "w3", "r0", "r1", "r2", "r3", "var_ready", "std_ready", "xn_ready", "xt_psum", "xt_ready", "l_psum", "gap_ready",
            "exp_ready", "both_ready", "count_psum", "place_ready", "scattered", "rt_psum", "rt_ready", "h_psum", "h_ready",
            "y_psum", "y_ready", "stored0", "stored1", "stored2", "stored3", "gathered")}
        wide, turned, summed = net.wide, net.turned, net.summed
        w_loaded, r_loaded, stored = ([sem[f"{n}{slot}"] for slot in range(SLOTS)] for n in ("w", "r", "stored"))

        with nc.Block() as block:
            @block.sync
            def _(sp):
                load_weights(sp, net, pairs, sem["loaded"])

                def load_expert(e, slot):
                    sp.dma_start(w1[:, slot], dram["l2f_w1"][e]).then_inc(w_loaded[slot], 16)
                    sp.dma_start(w2[:, slot], dram["l2f_w2"][e]).then_inc(w_loaded[slot], 16)

                def load_rows(e, slot):
                    sp.dma_start(rows[:, slot], sorted_x.rearrange("(e r s) d -> e s r d", r=RT, s=S)[e]).then_inc(r_loaded[slot], 16)

                for slot in range(SLOTS):
                    load_expert(slot, slot)
                sp.wait_ge(sem["scattered"], 16 * TOP * B)
                for slot in range(SLOTS):
                    load_rows(slot, slot)
                with sp.Fori(1, NE // SLOTS) as r:
                    for slot in range(SLOTS):
                        sp.wait_ge(sem["y_psum"], SLOTS * (r - 1) + slot + 1)
                        load_rows(SLOTS * r + slot, slot)
                        load_expert(SLOTS * r + slot, slot)

            @block.gpsimd
            def _(pool):
                pool.wait_ge(sem["place_ready"], 1)
                for b in range(B):
                    for k in range(TOP):
                        pool.indirect_dma_start(out=sorted_x, out_offset=bass.IndirectOffsetOnAxis(ap=placei[:, k * B + b:k * B + b + 1], axis=0),
                                                in_=xn[:, b, :], in_offset=None).then_inc(sem["scattered"], 16)
                for slot in range(SLOTS):
                    pool.wait_ge(stored[slot], 16 * NE // SLOTS)
                for b in range(B):
                    for k in range(TOP):
                        pool.indirect_dma_start(out=back[:, k * B + b, :], out_offset=None, in_=sorted_y,
                                                in_offset=bass.IndirectOffsetOnAxis(ap=placei[:, k * B + b:k * B + b + 1], axis=0)
                                                ).then_inc(sem["gathered"], 16)

            @block.tensor
            def _(pe):
                pe.wait_ge(sem["loaded"], n_loaded)
                for b in range(B):
                    pe.wait_ge(sem["xn_ready"], b + 1)
                    if b >= 2:
                        pe.wait_ge(sem["xt_ready"], b - 1)
                    for k in range(KC):
                        last = pe.transpose(turned[:, b % 2, k * S:(k + 1) * S], xn[:, b, k * P:(k + 1) * P], net.ident[0:S, 0:S])
                    last.then_inc(sem["xt_psum"], 1)
                    pe.wait_ge(sem["xt_ready"], b + 1)
                    for k in range(KC):
                        last = pe.matmul(summed[0:S, 0, b * NE:(b + 1) * NE], xt[:, k, b % 2, :], wr[:, k, :], start=k == 0, stop=k == KC - 1)
                last.then_inc(sem["l_psum"], 1)
                pe.wait_ge(sem["both_ready"], 1)
                chosen = both[:].rearrange("s b e -> s (b e)")
                pe.matmul(summed[0:S, 1, 0:B * NE], before[:], chosen, start=True, stop=True)
                pe.matmul(summed[0:S, 1, B * NE:2 * B * NE], ones[:], chosen, start=True, stop=True).then_inc(sem["count_psum"], 1)

                def turn(r, slot):
                    pe.wait_ge(r_loaded[slot], 16 * (r + 1))
                    for c in range(RT):
                        for k in range(KC):
                            last = pe.transpose(turned[:, c, k * S:(k + 1) * S], rows[:, slot, c, k * P:(k + 1) * P], net.ident[0:S, 0:S])
                    last.then_inc(sem["rt_psum"], 1)

                with pe.Fori(0, NE // SLOTS) as r:
                    turn(r, 0)
                    for slot in range(SLOTS):
                        e = SLOTS * r + slot
                        pe.wait_ge(sem["rt_ready"], e + 1)
                        pe.wait_ge(w_loaded[slot], 32 * (r + 1))
                        for f in range(FC):
                            if f >= 4:
                                pe.wait_ge(sem["h_ready"], e * FC + f - 3)
                            for k in range(KC):
                                last = pe.matmul(wide[:, f % 4, 0:CR], w1[:, slot, k, f * P:(f + 1) * P], rt[:, k, :], start=k == 0, stop=k == KC - 1)
                            last.then_inc(sem["h_psum"], 1)
                        if slot + 1 < SLOTS:
                            turn(r, slot + 1)
                        pe.wait_ge(sem["h_ready"], e * FC + FC)
                        for c in range(RT):
                            for f in range(FC):
                                last = pe.matmul(summed[0:S, c, 0:E], hidden[:, f, c * S:(c + 1) * S], w2[:, slot, f, :], start=f == 0, stop=f == FC - 1)
                        last.then_inc(sem["y_psum"], 1)

            @block.scalar
            def _(act):
                norm_stats_scalar(act, net, sem["var_ready"], sem["std_ready"])
                for b in range(B):
                    act.wait_ge(sem["xt_psum"], b + 1)
                    act.activation(xt[:, :, b % 2, :], turned[:, b % 2, 0:KC * S].rearrange("p (k s) -> p k s", k=KC), ACT.Copy).then_inc(sem["xt_ready"], 1)
                act.wait_ge(sem["gap_ready"], 1)
                act.activation(t.exp[:], t.gap[:], ACT.Exp).then_inc(sem["exp_ready"], 1)

                def copy_rt(e):
                    act.wait_ge(sem["rt_psum"], e + 1)
                    act.activation(rt[:].rearrange("p k (c s) -> p c k s", c=RT), turned[:, :, 0:KC * S].rearrange("p c (k s) -> p c k s", k=KC),
                                   ACT.Copy).then_inc(sem["rt_ready"], 1)

                with act.Fori(0, NE // SLOTS) as r:
                    copy_rt(SLOTS * r)
                    for slot in range(SLOTS):
                        e = SLOTS * r + slot
                        for f in range(FC):
                            act.wait_ge(sem["h_psum"], e * FC + f + 1)
                            act.activation(hidden[:, f, :], wide[:, f % 4, 0:CR], ACT.Gelu).then_inc(sem["h_ready"], 1)
                        if slot + 1 < SLOTS:
                            copy_rt(e + 1)
                        act.wait_ge(sem["y_ready"], e + 1)
                        act.dma_start(sorted_y.rearrange("(e r s) d -> e s r d", r=RT, s=S)[e], out[:, slot]).then_inc(stored[slot], 16)

            @block.vector
            def _(dve):
                dve.memset(ones[:], 1.0)
                dve.memset(start[:, 0, :], 0.0)
                dve.memset(base[:, 0:1], 0.0)
                norm_stats_vector(dve, net, sem["var_ready"], sem["std_ready"])
                for b in range(B):
                    normalise(dve, net, xn[:, b, :], b).then_inc(sem["xn_ready"], 1)
                dve.wait_ge(sem["loaded"], n_loaded)
                dve.wait_ge(sem["l_psum"], 1)
                dve.tensor_copy(t.logits[:], summed[0:S, 0, 0:B * NE].rearrange("s (b e) -> s b e", b=B))
                dve.drain()
                top_two_vector(dve, net, t, sem["gap_ready"], sem["exp_ready"], both, sem["both_ready"])
                dve.wait_ge(sem["count_psum"], 1)
                dve.tensor_copy(total[:], summed[0:S, 1, B * NE:2 * B * NE].rearrange("s (b e) -> s b e", b=B))
                dve.drain()
                for b in range(B):
                    dve.tensor_tensor(start[:, b + 1, :], start[:, b, :], total[:, b, :], ALU.add)
                    dve.drain()
                for e in range(NE - 1):
                    dve.tensor_tensor(base[:, e + 1:e + 2], base[:, e:e + 1], start[:, B, e:e + 1], ALU.add)
                    dve.drain()
                dve.tensor_tensor(rank[:], start[:, 0:B, :], summed[0:S, 1, 0:B * NE].rearrange("s (b e) -> s b e", b=B), ALU.add)
                dve.drain()
                dve.tensor_tensor(rank[:], rank[:], base[:].unsqueeze(1).broadcast_to([S, B, NE]), ALU.add)
                dve.drain()
                for k in range(TOP):
                    dve.tensor_tensor(mine[:], rank[:], t.hot[k][:], ALU.mult)
                    dve.drain()
                    dve.tensor_reduce(place[:, k, :], mine[:], X_AX, ALU.add)
                    dve.drain()
                dve.tensor_copy(placei[:], place[:].rearrange("s k b -> s (k b)")).then_inc(sem["place_ready"], 1)
                for slot in range(SLOTS):
                    dve.wait_ge(sem["y_psum"], slot + 1)
                    dve.tensor_copy(out[:, slot], summed[0:S, :, 0:E]).then_inc(sem["y_ready"], 1)
                with dve.Fori(1, NE // SLOTS) as r:
                    for slot in range(SLOTS):
                        dve.wait_ge(stored[slot], 16 * r)
                        dve.wait_ge(sem["y_psum"], SLOTS * r + slot + 1)
                        dve.tensor_copy(out[:, slot], summed[0:S, :, 0:E]).then_inc(sem["y_ready"], 1)
                dve.wait_ge(sem["gathered"], 16 * TOP * B)
                for k in range(TOP):
                    for b in range(B):
                        dve.scalar_tensor_tensor(out=net.x[:, b, :], in0=back[:, k * B + b, :], scalar=t.prob[k][:, b, :],
                                                 in1=net.x[:, b, :], op0=ALU.mult, op1=ALU.add)
                    dve.drain()


@sublayer
def l3_attn(net):
    nc, dram = net.nc, net.dram
    H, D, C, T = 16, 16, 64, B
    HC = H * C
    HALF = HC // 2
    PAIRS = T * (T + 1) // 2
    RING = 4
    TB = 4
    EARLY = 5
    AHEAD = 3

    def pairs_before(t):
        return t * (t + 1) // 2

    def gpsimd_share(n):
        return n // 3

    with ExitStack() as ctx:
        def sb(n, shape, dt=F32):
            return ctx.enter_context(nc.sbuf_tensor("l3a_" + n, shape, dt))

        wqk, wv, wo = sb("wqk", [P, KC, 2 * E]), sb("wv", [P, KC, E]), sb("wo", [P, KC, E])
        bqk, bv, bo = sb("bqk", [S, 2 * E]), sb("bv", [S, E]), sb("bo", [S, E])
        bkt = sb("bkt", [P, KC])
        qc = sb("qc", [P, KC, HC // KC])
        beta = sb("beta", [S, H])
        pairs = [(wqk[:], dram["l3a_wqk"]), (wv[:], dram["l3a_wv"]), (wo[:], dram["l3a_wo"]), (qc[:], dram["l3a_qc"]),
                 (bqk[:], dram["l3a_bqk"].partition_broadcast(S)), (bv[:], dram["l3a_bv"].partition_broadcast(S)),
                 (bkt[:], dram["l3a_bkt"]),
                 (bo[:], dram["l3a_bo"].partition_broadcast(S)), (beta[:], dram["l3a_beta"].partition_broadcast(S))]
        n_loaded = 16 * len(pairs)
        xn = sb("xn", [S, 2, E])
        xt = sb("xt", [P, KC, T, S])
        kt = sb("kt", [P, KC, T, S])
        qk = sb("qk", [S, T, 2 * E])
        ring = qk[:].rearrange("s (a t) n -> s a (t n)", a=RING)
        v = sb("v", [S, T, E])
        cw = sb("cw", [S, T, HC])
        top = sb("top", [S, HC])
        rnorm = sb("rnorm", [S, T, HC])
        prod = sb("prod", [S, T, HC])
        small = sb("small", [S, T, E])
        score = sb("score", [S, PAIRS, H])
        share = sb("share", [S, T, H])
        ex = sb("ex", [S, 2, H, C])
        exr = sb("exr", [S, 2, HC])
        mx, sm = sb("mx", [S, H]), sb("sm", [S, H])
        qs = sb("qs", [S, H])
        o = sb("o", [S, 2, E])
        ot = sb("ot", [P, KC, S])
        delta = sb("delta", [S, E])
        mark = sb("mark", [1, 1])
        sem = {n: net.sem("l3a_" + n) for n in (
            "loaded", "var_ready", "std_ready", "beta_ready", "xn_ready", "xt_psum", "xt_ready", "kt_psum", "kt_ready",
            "cw_psum", "cw_copied", "qkv_psum", "qkv_ready", "shifted", "cw_ready", "norm_ready", "rnorm_ready",
            "scored", "ring_ready", "ring_summed", "lg_ready", "ex_ready", "exr_ready", "prod_ready", "weighed",
            "o_ready", "ot_psum", "ot_ready", "out_psum", "added")}
        wide, turned, summed = net.wide, net.turned, net.summed
        kt_banks = [turned[:, 0, :], turned[:, 1, :], summed[:, 0, :], summed[:, 1, :]]

        with nc.Block() as block:
            @block.sync
            def _(sp):
                load_weights(sp, net, pairs, sem["loaded"])

            @block.tensor
            def _(pe):
                def turn_x(t, slot, first):
                    pe.wait_ge(sem["xn_ready"], t + 1)
                    if not first:
                        pe.wait_ge(sem["xt_ready"], t - 1)
                    for k in range(KC):
                        last = pe.transpose(turned[:, slot, k * S:(k + 1) * S], xn[:, slot, k * P:(k + 1) * P], net.ident[0:S, 0:S])
                    last.then_inc(sem["xt_psum"], 1)

                by_pairs(pe, T, turn_x)
                pe.wait_ge(sem["loaded"], n_loaded)
                pe.wait_ge(sem["xt_ready"], T)
                for m in range(KC):
                    for half in range(T // TB):
                        for k in range(KC):
                            last = pe.matmul(kt_banks[m * (T // TB) + half][:, 0:TB * S], wqk[:, k, E + m * P:E + (m + 1) * P],
                                             xt[:, k, half * TB:(half + 1) * TB, :].rearrange("p t s -> p (t s)"),
                                             start=k == 0, stop=k == KC - 1)
                        last.then_inc(sem["kt_psum"], 1)
                pe.wait_ge(sem["kt_ready"], 2 * T // TB)

                for t in range(T):
                    if t >= 2:
                        pe.wait_ge(sem["cw_copied"], t - 1)
                    for m in range(KC):
                        last = pe.matmul(wide[0:S, 2 * (t % 2) + m, :], kt[:, m, t, :], qc[:, m, :], start=True, stop=True)
                    last.then_inc(sem["cw_psum"], 1)
                    if t >= 2:
                        pe.wait_ge(sem["qkv_ready"], t - 1)
                    for w, dst in ((wqk, turned[0:S, t % 2, :]), (wv, summed[0:S, t % 2, 0:E])):
                        for k in range(KC):
                            last = pe.matmul(dst, xt[:, k, t, :], w[:, k, :], start=k == 0, stop=k == KC - 1)
                    last.then_inc(sem["qkv_psum"], 1)

                def average(t):
                    if t >= 2:
                        pe.wait_ge(sem["lg_ready"], t - 1)
                    for u in range(t + 1):
                        n = pairs_before(t) + u
                        pe.wait_ge(sem["ring_ready"], n + 1)
                        for half in range(2):
                            last = pe.matmul(wide[0:S, 2 * (t % 2) + half, :], net.ident[0:S, 0:S],
                                             ring[:, n % RING, half * HALF:(half + 1) * HALF], start=u == 0, stop=u == t)
                        last.then_inc(sem["ring_summed"], 1)

                for t in range(AHEAD):
                    average(t)
                for t in range(T):
                    if t + AHEAD < T:
                        average(t + AHEAD)
                    pe.wait_ge(sem["o_ready"], t + 1)
                    for k in range(KC):
                        last = pe.transpose(turned[:, t % 2, k * S:(k + 1) * S], o[:, t % 2, k * P:(k + 1) * P], net.ident[0:S, 0:S])
                    last.then_inc(sem["ot_psum"], 1)
                    pe.wait_ge(sem["ot_ready"], t + 1)
                    if t >= 2:
                        pe.wait_ge(sem["added"], t - 1)
                    for k in range(KC):
                        last = pe.matmul(summed[0:S, t % 2, 0:E], ot[:, k, :], wo[:, k, :], start=k == 0, stop=k == KC - 1)
                    last.then_inc(sem["out_psum"], 1)

            @block.scalar
            def _(act):
                norm_stats_scalar(act, net, sem["var_ready"], sem["std_ready"])

                def copy_xt(t, slot, first):
                    act.wait_ge(sem["xt_psum"], t + 1)
                    act.activation(xt[:, :, bass.ds(t, 1), :].rearrange("p k o s -> p k (o s)"),
                                   turned[:, slot, 0:KC * S].rearrange("p (k s) -> p k s", k=KC), ACT.Copy).then_inc(sem["xt_ready"], 1)

                by_pairs(act, T, copy_xt)
                act.wait_ge(sem["loaded"], n_loaded)
                for m in range(KC):
                    for half in range(T // TB):
                        n = m * (T // TB) + half
                        act.wait_ge(sem["kt_psum"], n + 1)
                        act.activation(kt[:, m, half * TB:(half + 1) * TB, :].rearrange("p t s -> p (t s)"), kt_banks[n][:, 0:TB * S],
                                       ACT.Identity, bias=bkt[:, m:m + 1]).then_inc(sem["kt_ready"], 1)
                act.activation(beta[:], beta[:], ACT.Exp).then_inc(sem["beta_ready"], 1)

                def copy_cw(t, slot, first):
                    act.wait_ge(sem["cw_psum"], t + 1)
                    act.activation(cw[:, bass.ds(t, 1), :].rearrange("s o n -> s (o n)"), wide[0:S, 2 * slot:2 * slot + 2, :].rearrange("s a n -> s (a n)"),
                                   ACT.Copy).then_inc(sem["cw_copied"], 1)

                by_pairs(act, T, copy_cw)
                with act.Fori(0, T) as t:
                    act.wait_ge(sem["shifted"], t + 1)
                    act.activation(cw[:, t, :], cw[:, t, :], ACT.Exp).then_inc(sem["cw_ready"], 1)
                act.drain()
                act.activation(rnorm[:, 0, :], cw[:, 0, :], ACT.Ln)
                with act.Fori(1, T) as t:
                    act.wait_ge(sem["norm_ready"], t)
                    act.activation(rnorm[:, t, :], rnorm[:, t, :], ACT.Ln)
                act.drain()
                for t in range(T):
                    act.activation(rnorm[:, t, :], rnorm[:, t, :], ACT.Exp, scale=-1.0).then_inc(sem["rnorm_ready"], 1)

                def exps(t):
                    act.wait_ge(sem["lg_ready"], t + 1)
                    act.activation(ex[:, t % 2], ex[:, t % 2], ACT.Exp).then_inc(sem["ex_ready"], 1)

                exps(0)
                exps(1)
                for t in range(T):
                    if t + 2 < T:
                        exps(t + 2)
                    act.wait_ge(sem["ot_psum"], t + 1)
                    act.activation(ot[:], turned[:, t % 2, 0:KC * S].rearrange("p (k s) -> p k s", k=KC), ACT.Copy).then_inc(sem["ot_ready"], 1)

            @block.gpsimd
            def _(pool):
                for t in range(1, T):
                    pool.wait_ge(sem["cw_ready"], t + 1)
                    if t >= 2:
                        pool.drain()
                    pool.tensor_tensor(rnorm[:, t, :], cw[:, 0, :] if t == 1 else rnorm[:, t - 1, :], cw[:, t, :], ALU.add)
                    if t >= 2:
                        pool.drain()
                        pool.memset(mark[:], 0.0).then_inc(sem["norm_ready"], 1)
                pool.drain()
                pool.memset(mark[:], 0.0).then_inc(sem["norm_ready"], 1)

                def products(t):
                    for u in range(t + 1):
                        n = pairs_before(t) + u
                        if n >= RING:
                            pool.wait_ge(sem["ring_summed"], n - RING + 1)
                        pool.tensor_tensor(ring[:, n % RING, :].rearrange("s (h c) -> s h c", h=H), cw[:, u, :].rearrange("s (h c) -> s h c", h=H),
                                           score[:, n, :].unsqueeze(2).broadcast_to([S, H, C]), ALU.mult).then_inc(sem["ring_ready"], 1)

                def weigh(t):
                    pool.wait_ge(sem["ex_ready"], t + 1)
                    pool.wait_ge(sem["rnorm_ready"], t + 1)
                    if t >= 2:
                        pool.wait_ge(sem["weighed"], t - 1)
                    pool.tensor_tensor(exr[:, t % 2, :], ex[:, t % 2].rearrange("s h c -> s (h c)"), rnorm[:, t, :],
                                       ALU.mult).then_inc(sem["exr_ready"], 1)
                    n, mine = t + 1, gpsimd_share(t + 1)
                    if mine:
                        pool.drain()
                        if t >= 1:
                            pool.wait_ge(sem["weighed"], t)
                        pool.tensor_tensor(prod[:, n - mine:n, :], cw[:, n - mine:n, :],
                                           exr[:, t % 2, :].unsqueeze(1).broadcast_to([S, mine, HC]), ALU.mult).then_inc(sem["prod_ready"], 1)

                pool.wait_ge(sem["scored"], 1)
                for t in range(AHEAD):
                    products(t)
                for t in range(T):
                    weigh(t)
                    if t + AHEAD < T:
                        products(t + AHEAD)

            @block.vector
            def _(dve):
                norm_stats_vector(dve, net, sem["var_ready"], sem["std_ready"])

                def normal(t, slot, first):
                    if not first:
                        dve.wait_ge(sem["xt_psum"], t - 1)
                    normalise(dve, net, xn[:, slot, :], t).then_inc(sem["xn_ready"], 1)

                by_pairs(dve, T, normal)
                dve.wait_ge(sem["beta_ready"], 1)
                dve.tensor_scalar(qs[:], beta[:], float(D) ** 0.5, None, ALU.mult)
                dve.drain()
                dve.reciprocal(qs[:], qs[:])
                dve.drain()

                def take(t):
                    one = qk[:, t, :]
                    dve.wait_ge(sem["qkv_psum"], t + 1)
                    dve.tensor_tensor(one, turned[0:S, t % 2, :], bqk[:], ALU.add)
                    dve.tensor_tensor(v[:, t, :], summed[0:S, t % 2, 0:E], bv[:], ALU.add).then_inc(sem["qkv_ready"], 1)
                    dve.wait_ge(sem["cw_copied"], t + 1)
                    if t == 0:
                        dve.tensor_copy(top[:], cw[:, t, :])
                    else:
                        dve.tensor_tensor(top[:], top[:], cw[:, t, :], ALU.max)
                    dve.drain()
                    dve.tensor_tensor(one[:, 0:E].rearrange("s (h d) -> s h d", h=H), one[:, 0:E].rearrange("s (h d) -> s h d", h=H),
                                      qs[:].unsqueeze(2).broadcast_to([S, H, D]), ALU.mult)
                    dve.drain()

                def scores(t):
                    n, at = t + 1, pairs_before(t)
                    dve.tensor_tensor(small[:, 0:n, :], qk[:, 0:n, E:2 * E], qk[:, t, 0:E].unsqueeze(1).broadcast_to([S, n, E]), ALU.mult)
                    dve.drain()
                    last = dve.tensor_reduce(score[:, at:at + n, :], small[:, 0:n, :].rearrange("s t (h d) -> s t h d", h=H), X_AX, ALU.add)
                    if t == T - 1:
                        last.then_inc(sem["scored"], 1)
                    dve.drain()

                for t in range(T):
                    take(t)
                    if t < EARLY:
                        scores(t)
                with dve.Fori(0, T) as t:
                    dve.tensor_tensor(cw[:, t, :], cw[:, t, :], top[:], ALU.subtract).then_inc(sem["shifted"], 1)
                for t in range(EARLY, T):
                    scores(t)

                def shift(t):
                    one = ex[:, t % 2]
                    dve.wait_ge(sem["ring_summed"], pairs_before(t + 1))
                    dve.wait_ge(sem["rnorm_ready"], t + 1)
                    dve.tensor_tensor(one.rearrange("s h c -> s (h c)"), wide[0:S, 2 * (t % 2):2 * (t % 2) + 2, :].rearrange("s a n -> s (a n)"),
                                      rnorm[:, t, :], ALU.mult)
                    dve.drain()
                    dve.tensor_reduce(mx[:], one, X_AX, ALU.max)
                    dve.drain()
                    dve.tensor_tensor(one, one, mx[:].unsqueeze(2).broadcast_to([S, H, C]), ALU.subtract).then_inc(sem["lg_ready"], 1)

                def values(t):
                    n, mine = t + 1, t + 1 - gpsimd_share(t + 1)
                    dve.wait_ge(sem["ex_ready"], t + 1)
                    dve.tensor_reduce(sm[:], ex[:, t % 2], X_AX, ALU.add)
                    dve.wait_ge(sem["exr_ready"], t + 1)
                    dve.tensor_tensor(prod[:, 0:mine, :], cw[:, 0:mine, :], exr[:, t % 2, :].unsqueeze(1).broadcast_to([S, mine, HC]), ALU.mult)
                    dve.drain()
                    dve.reciprocal(sm[:], sm[:])
                    dve.tensor_reduce(share[:, 0:mine, :], prod[:, 0:mine, :].rearrange("s t (h c) -> s t h c", h=H), X_AX, ALU.add)
                    if mine < n:
                        dve.wait_ge(sem["prod_ready"], sum(gpsimd_share(u + 1) > 0 for u in range(n)))
                        dve.tensor_reduce(share[:, mine:n, :], prod[:, mine:n, :].rearrange("s t (h c) -> s t h c", h=H), X_AX, ALU.add)
                    dve.drain()
                    dve.tensor_tensor(share[:, 0:n, :], share[:, 0:n, :], sm[:].unsqueeze(1).broadcast_to([S, n, H]), ALU.mult).then_inc(sem["weighed"], 1)
                    dve.drain()
                    dve.tensor_tensor(small[:, 0:n, :].rearrange("s t (h d) -> s t h d", h=H), v[:, 0:n, :].rearrange("s t (h d) -> s t h d", h=H),
                                      share[:, 0:n, :].unsqueeze(3).broadcast_to([S, n, H, D]), ALU.mult)
                    dve.drain()
                    if t >= 2:
                        dve.wait_ge(sem["ot_psum"], t - 1)
                    dve.tensor_reduce(o[:, t % 2, :], small[:, 0:n, :].rearrange("s t n -> s n t"), X_AX, ALU.add).then_inc(sem["o_ready"], 1)

                def add(t):
                    dve.drain()
                    dve.wait_ge(sem["out_psum"], t + 1)
                    dve.tensor_tensor(delta[:], summed[0:S, t % 2, 0:E], bo[:], ALU.add).then_inc(sem["added"], 1)
                    dve.drain()
                    dve.tensor_tensor(net.x[:, t, :], net.x[:, t, :], delta[:], ALU.add)

                shift(0)
                shift(1)
                for t in range(T):
                    values(t)
                    if t + 2 < T:
                        shift(t + 2)
                    if t >= 1:
                        add(t - 1)
                add(T - 1)
                dve.drain()


@sublayer
def l3_ffn(net):
    nc, dram = net.nc, net.dram
    BANKS = NE * E // 512
    with ExitStack() as ctx:
        def sb(n, shape, dt=F32):
            return ctx.enter_context(nc.sbuf_tensor("l3f_" + n, shape, dt))

        wg, we = sb("wg", [P, KC, E]), sb("we", [P, KC, NE * E])
        bg, be = sb("bg", [S, E]), sb("be", [NE, E])
        iota = sb("iota", [S, B, NE])
        pairs = [(wg[:], dram["l3f_wg"]), (bg[:], dram["l3f_bg"].partition_broadcast(S)),
                 (be[:], dram["l3f_be"]), (iota[:], dram["iota8"]), (we[:], dram["l3f_we"])]
        n_loaded = 16 * len(pairs)
        xn = sb("xn", [S, 2, E])
        xt = sb("xt", [P, KC, B, S])
        lg, ex = sb("lg", [S, B, E]), sb("ex", [S, B, E])
        top, peak = sb("top", [S, B, 8]), sb("peak", [S, B, 8])
        ntop, sm, p = sb("ntop", [S, B, 1]), sb("sm", [S, B, 1]), sb("p", [S, B, 1])
        which, expert = sb("which", [S, B, 8], U32), sb("expert", [S, B, 1])
        hot = sb("hot", [S, B, NE])
        hot_t = sb("hot_t", [NE, B, S])
        acc = sb("acc", [S, 2, E])
        sem = {n: net.sem("l3f_" + n) for n in (
            "loaded", "var_ready", "std_ready", "xn_ready", "xt_psum", "xt_ready", "g_psum", "lg_ready", "top_ready", "ex_ready",
            "hot_ready", "ht_psum", "ht_ready", "b_psum", "b_read", "z_psum", "z_read")}
        wide, turned, summed = net.wide, net.turned, net.summed

        with nc.Block() as block:
            @block.sync
            def _(sp):
                load_weights(sp, net, pairs, sem["loaded"])

            @block.tensor
            def _(pe):
                def turn_x(b, slot, first):
                    pe.wait_ge(sem["xn_ready"], b + 1)
                    if not first:
                        pe.wait_ge(sem["xt_ready"], b - 1)
                    for k in range(KC):
                        last = pe.transpose(turned[:, slot, k * S:(k + 1) * S], xn[:, slot, k * P:(k + 1) * P], net.ident[0:S, 0:S])
                    last.then_inc(sem["xt_psum"], 1)

                by_pairs(pe, B, turn_x)
                pe.wait_ge(sem["loaded"], n_loaded)
                for b in range(B):
                    pe.wait_ge(sem["xt_ready"], b + 1)
                    if b >= 2:
                        pe.wait_ge(sem["lg_ready"], b - 1)
                    for k in range(KC):
                        last = pe.matmul(summed[0:S, b % 2, 0:E], xt[:, k, b, :], wg[:, k, :], start=k == 0, stop=k == KC - 1)
                    last.then_inc(sem["g_psum"], 1)
                for b in range(B):
                    if b >= 1:
                        if b >= 2:
                            pe.wait_ge(sem["b_read"], b - 1)
                        pe.matmul(summed[0:S, b % 2, 0:E], hot_t[:, b, :], be[:], start=True, stop=True).then_inc(sem["b_psum"], 1)
                    for n in range(BANKS):
                        if b >= 1:
                            pe.wait_ge(sem["z_read"], (b - 1) * BANKS + n + 1)
                        for k in range(KC):
                            last = pe.matmul(wide[0:S, n, :], xt[:, k, b, :], we[:, k, n * 512:(n + 1) * 512], start=k == 0, stop=k == KC - 1)
                        last.then_inc(sem["z_psum"], 1)
                    if b == 0:
                        pe.wait_ge(sem["hot_ready"], 1)
                        for c in range(B):
                            last = pe.transpose(turned[0:NE, c // 4, (c % 4) * S:(c % 4 + 1) * S], hot[:, c, :], net.ident[0:S, 0:S])
                        last.then_inc(sem["ht_psum"], 1)
                        pe.wait_ge(sem["ht_ready"], 1)
                        pe.matmul(summed[0:S, 0, 0:E], hot_t[:, 0, :], be[:], start=True, stop=True).then_inc(sem["b_psum"], 1)

            @block.scalar
            def _(act):
                norm_stats_scalar(act, net, sem["var_ready"], sem["std_ready"])

                def copy_xt(b, slot, first):
                    act.wait_ge(sem["xt_psum"], b + 1)
                    act.activation(xt[:, :, bass.ds(b, 1), :].rearrange("p k o s -> p k (o s)"),
                                   turned[:, slot, 0:KC * S].rearrange("p (k s) -> p k s", k=KC), ACT.Copy).then_inc(sem["xt_ready"], 1)

                by_pairs(act, B, copy_xt)
                for b in range(B):
                    act.wait_ge(sem["top_ready"], b + 1)
                    act.activation(ex[:, b, :], lg[:, b, :], ACT.Exp, bias=ntop[:, b, :], accum_out=sm[:, b, :]).then_inc(sem["ex_ready"], 1)
                act.wait_ge(sem["ht_psum"], 1)
                act.activation(hot_t[:].rearrange("e (a b) s -> e a (b s)", a=2), turned[0:NE, :, 0:4 * S], ACT.Copy).then_inc(sem["ht_ready"], 1)

            @block.vector
            def _(dve):
                norm_stats_vector(dve, net, sem["var_ready"], sem["std_ready"])

                def normal(b, slot, first):
                    if not first:
                        dve.wait_ge(sem["xt_psum"], b - 1)
                    normalise(dve, net, xn[:, slot, :], b).then_inc(sem["xn_ready"], 1)

                by_pairs(dve, B, normal)
                dve.wait_ge(sem["loaded"], n_loaded)
                for b in range(B):
                    dve.wait_ge(sem["g_psum"], b + 1)
                    dve.tensor_tensor(lg[:, b, :], summed[0:S, b % 2, 0:E], bg[:], ALU.add).then_inc(sem["lg_ready"], 1)
                    dve.drain()
                    dve.max(top[:, b, :], lg[:, b, :])
                    dve.drain()
                    dve.tensor_scalar(ntop[:, b, :], top[:, b, 0:1], -1.0, None, ALU.mult).then_inc(sem["top_ready"], 1)
                for b in range(B):
                    dve.wait_ge(sem["ex_ready"], b + 1)
                    dve.max(peak[:, b, :], ex[:, b, :])
                dve.drain()
                for b in range(B):
                    dve.max_index(which[:, b, :], peak[:, b, :], ex[:, b, :])
                dve.reciprocal(p[:], sm[:])
                dve.drain()
                dve.tensor_scalar(which[:, :, 0:1], which[:, :, 0:1], NE - 1, None, ALU.bitwise_and)
                dve.tensor_tensor(p[:], p[:], peak[:, :, 0:1], ALU.mult)
                dve.drain()
                dve.tensor_copy(expert[:], which[:, :, 0:1])
                dve.drain()
                dve.tensor_tensor(hot[:], expert[:].broadcast_to([S, B, NE]), iota[:], ALU.is_equal).then_inc(sem["hot_ready"], 1)
                dve.drain()

                def choose(b, slot, first):
                    one = acc[:, slot, :]
                    dve.wait_ge(sem["b_psum"], b + 1)
                    dve.tensor_copy(one, summed[0:S, slot, 0:E]).then_inc(sem["b_read"], 1)
                    for e in range(NE):
                        dve.drain()
                        if e % 2 == 0:
                            dve.wait_ge(sem["z_psum"], b * BANKS + e // 2 + 1)
                        last = dve.scalar_tensor_tensor(out=one, in0=wide[0:S, e // 2, (e % 2) * E:(e % 2 + 1) * E],
                                                        scalar=hot[:, bass.ds(b, 1), e:e + 1].rearrange("s o e -> s (o e)"),
                                                        in1=one, op0=ALU.mult, op1=ALU.add)
                        if e % 2 == 1:
                            last.then_inc(sem["z_read"], 1)
                    dve.drain()
                    dve.tensor_scalar(one, one, 0.0, p[:, bass.ds(b, 1), :].rearrange("s o e -> s (o e)"), ALU.max, ALU.mult)
                    dve.drain()
                    dve.tensor_tensor(net.x[:, b, :], net.x[:, b, :], one, ALU.add)

                by_pairs(dve, B, choose)
                dve.drain()


def more_layouts(a, d, wide, col):
    def experts(w):
        return w.reshape(w.shape[0], -1, P, w.shape[-1]).transpose(0, 2, 1, 3)

    d["iota8"] = np.broadcast_to(np.arange(NE, dtype=np.float32), (S, B, NE))
    d["before"] = (np.arange(S)[:, None] < np.arange(S)[None, :]).astype(np.float32)
    d["l0f_w1"] = experts(np.concatenate([a["L0_ffn_W1"], a["L0_ffn_Ws1"][None]]))
    d["l0f_w2"] = np.concatenate([a["L0_ffn_W2"], a["L0_ffn_Ws2"][None]])
    d["l0f_wr"] = wide(a["L0_ffn_Wr"])
    w1 = np.concatenate([a["L1_ffn_w1"], a["L1_ffn_ws1"][None]])
    w2 = np.concatenate([a["L1_ffn_w2"], a["L1_ffn_ws2"][None]])
    b1 = np.concatenate([a["L1_ffn_b1"], a["L1_ffn_bs1"][None]])
    pack = np.concatenate([experts(w1).reshape(NE + 1, P, -1), experts(w2).reshape(NE + 1, P, -1),
                           b1.reshape(NE + 1, -1, P).transpose(0, 2, 1)], axis=2)
    d["l1f_pack"], d["l1f_shared"] = pack[:NE].reshape(NE * P, -1), pack[NE]
    d["l1f_b2"], d["l1f_b2s"] = a["L1_ffn_b2"], a["L1_ffn_bs2"]
    d["l1f_wr"], d["l1f_br"] = wide(a["L1_ffn_gate_w"]), a["L1_ffn_gate_b"]
    tile_rows = 2 * S
    n_tiles = (2 * B * S + NE * (tile_rows - 1)) // tile_rows
    d["l1f_tiles"] = np.broadcast_to(np.arange(n_tiles, dtype=np.float32), (P, n_tiles))
    d["l1f_partition"] = np.broadcast_to(np.arange(P, dtype=np.float32)[:, None], (P, n_tiles))
    d["l1a_wqk"] = wide(np.concatenate([a["L1_attn_Wq"], a["L1_attn_Wk"]], axis=1))
    d["l1a_bqk"] = np.concatenate([a["L1_attn_bq"], a["L1_attn_bk"]])
    d["l1a_wv"], d["l1a_wo"] = wide(a["L1_attn_Wv"]), wide(a["L1_attn_Wo"])
    d["l1a_bv"], d["l1a_bo"] = a["L1_attn_bv"], a["L1_attn_bo"]
    for n in ("delta", "alpha", "beta", "gamma"):
        d["l2a_" + n] = a["L2_attn_" + n].reshape(KC, P, 2).transpose(1, 0, 2)
    d["l2a_omega"] = col(a["L2_attn_omega"])
    d["l2f_wr"] = wide(a["L2_ffn_Wr"].T)
    d["l2f_w1"], d["l2f_w2"] = experts(a["L2_ffn_W1"]), experts(a["L2_ffn_W2"])
    d["l3a_wqk"] = wide(np.concatenate([a["L3_attn_Wq"].T, a["L3_attn_Wk"].T], axis=1))
    d["l3a_bqk"] = np.concatenate([a["L3_attn_bq"], a["L3_attn_bk"]])
    d["l3a_bkt"] = col(a["L3_attn_bk"])
    d["l3a_wv"], d["l3a_wo"] = wide(a["L3_attn_Wv"].T), wide(a["L3_attn_Wo"].T)
    d["l3a_bv"], d["l3a_bo"], d["l3a_beta"] = a["L3_attn_bv"], a["L3_attn_bo"], a["L3_attn_beta"]
    H, D, C = 16, 16, 64
    blocks = np.zeros((H, D, H, C), np.float32)
    for h in range(H):
        blocks[h, :, h, :] = a["L3_attn_q_c"].reshape(C, H, D)[:, h, :].T
    half = H // KC
    d["l3a_qc"] = np.stack([blocks[m * half:(m + 1) * half, :, m * half:(m + 1) * half].reshape(P, half * C) for m in range(KC)], axis=1)
    d["l3f_wg"] = wide(a["L3_ffn_Wg"])
    d["l3f_we"] = wide(a["L3_ffn_We"].transpose(1, 0, 2).reshape(E, NE * E))
    d["l3f_bg"], d["l3f_be"] = a["L3_ffn_bg"], a["L3_ffn_be"]


def build(nc, dram):
    with ExitStack() as ctx:
        net = Net(nc, ctx, dram)
        setup(net)
        l0_attn(net)
        cross_attn(net, "l0x", 16, rope=True, biases=True, mask=("key_mask", I32))
        l0_ffn(net)
        l1_attn(net)
        cross_attn(net, "l1x", 16, biases=True, gate=True)
        l1_ffn(net)
        l2_attn(net)
        cross_attn(net, "l2x", 4, mask=("query_mask", U8))
        l2_ffn(net)
        l3_attn(net)
        cross_attn(net, "l3x", 16)
        l3_ffn(net)
        store(net)


def _layouts(a):
    def wide(w):
        return w.reshape(-1, P, w.shape[-1]).transpose(1, 0, 2)

    def col(b):
        return b.reshape(-1, P).T

    d = {"x": a["x"], "ident": np.eye(P, dtype=np.float32)}
    d["causal"] = np.where(np.arange(S)[:, None] < np.arange(S)[None, :], np.float32(NEG), np.float32(0))
    d["ctxt"] = a["ctx_1024"].transpose(0, 2, 1).reshape(B, KC, P, SKV).transpose(0, 2, 1, 3)
    for D in (16, 64):
        d[f"headmask{D}"] = (np.arange(P)[:, None] // D == np.arange(P // D)[None, :]).astype(np.float32)
    for n in ("q", "k", "v"):
        d["l0a_w" + n] = wide(a["L0_attn_w_" + n].reshape(-1, E).T)
    d["l0a_wo"] = wide(a["L0_attn_w_o"])
    for k, n in (("l0x", "L0_xattn"), ("l1x", "L1_xattn")):
        for m in "qkvo":
            d[f"{k}_w{m}"] = wide(a[f"{n}_W{m}"])
        for m in "qk":
            d[f"{k}_b{m}"] = col(a[f"{n}_b{m}"])
        for m in "vo":
            d[f"{k}_b{m}"] = a[f"{n}_b{m}"]
    wkv = a["L2_xattn_Wkv"]
    for m, w in (("q", a["L2_xattn_Wq"]), ("k", wkv[:E]), ("v", wkv[E:]), ("o", a["L2_xattn_Wout"])):
        d["l2x_w" + m] = wide(w.T)
    for m in "qkvo":
        d["l3x_w" + m] = wide(a["L3_xattn_W" + m].T)
    d["l3x_bo"] = a["L3_xattn_bo"]
    d["key_mask"] = a["mask_Bx1x1xS2_if1"].reshape(B, SKV)
    bits = np.zeros((B, S, -(-SKV // 4) * 4), np.bool_)
    bits[:, :, 0:SKV] = a["mask_BxSxS2_bk0"]
    d["query_mask"] = bits.view(np.int32)
    D = 16
    r = np.arange(P) % D
    inv = (1.0 / np.float32(10000.0) ** (np.arange(0, D, 2, dtype=np.float32) / np.float32(D))).astype(np.float32)
    angle = (np.arange(SKV, dtype=np.float32)[None, :] * inv[r % (D // 2)][:, None]).astype(np.float32)
    d["rope_cos"], d["rope_sin"] = np.cos(angle), np.sin(angle)
    swap = np.zeros((P, P), np.float32)
    for p in range(P):
        lower = r[p] < D // 2
        swap[p + D // 2 if lower else p - D // 2, p] = -1.0 if lower else 1.0
    d["rope_swap"] = swap
    rows = np.minimum(np.arange(PADKV), SKV - 1)
    d["energy"] = a["ctxb_2048x8"][:, rows].reshape(B * NCH, CH, 8).transpose(1, 0, 2)
    more_layouts(a, d, wide, col)
    return {k: np.ascontiguousarray(v) for k, v in d.items()}


def kernel(**inputs):
    import concourse.bacc as bacc
    from concourse.bass_utils import run_bass_kernel_spmd

    nc = bacc.Bacc("TRN2", target_bir_lowering=False, num_devices=1)
    arrays = {k + "_dram": v for k, v in _layouts({k: np.asarray(v) for k, v in inputs.items()}).items()}
    dram = {k[:-5]: nc.dram_tensor(k, v.shape, mybir.dt.from_np(v.dtype), kind="ExternalInput").ap()
            for k, v in arrays.items()}
    dram["out"] = nc.dram_tensor("out_dram", (B, S, E), F32, kind="ExternalOutput").ap()
    build(nc, dram)
    return run_bass_kernel_spmd(nc, [arrays], core_ids=[0]).results[0]["out_dram"]
```
